# Optimizing a Trainium2 kernel written in Bass

```python
import numpy as np
import jax
import jax.numpy as jnp

def _softmax(x, axis=-1):
    return jax.nn.softmax(x, axis=axis)

def _gelu(x):
    return jax.nn.gelu(x, approximate=True)

def _silu(x):
    return jax.nn.silu(x)

def _sigmoid(x):
    return jax.nn.sigmoid(x)

def _layernorm(x, axis=-1, eps=1e-05):
    m = jnp.mean(x, axis=axis, keepdims=True)
    v = jnp.var(x, axis=axis, keepdims=True)
    return (x - m) / jnp.sqrt(v + eps)

def _scatter_add(tgt, idx, src, axis=0):
    return tgt.at[idx].add(src)

def _segment_sum(src, seg, n):
    return jax.ops.segment_sum(src, seg, n)
kernel_name = 'mk_perceiver_d1_seqx_r2_f1a7f1'

def setup_inputs(seed: int=0):
    np.random.seed(seed)
    _w = jnp.asarray

    def _rec_inputs():
        import jax
        import jax.numpy as jnp
        _rk = jax.random.key(seed)
        x = -0.0003929 + 0.9999 * jax.random.normal(jax.random.fold_in(_rk, 1), (2, 512, 512), jnp.float32)
        _lenS = 512 - jax.random.randint(jax.random.fold_in(_rk, 7), (2,), 0, max(1, 512 // 4) + 1, jnp.int32)
        _lenS2 = 8192 - jax.random.randint(jax.random.fold_in(_rk, 8), (2,), 0, max(1, 8192 // 4) + 1, jnp.int32)
        _ctx_1024P = jax.random.normal(jax.random.fold_in(_rk, 11), (2, 16, 512), jnp.float32)
        _ctx_1024c = jax.random.dirichlet(jax.random.fold_in(_rk, 511), 0.3 * jnp.ones((16,), jnp.float32), (2, 8192))
        _ctx_1024t = jnp.einsum('bsk,bkd->bsd', _ctx_1024c, _ctx_1024P)
        _ctx_1024t = _ctx_1024t * jax.lax.rsqrt(jnp.mean(jnp.square(_ctx_1024t)) + 1e-12) * 0.953939
        ctx_1024 = 2.81802e-05 + 1.00001 * (_ctx_1024t + 0.3 * jax.random.normal(jax.random.fold_in(_rk, 611), (2, 8192, 512), jnp.float32))
        return (x, ctx_1024, _lenS2)
    x, ctx_1024, _lenS2 = _rec_inputs()

    def _L0_xattn_setup():
        import jax, jax.numpy as jnp
        import numpy as np
        NEG = -10000000000000.0
        key = jax.random.key(seed)
        ks = jax.random.split(key, 7)
        B, L, D, E = (8, 1024, 512, 512)
        Q = jax.random.normal(ks[0], (B, L, D), dtype=jnp.float32)
        K = jax.random.normal(ks[1], (B, L, D), dtype=jnp.float32)
        V = jax.random.normal(ks[2], (B, L, D), dtype=jnp.float32)
        query_pad_idxs = jax.random.randint(ks[3], (B,), 0, L)
        key_pad_idxs = jax.random.randint(ks[4], (B,), 0, L)
        W = jax.random.normal(ks[5], (E, D), dtype=jnp.float32) / np.sqrt(D)
        b = jax.random.normal(ks[6], (E,), dtype=jnp.float32) * 0.01
        return {'Q': Q, 'K': K, 'V': V, 'query_pad_idxs': query_pad_idxs, 'key_pad_idxs': key_pad_idxs, 'W': W, 'b': b}
    _L0_xattn_all = _L0_xattn_setup()
    _L0_xattn_in = {k: v for k, v in _L0_xattn_all.items() if k in ('W', 'b')}
    del _L0_xattn_all

    def _L0_attn_setup():
        import jax, jax.numpy as jnp
        import numpy as np
        import math
        N_HEAD = 16
        HEAD_QKV = 512
        WM_DECAY_LENGTH = 1024
        WM_DECAY_RATE = 1.0
        WM_ECHOIC = 16

        def decay_weight_matrix(n):
            dl = WM_DECAY_LENGTH - WM_ECHOIC + 1
            nums = jnp.linspace(0.0, 1.0, dl)
            decay_values = 1.0 - jnp.power(nums, 1.0 / (np.e * WM_DECAY_RATE))
            decay_values = jnp.concatenate([jnp.ones(WM_ECHOIC - 1), decay_values])
            decay_values = decay_values[:n]
            idx = jnp.arange(n)[:, None] - jnp.arange(n)[None, :]
            mat = decay_values[jnp.clip(idx, 0, n - 1)]
            return jnp.tril(mat).astype(jnp.float32)
        key = jax.random.key(seed)
        k1, k2, k3 = jax.random.split(key, 3)
        B, T, C = (2, 1024, 512)
        x = jax.random.normal(k1, (B, T, C), dtype=jnp.float32)
        W_attn = jax.random.normal(k2, (C, 3 * HEAD_QKV), dtype=jnp.float32) * (1.0 / math.sqrt(C))
        W_proj = jax.random.normal(k3, (HEAD_QKV, C), dtype=jnp.float32) * (1.0 / math.sqrt(HEAD_QKV))
        return {'x': x, 'W_attn': W_attn, 'W_proj': W_proj}
    _L0_attn_all = _L0_attn_setup()
    _L0_attn_in = {k: v for k, v in _L0_attn_all.items() if k in ('W_attn', 'W_proj')}
    del _L0_attn_all

    def _L0_ffn_setup():
        import jax, jax.numpy as jnp
        import numpy as np
        B, SEQ, DIM = (2, 2048, 512)
        E, S = (8, 256)
        HID = 4 * DIM
        SCALE = DIM ** 0.5

        def rmsnorm(x, gamma):
            n = jnp.linalg.norm(x, axis=-1, keepdims=True)
            return x / jnp.maximum(n, 1e-12) * SCALE * gamma
        key = jax.random.key(seed)
        ks = jax.random.split(key, 4)
        w_init = lambda k, shape: jax.random.normal(k, shape, dtype=jnp.float32) * 0.02
        return {'x': jax.random.normal(ks[0], (B, SEQ, DIM), dtype=jnp.float32), 'norm_gamma': jnp.ones((DIM,), jnp.float32), 'slot_norm_gamma': jnp.ones((DIM,), jnp.float32), 'slot_embeds': jax.random.normal(ks[1], (E, S, DIM), dtype=jnp.float32), 'w1': w_init(ks[2], (E, DIM, HID)), 'b1': jnp.zeros((E, HID), jnp.float32), 'w2': w_init(ks[3], (E, HID, DIM)), 'b2': jnp.zeros((E, DIM), jnp.float32)}
    _L0_ffn_all = _L0_ffn_setup()
    _L0_ffn_in = {k: v for k, v in _L0_ffn_all.items() if k in ('norm_gamma', 'slot_norm_gamma', 'slot_embeds', 'w1', 'b1', 'w2', 'b2')}
    del _L0_ffn_all
    return {'x': x, 'ctx_1024': ctx_1024, '_lenS2': _lenS2, 'L0_xattn_W': _L0_xattn_in['W'], 'L0_xattn_b': _L0_xattn_in['b'], 'L0_attn_W_attn': _L0_attn_in['W_attn'], 'L0_attn_W_proj': _L0_attn_in['W_proj'], 'L0_ffn_norm_gamma': _L0_ffn_in['norm_gamma'], 'L0_ffn_slot_norm_gamma': _L0_ffn_in['slot_norm_gamma'], 'L0_ffn_slot_embeds': _L0_ffn_in['slot_embeds'], 'L0_ffn_w1': _L0_ffn_in['w1'], 'L0_ffn_b1': _L0_ffn_in['b1'], 'L0_ffn_w2': _L0_ffn_in['w2'], 'L0_ffn_b2': _L0_ffn_in['b2']}

def reference(x, ctx_1024, _lenS2, L0_xattn_W, L0_xattn_b, L0_attn_W_attn, L0_attn_W_proj, L0_ffn_norm_gamma, L0_ffn_slot_norm_gamma, L0_ffn_slot_embeds, L0_ffn_w1, L0_ffn_b1, L0_ffn_w2, L0_ffn_b2):
    import jax
    import jax.numpy as jnp

    def _L0_xattn_ref(Q, K, V, query_pad_idxs, key_pad_idxs, W, b):
        import jax, jax.numpy as jnp
        import numpy as np
        NEG = -10000000000000.0
        B, Lq, D = Q.shape
        Lk = K.shape[1]
        scale = 1.0 / jnp.sqrt(jnp.asarray(D, dtype=Q.dtype))
        scores = jnp.einsum('bqd,bkd->bqk', Q, K) * scale
        qpos = jnp.arange(Lq)[None, :, None]
        kpos = jnp.arange(Lk)[None, None, :]
        mask = (qpos >= query_pad_idxs[:, None, None]) & (kpos >= key_pad_idxs[:, None, None])
        scores = jnp.where(mask, jnp.asarray(NEG, scores.dtype), scores)
        attn = jax.nn.softmax(scores, axis=2)
        out = jnp.einsum('bqk,bkd->bqd', attn, V)
        return out @ W.T + b

    def _L0_attn_ref(x, W_attn, W_proj):
        import jax, jax.numpy as jnp
        import numpy as np
        import math
        N_HEAD = 16
        HEAD_QKV = 512
        WM_DECAY_LENGTH = 1024
        WM_DECAY_RATE = 1.0
        WM_ECHOIC = 16

        def decay_weight_matrix(n):
            dl = WM_DECAY_LENGTH - WM_ECHOIC + 1
            nums = jnp.linspace(0.0, 1.0, dl)
            decay_values = 1.0 - jnp.power(nums, 1.0 / (np.e * WM_DECAY_RATE))
            decay_values = jnp.concatenate([jnp.ones(WM_ECHOIC - 1), decay_values])
            decay_values = decay_values[:n]
            idx = jnp.arange(n)[:, None] - jnp.arange(n)[None, :]
            mat = decay_values[jnp.clip(idx, 0, n - 1)]
            return jnp.tril(mat).astype(jnp.float32)
        B, T, C = x.shape
        hd = HEAD_QKV // N_HEAD
        qkv = x @ W_attn
        q, k, v = jnp.split(qkv, 3, axis=-1)
        q = q.reshape(B, T, N_HEAD, hd).transpose(0, 2, 1, 3)
        k = k.reshape(B, T, N_HEAD, hd).transpose(0, 2, 1, 3)
        v = v.reshape(B, T, N_HEAD, hd).transpose(0, 2, 1, 3)
        att = jnp.einsum('bhqd,bhkd->bhqk', q, k) * (1.0 / math.sqrt(hd))
        causal = jnp.tril(jnp.ones((T, T), dtype=bool))
        att = jnp.where(causal, att, -jnp.inf)
        att = jax.nn.softmax(att, axis=-1)
        att = att * decay_weight_matrix(T)
        y = jnp.einsum('bhqk,bhkd->bhqd', att, v)
        y = y.transpose(0, 2, 1, 3).reshape(B, T, HEAD_QKV)
        return y @ W_proj

    def _L0_ffn_ref(x, norm_gamma, slot_norm_gamma, slot_embeds, w1, b1, w2, b2):
        import jax, jax.numpy as jnp
        import numpy as np
        B, SEQ, DIM = (2, 2048, 512)
        E, S = (8, 256)
        HID = 4 * DIM
        SCALE = DIM ** 0.5

        def rmsnorm(x, gamma):
            n = jnp.linalg.norm(x, axis=-1, keepdims=True)
            return x / jnp.maximum(n, 1e-12) * SCALE * gamma
        xn = rmsnorm(x, norm_gamma)
        sn = rmsnorm(slot_embeds, slot_norm_gamma)
        logits = jnp.einsum('bnd,esd->bnes', xn, sn)
        dispatch = jax.nn.softmax(logits, axis=1)
        b, n, e, s = logits.shape
        combine = jax.nn.softmax(logits.reshape(b, n, e * s), axis=-1)
        slots = jnp.einsum('bnd,bnes->besd', xn, dispatch)
        h = jnp.einsum('besd,edh->besh', slots, w1) + b1[None, :, None, :]
        h = jax.nn.gelu(h, approximate=False)
        eo = jnp.einsum('besh,ehd->besd', h, w2) + b2[None, :, None, :]
        eo = eo.reshape(b, e * s, DIM)
        out = jnp.einsum('bmd,bnm->bnd', eo, combine)
        return out
    x = x + _L0_xattn_ref(_layernorm(x, axis=-1), ctx_1024, ctx_1024, _lenS2, _lenS2, L0_xattn_W, L0_xattn_b)
    x = x + _L0_attn_ref(_layernorm(x, axis=-1), L0_attn_W_attn, L0_attn_W_proj)
    x = x + _L0_ffn_ref(_layernorm(x, axis=-1), L0_ffn_norm_gamma, L0_ffn_slot_norm_gamma, L0_ffn_slot_embeds, L0_ffn_w1, L0_ffn_b1, L0_ffn_w2, L0_ffn_b2)
    return x

_drawn_inputs = setup_inputs


def setup_inputs(seed=0):
    import zlib

    import numpy as np

    out = dict(_drawn_inputs(seed))
    spreads = {'L0_ffn_norm_gamma': (1.0, 0.2),
     'L0_ffn_slot_norm_gamma': (1.0, 0.2),
     'L0_ffn_b1': (0.0, 0.1),
     'L0_ffn_b2': (0.0, 0.1)}
    factors = {'L0_xattn_b': 5.706}
    for name, (base, spread) in spreads.items():
        noise = np.random.default_rng([zlib.crc32(name.encode()), seed]).standard_normal(out[name].shape)
        drawn = base * np.exp(spread * noise) if base else spread * noise
        out[name] = jnp.asarray(drawn.astype(out[name].dtype))
    for name, factor in factors.items():
        out[name] = (out[name] * factor).astype(out[name].dtype)
    return out
```

```python
from contextlib import ExitStack

import concourse.bass as bass
from concourse import mybir

ALU = mybir.AluOpType
ACT = mybir.ActivationFunctionType
AX = mybir.AxisListType
F32 = mybir.dt.float32
F16 = mybir.dt.float16
BF16 = mybir.dt.bfloat16
I32 = mybir.dt.int32

P = 128
D = 512
DC = D // P
B = 2
NQ = 512
QT = NQ // P
T = B * QT
NK = 8192
KT = NK // P
CT = 4
KC = KT // CT
H = 16
HD = D // H
E = 8
ES = 256
M = E * ES
HID = 2048
HC = HID // 512
MC = M // 512

UP = 32.0
DOWN = 1.0 / (UP * UP)
EXP_UP = 7.0
NEG = -1e13
EPS = 1e-5
MASKED = -1e30

C_ID = 0
C_ONE = C_ID + P
C_SET = C_ONE + P
C_QPOS = C_SET
C_KPOS = C_QPOS + NQ
C_DECAY = C_SET
C_CAUSAL = C_DECAY + QT * P
C_END = C_CAUSAL + P

N_CTX = B * 2 * KC
N_WO, N_WQ, N_WK, N_WV, N_WP = range(N_CTX, N_CTX + 5)
N_EXP = N_CTX + 5
SMALL = 8


def products_after(n):
    if isinstance(n, int) and n >= N_CTX:
        if n < N_EXP:
            return 4 * N_CTX + SMALL * (n + 1 - N_CTX)
        return 4 * N_CTX + SMALL * 5 + 4 * (n + 1 - N_EXP)
    return 4 * n + 4


def program(nc, x, ctx_stream, square_stream, expert_stream, lens, xattn_b, gamma, slot_gamma,
            slot_embeds, b1, b2, consts, out):
    with ExitStack() as ctx:
        def sb(name, shape, dt):
            return ctx.enter_context(nc.sbuf_tensor(name, shape, dt))

        def sem(name):
            return ctx.enter_context(nc.semaphore(name))

        def dram(name, shape, dt):
            return nc.dram_tensor(name, shape, dt, kind="Internal").ap()

        psum = ctx.enter_context(nc.psum_tensor("psum", [P, 8, 512], F32))
        S = sb("S", [P, KT, 512], F32)
        A = sb("A", [P, 16, 512], F32)
        raw = sb("raw", [P, 2, CT * 512], F32)
        whi = sb("whi", [P, 2, CT, 512], F16)
        wlo = sb("wlo", [P, 2, CT, 512], F16)
        cst = sb("cst", [P, C_END], F32)
        run_max = sb("run_max", [P, 512], F32)
        run_sum = sb("run_sum", [P, 512], F32)
        bcast = sb("bcast", [P, 512], F32)
        diag = sb("diag", [P, 4, P], F32)
        qneg = sb("qneg", [P, 512], F32)
        lens_i = sb("lens_i", [P, B], I32)
        lens_f = sb("lens_f", [P, B], F32)
        kmask = sb("kmask", [P, KT], F32)
        col = sb("col", [P, 4], F32)
        rcol = sb("rcol", [P, 4], F32)
        ident16 = sb("ident16", [P, P], BF16)
        causal16 = sb("causal16", [P, P], BF16)
        one16 = sb("one16", [P, 2], F16)
        bn6 = sb("bn6", [P, T, 6], F32)
        mean_var = sb("mean_var", [P, T, 2], F32)
        var_eps = sb("var_eps", [P, 2 * T], F32)
        std = sb("std", [P, 2 * T], F32)
        rstd = sb("rstd", [P, 2 * T], F32)
        exp_up = sb("exp_up", [P, 1], F32)
        head_max = sb("head_max", [P, 2, QT], F32)
        head_bias = sb("head_bias", [P, 2, QT], F32)
        head_sum = sb("head_sum", [P, 2, QT], F32)
        head_rec = sb("head_rec", [P, 2, QT], F32)
        row_max = sb("row_max", [P, QT], F32)
        row_bias = sb("row_bias", [P, B, QT], F32)
        row_sum = sb("row_sum", [P, B, QT, MC], F32)
        row_rec = sb("row_rec", [P, T], F32)
        sq_sum = sb("sq_sum", [P, T + M // P], F32)
        sq_root = sb("sq_root", [P, T + M // P], F32)
        sq_rec = sb("sq_rec", [P, T + M // P], F32)

        ident = cst[:, C_ID:C_ID + P]
        ones = cst[:, C_ONE:C_ONE + P]
        decay = cst[:, C_DECAY:C_DECAY + QT * P]

        def view(buf, at, n, dt, *dims):
            v = buf[:, at:at + n, :].rearrange("p a b -> p (a b)")
            if dt != F32:
                v = v.bitcast(dt)
            names = "abc"[:len(dims)]
            if len(dims) > 1:
                v = v.rearrange(f"p ({' '.join(names)}) -> p {' '.join(names)}", **dict(zip(names, dims)))
            return v

        def flat(v):
            return v.rearrange("p a n -> p (a n)")

        NH = B * H
        qT = [view(A, 4 * i, 4, F16, DC, T * P) for i in range(2)]
        pp = [[view(A, 8 + 4 * u + 2 * i, 2, F16, CT, 512) for i in range(2)] for u in range(2)]
        resid = view(S, 0, 8, F32, T, 512)
        tT = [view(S, 8 + 4 * i, 4, F16, DC, T * P) for i in range(2)]
        nat = view(S, 16, 8, F32, T, 512)
        q_stack = view(S, 24, 16, F16, B, H, NQ)
        k_stack = view(S, 40, 16, F16, B, H, NQ)
        o_nat = view(S, 56, 8, F32, T, 512)
        v_nat = [view(S, 56 + 4 * i, 4, F16, NH, QT, HD) for i in range(2)]
        y_nat = view(S, 16, 8, F32, QT, NH, HD)
        qk = [[view(A, 8 * w + 4 * i, 4, F16, QT, T * P) for i in range(2)] for w in range(2)]
        a_flat = flat(A[:, :, :])
        NB = QT * (QT + 1) // 2 * P
        prob = [a_flat[:, u * NB:(u + 1) * NB] for u in range(2)]
        prob_t = [a_flat[:, (2 + u) * NB:(3 + u) * NB] for u in range(2)]
        prob_16 = [[a_flat[:, (4 + u) * NB:(5 + u) * NB].bitcast(F16)[:, i * NB:(i + 1) * NB]
                    for i in range(2)] for u in range(2)]
        xn_nat = [view(S, 24 + 4 * i, 4, F16, T, 512) for i in range(2)]
        snT = [view(S, 32 + 8 * i, 8, F16, DC, M) for i in range(2)]
        L = view(S, 48, 16, F32, QT, M)
        se_nat = view(S, 48, 16, F32, M // P, 512)
        disp = view(A, 0, 4, F32, QT, 512)
        disp_16 = [[view(A, 4 + 4 * u + 2 * i, 2, F16, QT, 512) for i in range(2)] for u in range(2)]
        comb = view(A, 12, 4, F32, QT, 512)
        slots = view(S, 16, 4, F32, DC, 512)
        slots_16 = view(S, 20, 4, F16, 2, DC, 512)
        comb_16 = [whi[:, 0, :, :], wlo[:, 0, :, :]]
        e_slots = [view(S, 8 + 4 * u, 4, F16, 2, DC, 512) for u in range(2)]
        e_comb = [view(S, 16 + 4 * u, 4, F16, 2, 4, 512) for u in range(2)]
        hid = view(S, 24, 4, F32, CT, 512)
        hid_16 = [[view(S, 28 + 4 * u + 2 * i, 2, F16, CT, 512) for i in range(2)] for u in range(2)]
        eo = view(S, 36, 4, F32, 4, 512)
        eo_16 = [view(S, 40 + 2 * i, 2, F16, 4, 512) for i in range(2)]
        b2_rows = view(S, 44, 8, F32, E, 512)
        b1_cols = S[:, 52, 0:E * HID // P]

        o_scratch = dram("o_scratch", [P, QT * 512], F32)
        slots_dram = dram("slots_dram", [E, P, 2, DC, B, ES], F16)
        comb_dram = dram("comb_dram", [E, P, 2, B, 2, NQ], F16)

        raw_loaded = [sem(f"raw_loaded{u}") for u in range(2)]
        split_hi = sem("split_hi")
        split_lo = sem("split_lo")
        products = sem("products")
        const_loaded = sem("const_loaded")
        x_loaded = sem("x_loaded")
        dve_step = sem("dve_step")
        setup_done = sem("setup_done")
        var_ready = sem("var_ready")
        std_ready = sem("std_ready")
        squares_ready = sem("squares_ready")
        z_ready = sem("z_ready")
        rows_ready = sem("rows_ready")
        turned = sem("turned")
        turned_hi = sem("turned_hi")
        turned_lo = sem("turned_lo")
        scores_kept = sem("scores_kept")
        max_kept = sem("max_kept")
        sum_kept = sem("sum_kept")
        stat_mm = sem("stat_mm")
        stat_dve = sem("stat_dve")
        shifted = sem("shifted")
        exp_done = sem("exp_done")
        p_hi = sem("p_hi")
        p_lo = sem("p_lo")
        o_ready = sem("o_ready")
        o_moved = sem("o_moved")
        phase2_loaded = sem("phase2_loaded")
        proj_kept = sem("proj_kept")
        qkv_hi = sem("qkv_hi")
        qkv_lo = sem("qkv_lo")
        q_stacked = sem("q_stacked")
        k_stacked = sem("k_stacked")
        head_scores = sem("head_scores")
        head_maxed = sem("head_maxed")
        head_reduced = sem("head_reduced")
        head_rec_ready = sem("head_rec_ready")
        head_exp = sem("head_exp")
        head_turned = sem("head_turned")
        head_decayed = sem("head_decayed")
        head_hi = sem("head_hi")
        head_lo = sem("head_lo")
        head_y = sem("head_y")
        head_kept = sem("head_kept")
        se_loaded = sem("se_loaded")
        xn_hi = sem("xn_hi")
        xn_lo = sem("xn_lo")
        logit_mm = sem("logit_mm")
        logit_kept = sem("logit_kept")
        row_biased = sem("row_biased")
        cmax_ready = sem("cmax_ready")
        max_mm = sem("max_mm")
        sum_mm = sem("sum_mm")
        max_diag = sem("max_diag")
        sum_diag = sem("sum_diag")
        disp_shift = sem("disp_shift")
        disp_exp = sem("disp_exp")
        disp_hi = sem("disp_hi")
        disp_lo = sem("disp_lo")
        slot_mm = sem("slot_mm")
        slot_kept = sem("slot_kept")
        slot_hi = sem("slot_hi")
        slot_lo = sem("slot_lo")
        slot_moved = sem("slot_moved")
        comb_exp = sem("comb_exp")
        comb_turned = sem("comb_turned")
        comb_hi = sem("comb_hi")
        comb_lo = sem("comb_lo")
        comb_moved = sem("comb_moved")
        bias_loaded = sem("bias_loaded")
        e_slots_in = [sem(f"e_slots_in{u}") for u in range(2)]
        e_comb_in = [sem(f"e_comb_in{u}") for u in range(2)]
        hid_done = sem("hid_done")
        hid_hi = sem("hid_hi")
        hid_lo = sem("hid_lo")
        eo_kept = sem("eo_kept")
        eo_hi = sem("eo_hi")
        eo_lo = sem("eo_lo")
        comb_mm = sem("comb_mm")
        comb_kept = sem("comb_kept")
        stored = sem("stored")

        block = ctx.enter_context(nc.Block())

        TURN_X, TURN_O, TURN_HN, TURN_Y, TURN_XN, TURN_SN = (T * i for i in range(6))
        ROWS_X, ROWS_HN, ROWS_XN, ROWS_SN = 0, T, 2 * T, 3 * T
        SCORE_BANKS = [(0, [(0, 0), (2, P)]), (1, [(1, 0)]), (2, [(3, 0)])]
        SCORE_COL = {q: n for n, q in enumerate([0, 2, 1, 3])}
        TURN_BANKS = [(3, [(0, 0)]), (4, [(1, 0), (3, 3 * P)]), (5, [(2, 0)])]
        BLOCK_AT = {0: 0, 1: 512, 3: 512 + 3 * P, 2: 1024}
        PROB_AT = {q: q * (q + 1) // 2 * P for q in range(QT)}
        STACKED = 16 * B * (P // HD) ** 2
        GROUPS = B * MC

        N_CHUNKS = N_EXP + 2 * E * HC

        @block.sync
        def _(sp):
            sp.dma_start(cst[:, :], consts[0]).then_inc(const_loaded, 16)
            sp.dma_start(lens_i[:, :], lens.partition_broadcast(P)).then_inc(const_loaded, 16)
            x_rows = x.rearrange("b (t p) d -> p (b t) d", p=P)
            sp.dma_start(nat, x_rows).then_inc(x_loaded, 16)

            def load(u, src):
                sp.dma_start(raw[:, u, :], src).then_inc(raw_loaded[u], 16)

            for u in range(2):
                load(u, ctx_stream[u])
            with sp.Fori(1, N_CTX // 2) as i:
                for u in range(2):
                    sp.wait_ge(split_lo, 2 * i + u - 1)
                    load(u, ctx_stream[bass.ds(2 * i + u, 1)].rearrange("a p n -> p (a n)"))
            for n in (N_WO, N_WQ):
                sp.wait_ge(split_lo, n - 1)
                load(n % 2, square_stream[n - N_WO])
            sp.wait_ge(o_ready, T)
            sp.wait_ge(o_moved, 16)
            for dst, src in ((resid, x_rows), (flat(o_nat[:, 0:QT, :]), o_scratch),
                             (cst[:, C_SET:C_END], consts[1][:, C_SET:C_END]),
                             (qneg[:, :], xattn_b.partition_broadcast(P)),
                             (run_max[:, :], gamma.partition_broadcast(P)),
                             (run_sum[:, :], slot_gamma.partition_broadcast(P))):
                sp.dma_start(dst, src).then_inc(phase2_loaded, 16)
            for n in (N_WK, N_WV, N_WP):
                sp.wait_ge(split_lo, n - 1)
                load(n % 2, square_stream[n - N_WO])
            for w, (stack, done, parts) in enumerate(((q_stack, q_stacked, (0, 0, 1, 1)),
                                                      (k_stack, k_stacked, (0, 1, 0, 1)))):
                sp.wait_ge(qkv_lo, T * (w + 1))
                if w:
                    sp.wait_ge(split_lo, N_EXP - 1)
                    load(N_EXP % 2, expert_stream[0])
                for j in range(P // HD):
                    for g, part in enumerate(parts):
                        for b in range(B):
                            sp.dma_start(stack[HD * g:HD * (g + 1), b, j::P // HD, :],
                                         qk[w][part][HD * j:HD * (j + 1), :, b * NQ:(b + 1) * NQ]
                                         ).then_inc(done, 16)
            sp.wait_ge(head_y, NH)
            sp.dma_start(se_nat, slot_embeds.rearrange("(t p) d -> p t d", p=P)).then_inc(se_loaded, 16)
            sp.wait_ge(split_lo, N_EXP)
            load((N_EXP + 1) % 2, expert_stream[1])

            for g in range(GROUPS):
                b, mc = divmod(g, MC)
                sp.wait_ge(comb_lo, 4 * (g + 1))
                for part in range(2):
                    sp.dma_start(comb_dram[2 * mc:2 * mc + 2, :, part, b, :, :].rearrange("e p m n -> p e (m n)"),
                                 comb_16[part].rearrange("p (e m) n -> p e (m n)", e=2)).then_inc(comb_moved, 16)
                sp.wait_ge(slot_lo, g + 1)
                for e in range(2):
                    for part in range(2):
                        sp.dma_start(slots_dram[2 * mc + e, :, part, :, b, :],
                                     slots_16[:, part, :, e * ES:(e + 1) * ES]).then_inc(slot_moved, 16)

            def load_expert(e, u, what):
                if what == "slots":
                    sp.dma_start(e_slots[u].rearrange("p a b n -> p (a b n)"),
                                 slots_dram[bass.ds(e, 1)].rearrange("e p a c b s -> p (e a c b s)")
                                 ).then_inc(e_slots_in[u], 16)
                else:
                    sp.dma_start(e_comb[u].rearrange("p a b n -> p (a b n)"),
                                 comb_dram[bass.ds(e, 1)].rearrange("e p a b m n -> p (e a b m n)")
                                 ).then_inc(e_comb_in[u], 16)

            sp.wait_ge(slot_moved, 16 * 4 * GROUPS)
            sp.wait_ge(comb_moved, 16 * 2 * GROUPS)
            load_expert(0, 0, "slots")
            load_expert(0, 0, "comb")
            sp.dma_start(b2_rows, b2.partition_broadcast(P)).then_inc(bias_loaded, 16)
            sp.dma_start(b1_cols, b1).then_inc(bias_loaded, 16)

            def expert_loads(e, u, first=False, last=False):
                for s in range(2, 8 if last else 10):
                    n = N_EXP + s
                    sp.wait_ge(split_lo, 8 * e + n - 1)
                    load(n % 2, expert_stream[bass.ds(8 * e + s, 1)].rearrange("a p n -> p (a n)"))
                    if s == 2 and not last:
                        load_expert(e + 1, 1 - u, "slots")
                    if s == 8:
                        if not first:
                            sp.wait_ge(comb_mm, T * e)
                        load_expert(e + 1, 1 - u, "comb")

            expert_loads(0, 0, first=True)
            with sp.Fori(0, E // 2 - 1) as i:
                expert_loads(2 * i + 1, 1)
                expert_loads(2 * i + 2, 0)
            expert_loads(E - 1, 1, last=True)

            out_rows = out.rearrange("b (t p) d -> p (b t) d", p=P)
            for t in range(T):
                sp.wait_ge(comb_kept, T * (E - 1) + t + 1)
                sp.dma_start(out_rows[:, t, :], resid[:, t, :]).then_inc(stored, 16)
            sp.wait_ge(stored, 16 * T)

        @block.gpsimd
        def _(pool):
            for b in range(B):
                if b:
                    pool.wait_ge(stat_mm, 3 * b)
                nc.gpsimd.memset(run_sum[:, :], 0.0).then_inc(sum_kept, 1)
                with pool.Fori(0, KC) as j:
                    pool.wait_ge(exp_done, KC * b + j + 1)
                    for k in range(CT):
                        tile = 4 * j + k
                        pool.wait_ge(sum_kept, (KT + 1) * b + 1 + tile)
                        nc.gpsimd.tensor_tensor(
                            run_sum[:, :], run_sum[:, :], flat(S[:, bass.ds(tile, 1), :]),
                            ALU.add).then_inc(sum_kept, 1)
                if b == 0:
                    pool.wait_ge(o_ready, QT)
                    pool.dma_start(o_scratch, flat(S[:, KT - QT:KT, :])).then_inc(o_moved, 16)

            with pool.Fori(0, NH // 2) as i:
                for u in range(2):
                    pool.wait_ge(head_hi, 2 * i + u + 1)
                    nc.gpsimd.tensor_tensor(prob_16[u][1], prob_t[u], prob_16[u][0],
                                            ALU.subtract).then_inc(head_lo, 1)

            for g in range(GROUPS):
                pool.wait_ge(slot_hi, g + 1)
                nc.gpsimd.tensor_tensor(slots_16[:, 1, :, :], slots, slots_16[:, 0, :, :],
                                        ALU.subtract).then_inc(slot_lo, 1)

        @block.scalar
        def _(act):
            def hi_part(pair, u):
                n = 2 * pair + u
                act.wait_ge(raw_loaded[u], 16 * pair + 16)
                if not (isinstance(n, int) and n < 2):
                    act.wait_ge(products, products_after(n - 2))
                nc.scalar.activation(flat(whi[:, u, :, :]), raw[:, u, :], ACT.Copy, scale=UP).then_inc(split_hi, 1)

            roots = [0]

            def square_root(n):
                roots[0] += 1
                act.wait_ge(var_ready, roots[0])
                nc.scalar.activation(std[:, 0:n], var_eps[:, 0:n], ACT.Sqrt).then_inc(std_ready, 1)

            def turn_hi(first, tiles, dst, scale):
                for t in range(tiles):
                    act.wait_ge(turned, first + t + 1)
                    nc.scalar.activation(dst[:, :, t * P:(t + 1) * P],
                                         psum[:, (first + t) % 4, :].rearrange("p (c n) -> p c n", c=DC),
                                         ACT.Copy, scale=scale).then_inc(turned_hi, 1)

            square_root(T)
            hi_part(0, 0)
            turn_hi(TURN_X, T, qT[0], UP)
            act.wait_ge(setup_done, 3)

            for b in range(B):
                start = b * N_CTX // 4
                if b == 0:
                    hi_part(0, 1)
                    hi_part(1, 0)
                with act.Fori(start + (b == 0), start + KC // 2) as i:
                    hi_part(i, 1)
                    hi_part(i + 1, 0)

                def probabilities(i, u):
                    j = 2 * i + u - KC * (2 * b + 1)
                    act.wait_ge(shifted, KC * b + j + 1)
                    act.nop(nofuse=True)
                    s = S[:, bass.ds(CT * j, CT), :]
                    nc.scalar.activation(s, s, ACT.Exp, bias=exp_up[:, 0:1],
                                         scale=DOWN / D ** 0.5).then_inc(exp_done, 1)
                    act.wait_ge(exp_done, KC * b + j + 1)
                    act.wait_ge(products, products_after(2 * i + u - 2))
                    act.nop(nofuse=True)
                    nc.scalar.activation(pp[u][0], s, ACT.Copy).then_inc(p_hi, 1)

                start += KC // 2
                with act.Fori(start, start + KC // 2) as i:
                    probabilities(i, 0)
                    hi_part(i, 1)
                    probabilities(i, 1)
                    hi_part(i + 1, 0)

            turn_hi(TURN_O, T, tT[0], UP)
            hi_part(N_WQ // 2, N_WQ % 2)
            square_root(T)
            turn_hi(TURN_HN, T, tT[0], UP)

            def qkv_high(n, t, dst):
                act.wait_ge(products, products_after(n - 1) + t + 1)
                src = psum[:, 4 + t % 4, :]
                if len(dst.shape) == 3:
                    src = src.rearrange("p (h d) -> p h d", h=H)
                nc.scalar.activation(dst, src, ACT.Copy, scale=1.0 / UP).then_inc(qkv_hi, 1)

            for w, n in enumerate((N_WQ, N_WK)):
                for t in range(T):
                    f, b = divmod(t, B)
                    qkv_high(n, t, qk[w][0][:, f, b * NQ:(b + 1) * NQ])
                    if t == 0:
                        hi_part((n + 1) // 2, (n + 1) % 2)
            for t in range(T):
                b, k = divmod(t, QT)
                qkv_high(N_WV, t, v_nat[0][:, b * H:(b + 1) * H, k, :])
                if t == 0:
                    hi_part(N_WP // 2, N_WP % 2)

            def head_exponentials(g, u):
                for n, (bank, tiles) in enumerate(SCORE_BANKS):
                    act.wait_ge(head_maxed, 3 * g + n + 1)
                    if not (isinstance(g, int) and g < 2):
                        act.wait_ge(head_turned, g - 1)
                    for q, at in tiles:
                        c, width = SCORE_COL[q], (q + 1) * P
                        last = nc.scalar.activation(
                            prob[u][:, PROB_AT[q]:PROB_AT[q] + width], psum[:, bank, at:at + width], ACT.Exp,
                            bias=head_bias[:, u, c:c + 1], scale=DOWN / HD ** 0.5,
                            accum_out=head_sum[:, u, q:q + 1])
                    last.then_inc(head_exp, 1)

            def head_high(g, u):
                act.wait_ge(head_decayed, g + 1)
                if not (isinstance(g, int) and g < 2):
                    act.wait_ge(head_y, g - 1)
                nc.scalar.activation(prob_16[u][0], prob_t[u], ACT.Copy).then_inc(head_hi, 1)

            act.wait_ge(q_stacked, STACKED)
            act.wait_ge(k_stacked, STACKED)
            head_exponentials(0, 0)
            for g in range(4):
                head_exponentials(g + 1, 1 - g % 2)
                head_high(g, g % 2)
            with act.Fori(2, NH // 2 - 1) as i:
                for u in range(2):
                    head_exponentials(2 * i + u + 1, 1 - u)
                    head_high(2 * i + u, u)
            head_exponentials(NH - 1, 1)
            head_high(NH - 2, 0)
            head_high(NH - 1, 1)
            turn_hi(TURN_Y, T, tT[0], UP)
            hi_part(N_EXP // 2, N_EXP % 2)

            square_root(T)

            def squares(src, n):
                nc.scalar.activation(bcast[:, :], src, ACT.Square, accum_out=sq_sum[:, n:n + 1]).then_inc(squares_ready, 1)
                act.wait_ge(squares_ready, n + 1)

            for t in range(T):
                act.wait_ge(z_ready, t + 1)
                squares(nat[:, t, :], t)
            nc.scalar.activation(sq_root[:, 0:T], sq_sum[:, 0:T], ACT.Sqrt).then_inc(std_ready, 1)
            act.wait_ge(se_loaded, 16)
            for t in range(M // P):
                squares(se_nat[:, t, :], T + t)
            nc.scalar.activation(sq_root[:, T:], sq_sum[:, T:], ACT.Sqrt).then_inc(std_ready, 1)
            for t in range(T):
                act.wait_ge(rows_ready, ROWS_XN + t + 1)
                nc.scalar.activation(xn_nat[0][:, t, :], nat[:, t, :], ACT.Copy, scale=UP).then_inc(xn_hi, 1)
            turn_hi(TURN_XN, T, tT[0], UP)
            turn_hi(TURN_SN, M // P, snT[0], UP)

            def disp_high(g):
                act.wait_ge(disp_shift, g + 1)
                nc.scalar.activation(disp, disp, ACT.Exp, bias=exp_up[:, 0:1]).then_inc(disp_exp, 1)
                act.wait_ge(disp_exp, g + 1)
                if g >= 2:
                    act.wait_ge(slot_mm, 4 * (g - 1))
                nc.scalar.activation(disp_16[g % 2][0], disp, ACT.Copy).then_inc(disp_hi, 1)

            def combine_high(g):
                b, mc = divmod(g, MC)
                act.wait_ge(row_biased, b + 1)
                if g:
                    act.wait_ge(comb_turned, 4 * g)
                for q in range(QT):
                    last = nc.scalar.activation(comb[:, q, :], L[:, q, mc * 512:(mc + 1) * 512], ACT.Exp,
                                                bias=row_bias[:, b, q:q + 1],
                                                accum_out=row_sum[:, b, q, mc:mc + 1])
                last.then_inc(comb_exp, 1)
                if g:
                    act.wait_ge(comb_moved, 32 * g)
                for m in range(4):
                    act.wait_ge(comb_turned, 4 * g + m + 1)
                    nc.scalar.activation(comb_16[0][:, m, :], psum[:, 2 + m % 2, :], ACT.Copy).then_inc(comb_hi, 1)
                act.wait_ge(slot_kept, 4 * g + 4)
                if g:
                    act.wait_ge(slot_moved, 64 * g)
                nc.scalar.activation(slots_16[:, 0, :, :], slots, ACT.Copy).then_inc(slot_hi, 1)

            for b in range(B):
                if b:
                    act.wait_ge(disp_shift, MC * b)
                for k in range(QT * MC):
                    q, mc = divmod(k, MC)
                    act.wait_ge(logit_mm, QT * MC * b + k + 1)
                    nc.scalar.activation(L[:, q, mc * 512:(mc + 1) * 512], psum[:, k % 2, :], ACT.Copy,
                                         scale=DOWN).then_inc(logit_kept, 1)
                disp_high(MC * b)
                for mc in range(MC):
                    if mc + 1 < MC:
                        disp_high(MC * b + mc + 1)
                    combine_high(MC * b + mc)

            def chunk_high(e, s):
                n = N_EXP + s
                act.wait_ge(raw_loaded[n % 2], 16 * (4 * e + n // 2 + 1))
                act.wait_ge(products, products_after(N_EXP - 1) + 4 * (8 * e + s - 1))
                nc.scalar.activation(flat(whi[:, n % 2, :, :]), raw[:, n % 2, :], ACT.Copy, scale=UP).then_inc(split_hi, 1)

            def hidden(e, hc, s):
                q = HC * e + hc
                first = isinstance(q, int) and q == 0
                if not first:
                    act.wait_ge(hid_lo, q)
                for k in range(CT):
                    act.wait_ge(products, products_after(N_EXP - 1) + 4 * (8 * e + s) + k + 1)
                    act.nop(nofuse=True)
                    nc.scalar.activation(hid[:, k, :], psum[:, k, :], ACT.Gelu,
                                         bias=b1_cols[:, bass.ds(CT * q + k, 1)], scale=DOWN).then_inc(hid_done, 1)
                act.wait_ge(hid_done, CT * q + CT)
                nc.scalar.activation(hid_16[hc % 2][0], hid, ACT.Copy, scale=UP).then_inc(hid_hi, 1)

            def out_high(e):
                act.wait_ge(eo_kept, 4 * e + 4)
                if not (isinstance(e, int) and e == 0):
                    act.wait_ge(comb_mm, T * e)
                nc.scalar.activation(eo_16[0], eo, ACT.Copy).then_inc(eo_hi, 1)

            def expert(e, first=False, last=False):
                chunk_high(e, 2)
                if not first:
                    out_high(e - 1)
                hidden(e, 1, 1)
                chunk_high(e, 3)
                chunk_high(e, 4)
                hidden(e, 2, 3)
                chunk_high(e, 5)
                chunk_high(e, 6)
                hidden(e, 3, 5)
                chunk_high(e, 7)
                if not last:
                    chunk_high(e, 8)
                    hidden(e + 1, 0, -1)
                    chunk_high(e, 9)

            act.wait_ge(comb_moved, 32 * GROUPS)
            chunk_high(0, 1)
            act.wait_ge(bias_loaded, 32)
            hidden(0, 0, 0)
            expert(0, first=True)
            with act.Fori(1, E - 1) as e:
                expert(e)
            expert(E - 1, last=True)
            out_high(E - 1)

        @block.vector
        def _(dve):
            steps = [0]

            def link(ins):
                steps[0] += 1
                ins.then_inc(dve_step, 1)
                dve.wait_ge(dve_step, steps[0])

            def lo_part(pair, u):
                dve.wait_ge(split_hi, 2 * pair + u + 1)
                nc.vector.scalar_tensor_tensor(flat(wlo[:, u, :, :]), raw[:, u, :], UP, flat(whi[:, u, :, :]),
                                               ALU.mult, ALU.subtract).then_inc(split_lo, 1)

            roots = [0]

            def layernorm(dst, src, done):
                for t in range(T):
                    last = nc.vector.bn_stats(bn6[:, t, :], src[:, t, :])
                link(last)
                for t in range(T):
                    last = nc.vector.bn_aggr(mean_var[:, t, :], bn6[:, t, :])
                link(last)
                nc.vector.tensor_scalar(var_eps[:, 0:T], mean_var[:, :, 1], EPS, None, ALU.add).then_inc(var_ready, 1)
                roots[0] += 1
                dve.wait_ge(std_ready, roots[0])
                link(nc.vector.reciprocal(rstd[:, 0:T], std[:, 0:T]))
                for t in range(T):
                    nc.vector.tensor_scalar(dst[:, t, :], src[:, t, :], mean_var[:, t, 0:1], rstd[:, t:t + 1],
                                            ALU.subtract, ALU.mult).then_inc(done, 1)

            def turn_lo(first, tiles, dst, hi, scale):
                for t in range(tiles):
                    dve.wait_ge(turned_hi, first + t + 1)
                    nc.vector.scalar_tensor_tensor(
                        dst[:, :, t * P:(t + 1) * P],
                        psum[:, (first + t) % 4, :].rearrange("p (c n) -> p c n", c=DC), scale,
                        hi[:, :, t * P:(t + 1) * P], ALU.mult, ALU.subtract).then_inc(turned_lo, 1)

            def diagonals():
                return nc.vector.tensor_tensor(diag[:, :, :], ident.unsqueeze(1).broadcast_to([P, 4, P]),
                                               col[:, :].unsqueeze(2).broadcast_to([P, 4, P]), ALU.mult)

            dve.wait_ge(const_loaded, 32)
            nc.vector.tensor_copy(ident16[:, :], ident).then_inc(setup_done, 1)
            nc.vector.memset(one16[:, :], 1.0).then_inc(setup_done, 1)
            nc.vector.memset(exp_up[:, :], EXP_UP).then_inc(setup_done, 1)
            link(nc.vector.tensor_copy(lens_f[:, :], lens_i[:, :]))
            dve.wait_ge(x_loaded, 16)
            layernorm(nat, nat, rows_ready)
            lo_part(0, 0)
            turn_lo(TURN_X, T, qT[1], qT[0], UP)

            for b in range(B):
                link(nc.vector.tensor_scalar(qneg[:, :], cst[:, C_QPOS:C_QPOS + NQ], lens_f[:, b:b + 1],
                                             NEG * D ** 0.5 / DOWN, ALU.is_ge, ALU.mult))
                link(nc.vector.tensor_scalar(kmask[:, :], cst[:, C_KPOS:C_KPOS + KT], lens_f[:, b:b + 1],
                                             None, ALU.is_ge))
                if b:
                    dve.wait_ge(o_moved, 16)

                def keep_scores(i, u, k):
                    tile = CT * (2 * i + u - 2 * KC * b) + k
                    dve.wait_ge(products, 4 * (2 * i + u) + k + 1)
                    nc.vector.scalar_tensor_tensor(
                        flat(S[:, bass.ds(tile, 1), :]), qneg[:, :],
                        kmask[:, bass.ds(tile, 1)], psum[:, k, :], ALU.mult, ALU.add).then_inc(scores_kept, 1)

                def keep_maximum(i, u, k):
                    tile = CT * (2 * i + u - 2 * KC * b) + k
                    dve.wait_ge(scores_kept, KT * b + tile + 1)
                    dve.wait_ge(max_kept, (KT + 1) * b + tile + 1)
                    nc.vector.tensor_tensor(run_max[:, :], run_max[:, :], flat(S[:, bass.ds(tile, 1), :]),
                                            ALU.max).then_inc(max_kept, 1)

                nc.vector.memset(run_max[:, :], -3.0e38).then_inc(max_kept, 1)
                start = b * N_CTX // 4
                with dve.Fori(start, start + KC // 2) as i:
                    for u in range(2):
                        keep_scores(i, u, 0)
                        lo_part(i + u, 1 - u)
                        for k in range(1, CT):
                            keep_scores(i, u, k)
                            keep_maximum(i, u, k - 1)
                        keep_maximum(i, u, CT - 1)
                dve.wait_ge(stat_mm, 3 * b + 1)
                link(nc.vector.tensor_reduce(col[:, :], psum[:, 0, :].rearrange("p (a n) -> p a n", a=QT),
                                             AX.X, ALU.max))
                diagonals().then_inc(stat_dve, 1)
                dve.wait_ge(stat_mm, 3 * b + 2)
                link(nc.vector.tensor_copy(bcast[:, :], psum[:, 1, :]))

                def shift(i, u):
                    s = S[:, bass.ds(CT * (2 * i + u - KC * (2 * b + 1)), CT), :]
                    nc.vector.tensor_tensor(s, s, bcast[:, :].unsqueeze(1).broadcast_to([P, CT, 512]),
                                            ALU.subtract).then_inc(shifted, 1)

                def p_low(i, u):
                    j = 2 * i + u - KC * (2 * b + 1)
                    dve.wait_ge(p_hi, KC * b + j + 1)
                    nc.vector.tensor_tensor(pp[u][1], S[:, bass.ds(CT * j, CT), :], pp[u][0],
                                            ALU.subtract).then_inc(p_lo, 1)

                last = (b + 1) * N_CTX // 4
                start = last - KC // 2
                shift(start, 0)
                with dve.Fori(start, last - 1) as i:
                    shift(i, 1)
                    p_low(i, 0)
                    lo_part(i, 1)
                    shift(i + 1, 0)
                    p_low(i, 1)
                    lo_part(i + 1, 0)
                shift(last - 1, 1)
                p_low(last - 1, 0)
                lo_part(last - 1, 1)
                p_low(last - 1, 1)
                lo_part(last, 0)
                dve.wait_ge(stat_mm, 3 * b + 3)
                link(nc.vector.reciprocal(rcol[:, :], psum[:, CT - 1, 0:2 * QT].rearrange("p (a n) -> p a n", n=2)[:, :, 0]))
                for q in range(QT):
                    nc.vector.tensor_scalar(S[:, KT - QT + q, :], psum[:, 4 + q, :], rcol[:, q:q + 1], 1.0 / UP,
                                            ALU.mult, ALU.mult).then_inc(o_ready, 1)

            turn_lo(TURN_O, T, tT[1], tT[0], UP)
            dve.wait_ge(phase2_loaded, 16 * 6)
            nc.vector.tensor_copy(causal16[:, :], cst[:, C_CAUSAL:C_CAUSAL + P]).then_inc(setup_done, 1)
            link(nc.vector.tensor_tensor(resid, resid, qneg[:, :].unsqueeze(1).broadcast_to([P, T, 512]), ALU.add))
            lo_part(N_WQ // 2, N_WQ % 2)

            def keep_projection(n):
                for t in range(T):
                    dve.wait_ge(products, products_after(n - 1) + t + 1)
                    last = nc.vector.scalar_tensor_tensor(resid[:, t, :], psum[:, 4 + t % 4, :], DOWN, resid[:, t, :],
                                                          ALU.mult, ALU.add)
                    last.then_inc(proj_kept, 1)

            keep_projection(N_WO)
            dve.wait_ge(proj_kept, T)
            layernorm(nat, resid, rows_ready)
            turn_lo(TURN_HN, T, tT[1], tT[0], UP)

            def qkv_low(w, t, dst, hi):
                dve.wait_ge(qkv_hi, T * w + t + 1)
                src = psum[:, 4 + t % 4, :]
                if len(dst.shape) == 3:
                    src = src.rearrange("p (h d) -> p h d", h=H)
                nc.vector.scalar_tensor_tensor(dst, src, 1.0 / UP, hi, ALU.mult, ALU.subtract).then_inc(qkv_lo, 1)

            for w, n in enumerate((N_WQ, N_WK)):
                for t in range(T):
                    f, b = divmod(t, B)
                    qkv_low(w, t, *(qk[w][i][:, f, b * NQ:(b + 1) * NQ] for i in (1, 0)))
                    if t == 0:
                        lo_part((n + 1) // 2, (n + 1) % 2)
            for t in range(T):
                b, k = divmod(t, QT)
                qkv_low(2, t, *(v_nat[i][:, b * H:(b + 1) * H, k, :] for i in (1, 0)))
                if t == 0:
                    lo_part(N_WP // 2, N_WP % 2)

            def head_maxima(g, u):
                for n, (bank, tiles) in enumerate(SCORE_BANKS):
                    dve.wait_ge(head_scores, 3 * g + n + 1)
                    for q, at in tiles:
                        c = SCORE_COL[q]
                        last = nc.vector.tensor_reduce(head_max[:, u, c:c + 1], psum[:, bank, at:at + (q + 1) * P],
                                                       AX.X, ALU.max)
                    last.then_inc(head_reduced, 1)
                    dve.wait_ge(head_reduced, 3 * g + n + 1)
                    c0 = SCORE_COL[tiles[0][0]]
                    cols = slice(c0, c0 + len(tiles))
                    nc.vector.tensor_scalar(head_bias[:, u, cols], head_max[:, u, cols], -DOWN / HD ** 0.5, EXP_UP,
                                            ALU.mult, ALU.add).then_inc(head_maxed, 1)

            def head_decay(g, u):
                dve.wait_ge(head_turned, g + 1)
                if not (isinstance(g, int) and g < 2):
                    dve.wait_ge(head_lo, g - 1)
                for bank, tiles in TURN_BANKS:
                    for k, at in tiles:
                        width = (QT - k) * P
                        last = nc.vector.tensor_tensor(prob_t[u][:, BLOCK_AT[k]:BLOCK_AT[k] + width],
                                                       psum[:, bank, at:at + width], decay[:, 0:width], ALU.mult)
                last.then_inc(head_decayed, 1)

            def head_reciprocal(g, u):
                if not isinstance(g, int) or g >= 2:
                    dve.wait_ge(head_kept, g - 1)
                nc.vector.reciprocal(head_rec[:, u, :], head_sum[:, u, :]).then_inc(head_rec_ready, 1)

            def head_keep(g, u):
                dve.wait_ge(head_rec_ready, g + 1)
                dve.wait_ge(head_y, g + 1)
                nc.vector.scalar_tensor_tensor(
                    y_nat[:, :, bass.ds(g, 1), :].rearrange("p q a d -> p (q a) d"),
                    psum[:, 6 + u, 0:QT * HD].rearrange("p (q d) -> p q d", q=QT), 1.0 / UP,
                    head_rec[:, u, :].unsqueeze(2).broadcast_to([P, QT, HD]), ALU.mult, ALU.mult).then_inc(head_kept, 1)

            head_maxima(0, 0)
            for g in range(4):
                head_maxima(g + 1, 1 - g % 2)
                head_decay(g, g % 2)
                if g >= 2:
                    head_keep(g - 2, g % 2)
                head_reciprocal(g, g % 2)
            with dve.Fori(2, NH // 2 - 1) as i:
                for u in range(2):
                    head_maxima(2 * i + u + 1, 1 - u)
                    head_decay(2 * i + u, u)
                    head_keep(2 * i + u - 2, u)
                    head_reciprocal(2 * i + u, u)
            head_maxima(NH - 1, 1)
            for g in range(NH - 2, NH):
                head_decay(g, g % 2)
                head_keep(g - 2, g % 2)
                head_reciprocal(g, g % 2)
            head_keep(NH - 2, 0)
            head_keep(NH - 1, 1)

            turn_lo(TURN_Y, T, tT[1], tT[0], UP)
            lo_part(N_EXP // 2, N_EXP % 2)
            keep_projection(N_WP)
            dve.wait_ge(proj_kept, 2 * T)
            layernorm(nat, resid, z_ready)

            def rms_rows(first, n, buf, weight):
                roots[0] += 1
                dve.wait_ge(std_ready, roots[0])
                cols = slice(first, first + n)
                link(nc.vector.tensor_scalar(sq_root[:, cols], sq_root[:, cols], 1e-12, None, ALU.max))
                link(nc.vector.reciprocal(sq_rec[:, cols], sq_root[:, cols]))
                link(nc.vector.tensor_scalar(sq_rec[:, cols], sq_rec[:, cols], D ** 0.5, None, ALU.mult))
                for t in range(n):
                    nc.vector.scalar_tensor_tensor(buf[:, t, :], buf[:, t, :], sq_rec[:, first + t:first + t + 1],
                                                   weight, ALU.mult, ALU.mult).then_inc(rows_ready, 1)

            rms_rows(0, T, nat, run_max[:, :])
            rms_rows(T, M // P, se_nat, run_sum[:, :])
            for t in range(T):
                dve.wait_ge(xn_hi, t + 1)
                nc.vector.scalar_tensor_tensor(xn_nat[1][:, t, :], nat[:, t, :], UP, xn_nat[0][:, t, :],
                                               ALU.mult, ALU.subtract).then_inc(xn_lo, 1)
            turn_lo(TURN_XN, T, tT[1], tT[0], UP)
            turn_lo(TURN_SN, M // P, snT[1], snT[0], UP)

            def disp_low(g):
                dve.wait_ge(disp_hi, g + 1)
                nc.vector.tensor_tensor(disp_16[g % 2][1], disp, disp_16[g % 2][0], ALU.subtract).then_inc(disp_lo, 1)

            def disp_maxima(g):
                b, mc = divmod(g, MC)
                cols = slice(mc * 512, (mc + 1) * 512)
                nc.vector.tensor_reduce(bcast[:, :], L[:, :, cols].rearrange("p q n -> p n q"),
                                        AX.X, ALU.max).then_inc(cmax_ready, 1)
                dve.wait_ge(max_mm, 2 * g + 1)
                link(nc.vector.tensor_reduce(col[:, :], psum[:, 4, :].rearrange("p (a n) -> p a n", a=4),
                                             AX.X, ALU.max))
                diagonals().then_inc(max_diag, 1)
                if mc:
                    disp_low(g - 1)
                if g:
                    dve.wait_ge(disp_lo, g)
                dve.wait_ge(max_mm, 2 * g + 2)
                nc.vector.tensor_tensor(disp, L[:, :, cols],
                                        psum[:, 5, :].unsqueeze(1).broadcast_to([P, QT, 512]),
                                        ALU.subtract).then_inc(disp_shift, 1)

            def disp_slots(g):
                dve.wait_ge(sum_mm, 2 * g + 1)
                link(nc.vector.reciprocal(col[:, :], psum[:, 4, 0:8].rearrange("p (a n) -> p a n", n=2)[:, :, 0]))
                diagonals().then_inc(sum_diag, 1)
                dve.wait_ge(sum_mm, 2 * g + 2)
                link(nc.vector.tensor_copy(qneg[:, :], psum[:, 5, :]))
                if g:
                    dve.wait_ge(slot_lo, g)
                for c in range(DC):
                    dve.wait_ge(slot_mm, 4 * g + c + 1)
                    nc.vector.tensor_tensor(slots[:, c, :], psum[:, 6 + c % 2, :], qneg[:, :],
                                            ALU.mult).then_inc(slot_kept, 1)

            def combine_low(g):
                for m in range(4):
                    dve.wait_ge(comb_hi, 4 * g + m + 1)
                    nc.vector.tensor_tensor(comb_16[1][:, m, :], psum[:, 2 + m % 2, :], comb_16[0][:, m, :],
                                            ALU.subtract).then_inc(comb_lo, 1)

            for b in range(B):
                for q in range(QT):
                    dve.wait_ge(logit_kept, QT * MC * b + MC * (q + 1))
                    last = nc.vector.tensor_reduce(row_max[:, q:q + 1], L[:, q, :], AX.X, ALU.max)
                link(last)
                nc.vector.tensor_scalar(row_bias[:, b, :], row_max[:, :], -1.0, EXP_UP, ALU.mult,
                                        ALU.add).then_inc(row_biased, 1)
                disp_maxima(MC * b)
                for mc in range(MC):
                    g = MC * b + mc
                    if mc + 1 < MC:
                        disp_maxima(g + 1)
                    else:
                        disp_low(g)
                    combine_low(g)
                    disp_slots(g)
            dve.wait_ge(comb_exp, GROUPS)
            link(nc.vector.tensor_reduce(row_rec[:, :], row_sum[:, :, :, :].rearrange("p b q m -> p (b q) m"),
                                         AX.X, ALU.add))
            link(nc.vector.reciprocal(row_rec[:, :], row_rec[:, :]))
            link(nc.vector.tensor_scalar(row_rec[:, :], row_rec[:, :], 1.0 / UP, None, ALU.mult))

            def chunk_low(e, s):
                n = N_EXP + s
                dve.wait_ge(split_hi, 8 * e + n + 1)
                nc.vector.scalar_tensor_tensor(flat(wlo[:, n % 2, :, :]), raw[:, n % 2, :], UP,
                                               flat(whi[:, n % 2, :, :]), ALU.mult, ALU.subtract).then_inc(split_lo, 1)

            def hidden_low(e, hc):
                dve.wait_ge(hid_hi, HC * e + hc + 1)
                nc.vector.scalar_tensor_tensor(hid_16[hc % 2][1], hid, UP, hid_16[hc % 2][0],
                                               ALU.mult, ALU.subtract).then_inc(hid_lo, 1)

            def keep_out(e):
                for r in range(4):
                    dve.wait_ge(products, products_after(N_EXP - 1) + 4 * (8 * e + (8 if not isinstance(e, int) or e < E - 1 else 7) + 1))
                    nc.vector.scalar_tensor_tensor(eo[:, r, :], psum[:, 4 + r, :], 1.0 / UP,
                                                   flat(b2_rows[:, bass.ds(e, 1), :]), ALU.mult, ALU.add).then_inc(eo_kept, 1)

            def out_low(e):
                dve.wait_ge(eo_hi, e + 1)
                nc.vector.tensor_tensor(eo_16[1], eo, eo_16[0], ALU.subtract).then_inc(eo_lo, 1)

            def keep_combined(e):
                for t in range(T):
                    dve.wait_ge(comb_mm, T * e + t + 1)
                    nc.vector.scalar_tensor_tensor(resid[:, t, :], psum[:, t % 4, :], row_rec[:, t:t + 1],
                                                   resid[:, t, :], ALU.mult, ALU.add).then_inc(comb_kept, 1)

            def expert(e, first=False, last=False):
                if not first:
                    keep_out(e - 1)
                chunk_low(e, 2)
                if not first:
                    out_low(e - 1)
                hidden_low(e, 1)
                chunk_low(e, 3)
                if not first:
                    keep_combined(e - 1)
                chunk_low(e, 4)
                hidden_low(e, 2)
                chunk_low(e, 5)
                chunk_low(e, 6)
                hidden_low(e, 3)
                chunk_low(e, 7)
                if not last:
                    chunk_low(e, 8)
                    hidden_low(e + 1, 0)
                    chunk_low(e, 9)

            dve.wait_ge(bias_loaded, 32)
            link(nc.vector.tensor_scalar(b2_rows, b2_rows, UP, None, ALU.mult))
            chunk_low(0, 1)
            hidden_low(0, 0)
            expert(0, first=True)
            with dve.Fori(1, E - 1) as e:
                expert(e)
            expert(E - 1, last=True)
            keep_out(E - 1)
            out_low(E - 1)
            keep_combined(E - 1)

        @block.tensor
        def _(pe):
            def product(out_, lhs, rhs, start, stop):
                nc.tensor.matmul(out_, lhs[0], rhs[0], start=start, stop=False)
                nc.tensor.matmul(out_, lhs[0], rhs[1], start=False, stop=False)
                return nc.tensor.matmul(out_, lhs[1], rhs[0], start=False, stop=stop)

            def turn(first, tiles, src):
                for t in range(tiles):
                    src_ready(first, t)
                    if first + t >= 4:
                        pe.wait_ge(turned_lo, first + t - 3)
                    for c in range(DC):
                        last = nc.tensor.transpose(psum[:, (first + t) % 4, c * P:(c + 1) * P], src(t, c), ident)
                    last.then_inc(turned, 1)

            def src_ready(first, t):
                rows = {TURN_X: ROWS_X, TURN_HN: ROWS_HN, TURN_XN: ROWS_XN, TURN_SN: ROWS_SN}
                if first in rows:
                    pe.wait_ge(rows_ready, rows[first] + t + 1)

            def rows_of(buf):
                return lambda t, c: buf[:, t, c * P:(c + 1) * P]

            w = [[x_[:, u, :, :] for x_ in (whi, wlo)] for u in range(2)]

            pe.wait_ge(const_loaded, 32)
            turn(TURN_X, T, rows_of(nat))
            pe.wait_ge(turned_lo, T)

            for b in range(B):
                def scores(i, u):
                    j = 2 * i + u - 2 * KC * b
                    pe.wait_ge(split_lo, 2 * i + u + 1)
                    for k in range(CT):
                        if not (isinstance(j, int) and j == 0):
                            pe.wait_ge(scores_kept, KT * b + CT * (j - 1) + k + 1)
                        elif b and k == CT - 1:
                            pe.wait_ge(o_ready, QT * b)
                        for c in range(DC):
                            last = product(psum[:, k, :], [x_[:, c, k * P:(k + 1) * P] for x_ in w[u]],
                                           [x_[:, c, b * NQ:(b + 1) * NQ] for x_ in qT], c == 0, c == DC - 1)
                        last.then_inc(products, 1)

                start = b * N_CTX // 4
                scores(start, 0)
                scores(start, 1)
                with pe.Fori(start + 1, start + KC // 2) as i:
                    scores(i, 0)
                    scores(i, 1)

                pe.wait_ge(max_kept, (KT + 1) * (b + 1))
                for q in range(QT):
                    last = nc.tensor.transpose(psum[:, 0, q * P:(q + 1) * P], run_max[:, q * P:(q + 1) * P], ident)
                last.then_inc(stat_mm, 1)
                pe.wait_ge(stat_dve, b + 1)
                nc.tensor.matmul(psum[:, 1, :], ones, diag[:, :, :].rearrange("p a n -> p (a n)"),
                                 start=True, stop=True).then_inc(stat_mm, 1)

                def values(i, u, first=False, last=False):
                    j = 2 * i + u - KC * (2 * b + 1)
                    pe.wait_ge(split_lo, 2 * i + u + 1)
                    pe.wait_ge(p_lo, KC * b + j + 1)
                    for q in range(QT):
                        for k in range(CT):
                            done = product(psum[:, 4 + q, :], [x_[:, k, q * P:(q + 1) * P] for x_ in pp[u]],
                                           [x_[:, k, :] for x_ in w[u]], first and k == 0, last and k == CT - 1)
                        done.then_inc(products, 1)

                if b:
                    pe.wait_ge(o_ready, QT * b)
                last_pair = (b + 1) * N_CTX // 4 - 1
                start = last_pair + 1 - KC // 2
                values(start, 0, first=True)
                values(start, 1)
                with pe.Fori(start + 1, last_pair) as i:
                    values(i, 0)
                    values(i, 1)
                values(last_pair, 0)
                values(last_pair, 1, last=True)
                pe.wait_ge(sum_kept, (KT + 1) * (b + 1))
                for q in range(QT):
                    done = nc.tensor.matmul(psum[:, CT - 1, 2 * q:2 * q + 2], run_sum[:, q * P:(q + 1) * P], ones[:, 0:2],
                                            start=True, stop=True)
                done.then_inc(stat_mm, 1)

            def project(n, first):
                pe.wait_ge(split_lo, n + 1)
                for t in range(T):
                    pe.wait_ge(turned_lo, first + t + 1)
                    if t >= 4:
                        pe.wait_ge(proj_kept, (T if n == N_WP else 0) + t - 3)
                    for c in range(DC):
                        last = product(psum[:, 4 + t % 4, :], [x_[:, c, t * P:(t + 1) * P] for x_ in tT],
                                       [x_[:, c, :] for x_ in w[n % 2]], c == 0, c == DC - 1)
                    last.then_inc(products, 1)

            pe.wait_ge(o_ready, T)
            pe.wait_ge(phase2_loaded, 16 * 6)
            turn(TURN_O, T, rows_of(o_nat))
            project(N_WO, TURN_O)
            turn(TURN_HN, T, rows_of(nat))

            pe.wait_ge(turned_lo, TURN_HN + T)
            pe.wait_ge(proj_kept, T)
            for k, n in enumerate((N_WQ, N_WK, N_WV)):
                pe.wait_ge(split_lo, n + 1)
                for t in range(T):
                    if T * k + t >= 4:
                        pe.wait_ge(qkv_lo, T * k + t - 3)
                    f, b = divmod(t, B)
                    for c in range(DC):
                        if n == N_WV:
                            lhs = [x_[:, c, t * P:(t + 1) * P] for x_ in tT]
                            rhs = [x_[:, c, :] for x_ in w[n % 2]]
                        else:
                            lhs = [x_[:, c, f * P:(f + 1) * P] for x_ in w[n % 2]]
                            rhs = [x_[:, c, b * NQ:(b + 1) * NQ] for x_ in tT]
                        last = product(psum[:, 4 + t % 4, :], lhs, rhs, c == 0, c == DC - 1)
                    last.then_inc(products, 1)

            q_heads, k_heads = (s_.rearrange("p b h n -> p (b h n)") for s_ in (q_stack, k_stack))

            def score_head(g, u):
                for n, (bank, tiles) in enumerate(SCORE_BANKS):
                    if not (isinstance(g, int) and g == 0):
                        pe.wait_ge(head_exp, 3 * (g - 1) + n + 1)
                    for q, at in tiles:
                        width = (q + 1) * P
                        nc.tensor.matmul(psum[:, bank, at:at + width], q_heads[:, bass.ds(NQ * g + q * P, P)],
                                         k_heads[:, bass.ds(NQ * g, width)], start=True, stop=False)
                        last = nc.tensor.matmul(psum[:, bank, at + q * P:at + width], ident16[:, :], causal16[:, :],
                                                start=False, stop=True)
                    last.then_inc(head_scores, 1)

            def turn_head(g, u):
                pe.wait_ge(head_exp, 3 * g + 3)
                if not (isinstance(g, int) and g == 0):
                    pe.wait_ge(head_decayed, g)
                for bank, tiles in TURN_BANKS:
                    for k, at in tiles:
                        for q in range(k, QT):
                            a_ = at + (q - k) * P
                            src = PROB_AT[q] + k * P
                            last = nc.tensor.transpose(psum[:, bank, a_:a_ + P], prob[u][:, src:src + P], ident)
                last.then_inc(head_turned, 1)

            v_heads = [v_.rearrange("p g k d -> p (g k d)") for v_ in v_nat]

            def head_out(g, u):
                pe.wait_ge(head_lo, g + 1)
                if not (isinstance(g, int) and g < 2):
                    pe.wait_ge(head_kept, g - 1)
                for q in range(QT):
                    for k in range(q + 1):
                        at = BLOCK_AT[k] + (q - k) * P
                        last = product(psum[:, 6 + u, q * HD:(q + 1) * HD],
                                       [x_[:, at:at + P] for x_ in prob_16[u]],
                                       [x_[:, bass.ds(QT * HD * g + k * HD, HD)] for x_ in v_heads], k == 0, k == q)
                last.then_inc(head_y, 1)

            pe.wait_ge(q_stacked, STACKED)
            pe.wait_ge(k_stacked, STACKED)
            pe.wait_ge(qkv_lo, 3 * T)
            pe.wait_ge(setup_done, 4)
            score_head(0, 0)
            for g in range(4):
                score_head(g + 1, 1 - g % 2)
                turn_head(g, g % 2)
                if g >= 2:
                    head_out(g - 2, g % 2)
            with pe.Fori(2, NH // 2 - 1) as i:
                for u in range(2):
                    score_head(2 * i + u + 1, 1 - u)
                    turn_head(2 * i + u, u)
                    head_out(2 * i + u - 2, u)
            score_head(NH - 1, 1)
            for g in range(NH - 2, NH):
                turn_head(g, g % 2)
                head_out(g - 2, g % 2)
            head_out(NH - 2, 0)
            head_out(NH - 1, 1)

            pe.wait_ge(head_kept, NH)
            turn(TURN_Y, T, lambda t, c: y_nat[:, t % QT, H * (t // QT) + 4 * c:H * (t // QT) + 4 * c + 4, :].rearrange(
                "p h d -> p (h d)"))
            project(N_WP, TURN_Y)
            turn(TURN_XN, T, rows_of(nat))
            turn(TURN_SN, M // P, rows_of(se_nat))

            def maxima(g):
                pe.wait_ge(cmax_ready, g + 1)
                for m in range(4):
                    last = nc.tensor.transpose(psum[:, 4, m * P:(m + 1) * P], bcast[:, m * P:(m + 1) * P], ident)
                last.then_inc(max_mm, 1)
                pe.wait_ge(max_diag, g + 1)
                nc.tensor.matmul(psum[:, 5, :], ones, diag[:, :, :].rearrange("p a n -> p (a n)"),
                                 start=True, stop=True).then_inc(max_mm, 1)

            def slot_products(g):
                b, mc = divmod(g, MC)
                pe.wait_ge(disp_lo, g + 1)
                for m in range(4):
                    for q in range(QT):
                        for part in range(2):
                            last = nc.tensor.matmul(psum[:, 4, 2 * m:2 * m + 2],
                                                    disp_16[g % 2][part][:, q, m * P:(m + 1) * P], one16[:, :],
                                                    start=q + part == 0, stop=q + part == QT)
                last.then_inc(sum_mm, 1)
                for c in range(DC):
                    if 4 * g + c >= 2:
                        pe.wait_ge(slot_kept, 4 * g + c - 1)
                    for q in range(QT):
                        last = product(psum[:, 6 + c % 2, :], [x_[:, QT * b + q, c * P:(c + 1) * P] for x_ in xn_nat],
                                       [x_[:, q, :] for x_ in disp_16[g % 2]], q == 0, q == QT - 1)
                    last.then_inc(slot_mm, 1)
                    if c == 0:
                        pe.wait_ge(sum_diag, g + 1)
                        if mc + 1 < MC:
                            pe.wait_ge(disp_shift, g + 2)
                        nc.tensor.matmul(psum[:, 5, :], ones, diag[:, :, :].rearrange("p a n -> p (a n)"),
                                         start=True, stop=True).then_inc(sum_mm, 1)

            def turn_combine(g):
                pe.wait_ge(comb_exp, g + 1)
                for m in range(4):
                    if 4 * g + m >= 2:
                        pe.wait_ge(comb_lo, 4 * g + m - 1)
                    for q in range(QT):
                        last = nc.tensor.transpose(psum[:, 2 + m % 2, q * P:(q + 1) * P],
                                                   comb[:, q, m * P:(m + 1) * P], ident)
                    last.then_inc(comb_turned, 1)

            pe.wait_ge(turned_lo, TURN_SN + M // P)
            pe.wait_ge(proj_kept, 2 * T)
            pe.wait_ge(xn_lo, T)
            for b in range(B):
                for k in range(QT * MC):
                    q, mc = divmod(k, MC)
                    if QT * MC * b + k >= 2:
                        pe.wait_ge(logit_kept, QT * MC * b + k - 1)
                    for c in range(DC):
                        at = (QT * b + q) * P
                        last = product(psum[:, k % 2, :], [x_[:, c, at:at + P] for x_ in tT],
                                       [x_[:, c, mc * 512:(mc + 1) * 512] for x_ in snT], c == 0, c == DC - 1)
                    last.then_inc(logit_mm, 1)
                maxima(MC * b)
                for mc in range(MC):
                    if mc + 1 < MC:
                        maxima(MC * b + mc + 1)
                    turn_combine(MC * b + mc)
                    slot_products(MC * b + mc)

            def first_products(e, hc, s, u):
                q = HC * e + hc
                n = N_EXP + s
                pe.wait_ge(split_lo, 8 * e + n + 1)
                for k in range(CT):
                    if not (isinstance(q, int) and q == 0):
                        pe.wait_ge(hid_done, CT * (q - 1) + k + 1)
                    for c in range(DC):
                        last = product(psum[:, k, :], [x_[:, c, k * P:(k + 1) * P] for x_ in w[n % 2]],
                                       [e_slots[u][:, i, c, :] for i in range(2)], c == 0, c == DC - 1)
                    last.then_inc(products, 1)

            def second_products(e, hc, s):
                q = HC * e + hc
                n = N_EXP + s
                pe.wait_ge(split_lo, 8 * e + n + 1)
                pe.wait_ge(hid_lo, q + 1)
                for k in range(CT):
                    for r in range(4):
                        last = product(psum[:, 4 + r, :], [x_[:, k, r * P:(r + 1) * P] for x_ in hid_16[hc % 2]],
                                       [x_[:, k, :] for x_ in w[n % 2]],
                                       hc == 0 and k == 0, hc == HC - 1 and k == CT - 1)
                    last.then_inc(products, 1)

            def combine(e, u, nth):
                pe.wait_ge(e_comb_in[u], 16 * nth)
                pe.wait_ge(eo_lo, e + 1)
                for t in range(T):
                    b, q = divmod(t, QT)
                    if t >= 4:
                        pe.wait_ge(comb_kept, T * e + t - 3)
                    for m in range(2):
                        last = product(psum[:, t % 4, :],
                                       [e_comb[u][:, i, 2 * b + m, q * P:(q + 1) * P] for i in range(2)],
                                       [x_[:, 2 * b + m, :] for x_ in eo_16], m == 0, m == 1)
                    last.then_inc(comb_mm, 1)

            def expert(e, u, nth, first=False, last=False):
                first_products(e, 1, 1, u)
                if not first:
                    pe.wait_ge(eo_kept, 4 * e)
                second_products(e, 0, 2)
                if not first:
                    pe.wait_ge(hid_done, CT * (HC * e + 1) + CT)
                    combine(e - 1, 1 - u, nth - (1 if u == 0 else 0))
                    pe.wait_ge(comb_kept, T * e)
                first_products(e, 2, 3, u)
                second_products(e, 1, 4)
                first_products(e, 3, 5, u)
                second_products(e, 2, 6)
                if not last:
                    pe.wait_ge(e_slots_in[1 - u], 16 * (nth + (1 if u == 1 else 0)))
                    first_products(e + 1, 0, -1 , 1 - u)
                    second_products(e, 3, 8)
                else:
                    second_products(e, 3, 7)

            pe.wait_ge(e_slots_in[0], 16)
            pe.wait_ge(comb_moved, 32 * GROUPS)
            first_products(0, 0, 0, 0)
            expert(0, 0, 1, first=True)
            with pe.Fori(0, E // 2 - 1) as i:
                expert(2 * i + 1, 1, i + 1)
                expert(2 * i + 2, 0, i + 2)
            expert(E - 1, 1, E // 2, last=True)
            pe.wait_ge(hid_done, CT * HC * E)
            combine(E - 1, 1, E // 2)


def kernel(**inputs):
    import numpy as np
    import concourse.bacc as bacc
    from concourse.bass_utils import run_bass_kernel_spmd

    a = {k: np.asarray(v) for k, v in inputs.items()}

    def cut(m, inner):
        return m.reshape(-1, P, inner).transpose(1, 0, 2).reshape(P, -1)

    ctx = a["ctx_1024"]
    ctx_stream = np.empty((N_CTX, P, CT * 512), ctx.dtype)
    for b in range(B):
        turned = ctx[b].T
        for j in range(KC):
            part = slice(512 * j, 512 * (j + 1))
            ctx_stream[2 * KC * b + j] = cut(turned[:, part], 512)
            ctx_stream[2 * KC * b + KC + j] = cut(ctx[b, part, :], 512)
    w_attn = a["L0_attn_W_attn"]
    square_stream = np.stack([cut(a["L0_xattn_W"].T, 512)]
                             + [cut(w_attn[:, D * i:D * (i + 1)], 512) for i in range(3)]
                             + [cut(a["L0_attn_W_proj"], 512)])
    w1, w2 = a["L0_ffn_w1"], a["L0_ffn_w2"]

    def first(e, hc):
        return cut(w1[e][:, 512 * hc:512 * (hc + 1)], 512)

    def second(e, hc):
        return cut(w2[e][512 * hc:512 * (hc + 1), :], 512)

    order = [first(0, 0)]
    for e in range(E):
        for hc in range(1, HC):
            order += [first(e, hc), second(e, hc - 1)]
        if e + 1 < E:
            order.append(first(e + 1, 0))
        order.append(second(e, HC - 1))
    expert_stream = np.stack(order)

    consts = np.zeros((2, P, C_END), np.float32)
    rows = np.arange(P)
    consts[:, rows, C_ID + rows] = 1.0
    consts[:, :, C_ONE:C_ONE + P] = 1.0
    consts[0, :, C_QPOS:C_QPOS + NQ] = np.arange(NQ)
    consts[0, :, C_KPOS:C_KPOS + KT] = rows[:, None] + P * np.arange(KT)
    length, echoic = 1024, 16
    fall = 1.0 - np.linspace(0.0, 1.0, length - echoic + 1) ** (1.0 / np.e)
    values = np.concatenate([np.ones(echoic - 1), fall])
    back = np.arange(QT * P)[None, :] - rows[:, None]
    consts[1, :, C_DECAY:C_DECAY + QT * P] = np.where(back >= 0, values[np.maximum(back, 0)], 0.0)
    consts[1, :, C_CAUSAL:C_CAUSAL + P] = np.where(rows[None, :P] <= rows[:, None], 0.0, MASKED)

    arrays = {
        "x": a["x"], "ctx_stream": ctx_stream, "square_stream": square_stream, "expert_stream": expert_stream,
        "lens": a["_lenS2"], "xattn_b": a["L0_xattn_b"], "gamma": a["L0_ffn_norm_gamma"],
        "slot_gamma": a["L0_ffn_slot_norm_gamma"], "slot_embeds": a["L0_ffn_slot_embeds"].reshape(M, D),
        "b1": np.ascontiguousarray(a["L0_ffn_b1"].reshape(E * HID // P, P).T), "b2": a["L0_ffn_b2"],
        "consts": consts,
    }
    arrays = {k: np.ascontiguousarray(v) for k, v in arrays.items()}
    nc = bacc.Bacc("TRN2", target_bir_lowering=False, num_devices=1)
    handles = {k: nc.dram_tensor(f"in_{k}", v.shape, mybir.dt.from_np(v.dtype), kind="ExternalInput").ap()
               for k, v in arrays.items()}
    out = nc.dram_tensor("out", a["x"].shape, F32, kind="ExternalOutput").ap()
    program(nc, **handles, out=out)
    result = run_bass_kernel_spmd(nc, [{f"in_{k}": v for k, v in arrays.items()}], core_ids=[0])
    return result.results[0]["out"]
```

```python
from contextlib import ExitStack

import concourse.bass as bass
from concourse import mybir

ALU = mybir.AluOpType
ACT = mybir.ActivationFunctionType
AX = mybir.AxisListType
F32 = mybir.dt.float32
F16 = mybir.dt.float16
BF16 = mybir.dt.bfloat16
I32 = mybir.dt.int32

P = 128
D = 512
DC = D // P
B = 2
NQ = 512
QT = NQ // P
T = B * QT
NK = 8192
KT = NK // P
CT = 4
KC = KT // CT
H = 16
HD = D // H
E = 8
ES = 256
M = E * ES
HID = 2048
HC = HID // 512
MC = M // 512

UP = 32.0
DOWN = 1.0 / (UP * UP)
EXP_UP = 7.0
NEG = -1e13
EPS = 1e-5
MASKED = -1e30

C_ID = 0
C_ONE = C_ID + P
C_SET = C_ONE + P
C_QPOS = C_SET
C_KPOS = C_QPOS + NQ
C_DECAY = C_SET
C_CAUSAL = C_DECAY + QT * P
C_END = C_CAUSAL + P

N_CTX = B * 2 * KC
N_WO, N_WQ, N_WK, N_WV, N_WP = range(N_CTX, N_CTX + 5)
N_EXP = N_CTX + 5
GROUPS = B * MC
COMBINED = [[], []] + [[c] for c in range(MC)] + [[c, c + 1] for c in range(MC, GROUPS, 2)]
SMALL = 8


def products_after(n):
    if isinstance(n, int) and n >= N_CTX:
        if n < N_EXP:
            return 4 * N_CTX + SMALL * (n + 1 - N_CTX)
        return 4 * N_CTX + SMALL * 5 + 4 * (n + 1 - N_EXP)
    return 4 * n + 4


def program(nc, x, ctx_stream, square_stream, expert_stream, lens, xattn_b, gamma, slot_gamma,
            slot_embeds, b1, b2, consts, out):
    with ExitStack() as ctx:
        def sb(name, shape, dt):
            return ctx.enter_context(nc.sbuf_tensor(name, shape, dt))

        def sem(name):
            return ctx.enter_context(nc.semaphore(name))

        def dram(name, shape, dt):
            return nc.dram_tensor(name, shape, dt, kind="Internal").ap()

        psum = ctx.enter_context(nc.psum_tensor("psum", [P, 8, 512], F32))
        S = sb("S", [P, KT, 512], F32)
        A = sb("A", [P, 16, 512], F32)
        raw = sb("raw", [P, 2, CT * 512], F32)
        whi = sb("whi", [P, 2, CT, 512], F16)
        wlo = sb("wlo", [P, 2, CT, 512], F16)
        cst = sb("cst", [P, C_END], F32)
        run_max = sb("run_max", [P, 512], F32)
        run_sum = sb("run_sum", [P, 512], F32)
        bcast = sb("bcast", [P, 512], F32)
        diag = sb("diag", [P, 4, P], F32)
        qneg = sb("qneg", [P, 512], F32)
        lens_i = sb("lens_i", [P, B], I32)
        lens_f = sb("lens_f", [P, B], F32)
        kmask = sb("kmask", [P, KT], F32)
        col = sb("col", [P, 4], F32)
        rcol = sb("rcol", [P, 4], F32)
        ident16 = sb("ident16", [P, P], BF16)
        causal16 = sb("causal16", [P, P], BF16)
        one16 = sb("one16", [P, 2], F16)
        bn6 = sb("bn6", [P, T, 6], F32)
        mean_var = sb("mean_var", [P, T, 2], F32)
        var_eps = sb("var_eps", [P, 2 * T], F32)
        std = sb("std", [P, 2 * T], F32)
        rstd = sb("rstd", [P, 2 * T], F32)
        table = sb("table", [P, B], F32)
        exp_up = sb("exp_up", [P, 1], F32)
        head_max = sb("head_max", [P, 2, QT], F32)
        head_bias = sb("head_bias", [P, 2, QT], F32)
        head_sum = sb("head_sum", [P, 2, QT], F32)
        head_rec = sb("head_rec", [P, 2, QT], F32)
        row_max = sb("row_max", [P, QT], F32)
        row_part = sb("row_part", [P, MC, QT], F32)
        row_bias = sb("row_bias", [P, B, QT], F32)
        row_sum = sb("row_sum", [P, B, QT, MC], F32)
        row_rec = sb("row_rec", [P, T], F32)
        sq_sum = sb("sq_sum", [P, T + M // P], F32)
        sq_root = sb("sq_root", [P, T + M // P], F32)
        sq_rec = sb("sq_rec", [P, T + M // P], F32)

        ident = cst[:, C_ID:C_ID + P]
        ones = cst[:, C_ONE:C_ONE + P]
        decay = cst[:, C_DECAY:C_DECAY + QT * P]

        def view(buf, at, n, dt, *dims):
            v = buf[:, at:at + n, :].rearrange("p a b -> p (a b)")
            if dt != F32:
                v = v.bitcast(dt)
            names = "abc"[:len(dims)]
            if len(dims) > 1:
                v = v.rearrange(f"p ({' '.join(names)}) -> p {' '.join(names)}", **dict(zip(names, dims)))
            return v

        def flat(v):
            return v.rearrange("p a n -> p (a n)")

        NH = B * H
        qT = [view(A, 4 * i, 4, F16, DC, T * P) for i in range(2)]
        pp = [[view(A, 8 + 4 * u + 2 * i, 2, F16, CT, 512) for i in range(2)] for u in range(2)]
        x_nat = [view(S, 16, 4, F32, QT, 512), view(A, 12, 4, F32, QT, 512)]
        resid = view(S, 0, 8, F32, T, 512)
        tT = [view(S, 8 + 4 * i, 4, F16, DC, T * P) for i in range(2)]
        nat = view(S, 16, 8, F32, T, 512)
        q_stack = view(S, 24, 16, F16, B, H, NQ)
        k_stack = view(S, 40, 16, F16, B, H, NQ)
        o_nat = view(S, 56, 8, F32, T, 512)
        v_nat = [view(S, 56 + 4 * i, 4, F16, NH, QT, HD) for i in range(2)]
        y_nat = view(S, 16, 8, F32, QT, NH, HD)
        qk = [[view(A, 8 * w + 4 * i, 4, F16, QT, T * P) for i in range(2)] for w in range(2)]
        a_flat = flat(A[:, :, :])
        NB = QT * (QT + 1) // 2 * P
        prob = [a_flat[:, u * NB:(u + 1) * NB] for u in range(2)]
        prob_t = [a_flat[:, (2 + u) * NB:(3 + u) * NB] for u in range(2)]
        prob_16 = [[a_flat[:, (4 + u) * NB:(5 + u) * NB].bitcast(F16)[:, i * NB:(i + 1) * NB]
                    for i in range(2)] for u in range(2)]
        xn_nat = [view(S, 24 + 4 * i, 4, F16, T, 512) for i in range(2)]
        snT = [view(S, 32 + 8 * i, 8, F16, DC, M) for i in range(2)]
        L = view(S, 48, 16, F32, QT, M)
        se_nat = view(S, 48, 16, F32, M // P, 512)
        disp = view(A, 0, 4, F32, QT, 512)
        disp_16 = [[view(A, 4 + 4 * u + 2 * i, 2, F16, QT, 512) for i in range(2)] for u in range(2)]
        comb = view(A, 12, 4, F32, QT, 512)
        slots = view(S, 16, 4, F32, DC, 512)
        slots_16 = view(S, 20, 4, F16, 2, DC, 512)
        comb_16 = [whi[:, 0, :, :], wlo[:, 0, :, :]]
        e_slots = [view(S, 8 + 4 * u, 4, F16, 2, DC, 512) for u in range(2)]
        e_comb = [view(S, 16 + 4 * u, 4, F16, 2, 4, 512) for u in range(2)]
        hid = view(S, 24, 4, F32, CT, 512)
        hid_16 = [[view(S, 28 + 4 * u + 2 * i, 2, F16, CT, 512) for i in range(2)] for u in range(2)]
        eo = view(S, 48, 4, F32, 4, 512)
        eo_16 = [view(S, 44 + 2 * i, 2, F16, 4, 512) for i in range(2)]
        b2_rows = view(S, 36, 8, F32, E, 512)
        b1_cols = run_max[:, 0:E * HID // P]

        o_scratch = dram("o_scratch", [P, QT * 512], F32)
        slots_dram = dram("slots_dram", [E, P, 2, DC, B, ES], F16)
        comb_dram = dram("comb_dram", [E, P, 2, B, 2, NQ], F16)

        raw_loaded = [sem(f"raw_loaded{u}") for u in range(2)]
        split_hi = sem("split_hi")
        split_lo = sem("split_lo")
        products = sem("products")
        const_loaded = sem("const_loaded")
        x_loaded = [sem(f"x_loaded{b}") for b in range(B)]
        dve_step = sem("dve_step")
        setup_done = sem("setup_done")
        var_ready = sem("var_ready")
        std_ready = sem("std_ready")
        squares_ready = sem("squares_ready")
        z_ready = sem("z_ready")
        rows_ready = sem("rows_ready")
        turned = sem("turned")
        turned_hi = sem("turned_hi")
        turned_lo = sem("turned_lo")
        scores_kept = sem("scores_kept")
        max_kept = sem("max_kept")
        sum_kept = sem("sum_kept")
        stat_mm = sem("stat_mm")
        stat_dve = sem("stat_dve")
        shifted = sem("shifted")
        tile_shifted = sem("tile_shifted")
        tile_exp = sem("tile_exp")
        tile_hi = sem("tile_hi")
        tile_lo = sem("tile_lo")
        exp_done = sem("exp_done")
        p_hi = sem("p_hi")
        p_lo = sem("p_lo")
        o_ready = sem("o_ready")
        o_moved = sem("o_moved")
        phase2_loaded = sem("phase2_loaded")
        o_loaded = sem("o_loaded")
        slot_gamma_loaded = sem("slot_gamma_loaded")
        proj_kept = sem("proj_kept")
        qkv_hi = sem("qkv_hi")
        qkv_lo = sem("qkv_lo")
        q_stacked = sem("q_stacked")
        k_stacked = sem("k_stacked")
        head_scores = sem("head_scores")
        head_maxed = sem("head_maxed")
        head_reduced = sem("head_reduced")
        head_rec_ready = sem("head_rec_ready")
        head_exp = sem("head_exp")
        head_turned = sem("head_turned")
        head_decayed = sem("head_decayed")
        head_hi = sem("head_hi")
        head_lo = sem("head_lo")
        head_y = sem("head_y")
        head_kept = sem("head_kept")
        se_loaded = sem("se_loaded")
        xn_hi = sem("xn_hi")
        xn_lo = sem("xn_lo")
        logit_mm = sem("logit_mm")
        logit_kept = sem("logit_kept")
        row_biased = sem("row_biased")
        cmax_ready = sem("cmax_ready")
        max_mm = sem("max_mm")
        sum_mm = sem("sum_mm")
        max_diag = sem("max_diag")
        sum_diag = sem("sum_diag")
        disp_shift = sem("disp_shift")
        disp_exp = sem("disp_exp")
        disp_hi = sem("disp_hi")
        disp_lo = sem("disp_lo")
        slot_mm = sem("slot_mm")
        slot_kept = sem("slot_kept")
        slot_hi = sem("slot_hi")
        slot_lo = sem("slot_lo")
        first_moved = sem("first_moved")
        slot_moved = sem("slot_moved")
        comb_exp = sem("comb_exp")
        comb_turned = sem("comb_turned")
        comb_hi = sem("comb_hi")
        comb_lo = sem("comb_lo")
        comb_moved = sem("comb_moved")
        bias_loaded = sem("bias_loaded")
        e_slots_in = [sem(f"e_slots_in{u}") for u in range(2)]
        e_comb_in = [sem(f"e_comb_in{u}") for u in range(2)]
        hid_done = sem("hid_done")
        hid_hi = sem("hid_hi")
        hid_lo = sem("hid_lo")
        eo_kept = sem("eo_kept")
        eo_hi = sem("eo_hi")
        eo_lo = sem("eo_lo")
        comb_mm = sem("comb_mm")
        comb_kept = sem("comb_kept")
        stored = sem("stored")

        block = ctx.enter_context(nc.Block())

        TURN_X, TURN_O, TURN_HN, TURN_Y, TURN_XN, TURN_SN = (T * i for i in range(6))
        ROWS_X, ROWS_HN, ROWS_XN, ROWS_SN = 0, T, 2 * T, 3 * T
        SCORE_BANKS = [(0, [(0, 0), (2, P)]), (1, [(1, 0)]), (2, [(3, 0)])]
        SCORE_COL = {q: n for n, q in enumerate([0, 2, 1, 3])}
        TURN_BANKS = [(3, [(0, 0)]), (4, [(1, 0), (3, 3 * P)]), (5, [(2, 0)])]
        BLOCK_AT = {0: 0, 1: 512, 3: 512 + 3 * P, 2: 1024}
        PROB_AT = {q: q * (q + 1) // 2 * P for q in range(QT)}
        STACKED = 16 * B * (P // HD) ** 2

        N_CHUNKS = N_EXP + 2 * E * HC

        @block.sync
        def _(sp):
            x_rows = x.rearrange("b (t p) d -> p (b t) d", p=P)

            def load(u, src):
                sp.dma_start(raw[:, u, :], src).then_inc(raw_loaded[u], 16)

            sp.dma_start(x_nat[0], x_rows[:, 0:QT, :]).then_inc(x_loaded[0], 16)
            load(0, ctx_stream[0])
            sp.dma_start(cst[:, :], consts[0]).then_inc(const_loaded, 16)
            sp.dma_start(lens_i[:, :], lens.partition_broadcast(P)).then_inc(const_loaded, 16)
            sp.dma_start(x_nat[1], x_rows[:, QT:T, :]).then_inc(x_loaded[1], 16)
            load(1, ctx_stream[1])
            with sp.Fori(1, N_CTX // 2) as i:
                for u in range(2):
                    sp.wait_ge(split_lo, 2 * i + u - 1)
                    load(u, ctx_stream[bass.ds(2 * i + u, 1)].rearrange("a p n -> p (a n)"))
            sp.wait_ge(split_lo, N_WO - 1)
            load(N_WO % 2, square_stream[0])
            sp.wait_ge(p_lo, KC * (B - 1) + 2)
            sp.wait_ge(sum_kept, (KT + 1) * (B - 1) + 1 + 2 * CT)
            for dst, src in ((resid, x_rows), (cst[:, C_SET:C_END], consts[1][:, C_SET:C_END]),
                             (qneg[:, :], xattn_b.partition_broadcast(P)),
                             (run_max[:, :], gamma.partition_broadcast(P))):
                sp.dma_start(dst, src).then_inc(phase2_loaded, 16)
            sp.wait_ge(p_lo, KC * B - 1)
            sp.wait_ge(sum_kept, (KT + 1) * B - CT)
            sp.wait_ge(o_moved, 16)
            sp.dma_start(flat(o_nat[:, 0:QT, :]), o_scratch).then_inc(o_loaded, 16)
            sp.wait_ge(split_lo, N_WQ - 1)
            load(N_WQ % 2, square_stream[N_WQ - N_WO])
            sp.wait_ge(o_ready, T)
            sp.dma_start(run_sum[:, :], slot_gamma.partition_broadcast(P)).then_inc(slot_gamma_loaded, 16)
            for n in (N_WK, N_WV, N_WP):
                sp.wait_ge(split_lo, n - 1)
                load(n % 2, square_stream[n - N_WO])
            for w, (stack, done, parts) in enumerate(((q_stack, q_stacked, (0, 0, 1, 1)),
                                                      (k_stack, k_stacked, (0, 1, 0, 1)))):
                sp.wait_ge(qkv_lo, T * (w + 1))
                if w:
                    sp.wait_ge(split_lo, N_EXP - 1)
                    load(N_EXP % 2, expert_stream[0])
                for j in range(P // HD):
                    for g, part in enumerate(parts):
                        for b in range(B):
                            sp.dma_start(stack[HD * g:HD * (g + 1), b, j::P // HD, :],
                                         qk[w][part][HD * j:HD * (j + 1), :, b * NQ:(b + 1) * NQ]
                                         ).then_inc(done, 16)
            sp.wait_ge(head_y, NH)
            sp.dma_start(se_nat, slot_embeds.rearrange("(t p) d -> p t d", p=P)).then_inc(se_loaded, 16)
            sp.wait_ge(split_lo, N_EXP)
            load((N_EXP + 1) % 2, expert_stream[1])

            def load_expert(e, u, what):
                if what == "slots":
                    sp.dma_start(e_slots[u].rearrange("p a b n -> p (a b n)"),
                                 slots_dram[bass.ds(e, 1)].rearrange("e p a c b s -> p (e a c b s)")
                                 ).then_inc(e_slots_in[u], 16)
                else:
                    sp.dma_start(e_comb[u].rearrange("p a b n -> p (a b n)"),
                                 comb_dram[bass.ds(e, 1)].rearrange("e p a b m n -> p (e a b m n)")
                                 ).then_inc(e_comb_in[u], 16)

            def store_combine(g):
                b, mc = divmod(g, MC)
                sp.wait_ge(comb_lo, 4 * (g + 1))
                for part in range(2):
                    sp.dma_start(comb_dram[2 * mc:2 * mc + 2, :, part, b, :, :].rearrange("e p m n -> p e (m n)"),
                                 comb_16[part].rearrange("p (e m) n -> p e (m n)", e=2)).then_inc(comb_moved, 16)

            def store_slots(g):
                b, mc = divmod(g, MC)
                sp.wait_ge(slot_lo, g + 1)
                for e in range(2 * mc, 2 * mc + 2):
                    for part in range(2):
                        sp.dma_start(slots_dram[e, :, part, :, b, :],
                                     slots_16[:, part, :, (e % 2) * ES:(e % 2 + 1) * ES]
                                     ).then_inc(slot_moved if e else first_moved, 16)

            for g in range(GROUPS):
                for c in COMBINED[g][:1]:
                    store_combine(c)
                if g:
                    store_slots(g - 1)
                for c in COMBINED[g][1:]:
                    store_combine(c)
                if g == GROUPS - 2:
                    sp.wait_ge(first_moved, 32 * B)
                    sp.wait_ge(logit_mm, QT * GROUPS)
                    load_expert(0, 0, "slots")
                    sp.dma_start(b1_cols, b1).then_inc(bias_loaded, 16)
                    sp.dma_start(b2_rows, b2.partition_broadcast(P)).then_inc(bias_loaded, 16)
                    load(N_EXP % 2, expert_stream[2])
            store_slots(GROUPS - 1)

            def expert_loads(e, u, first=False, last=False):
                for s in range(3 if first else 2, 8 if last else 10):
                    n = N_EXP + s
                    sp.wait_ge(split_lo, 8 * e + n - 1)
                    load(n % 2, expert_stream[bass.ds(8 * e + s, 1)].rearrange("a p n -> p (a n)"))
                    if s == 3 and first:
                        sp.wait_ge(slot_moved, 64 * GROUPS - 32 * B)
                        sp.wait_ge(comb_moved, 32 * GROUPS)
                        load_expert(e, u, "comb")
                    if s == 3 and not last:
                        load_expert(e + 1, 1 - u, "slots")
                    if s == 8:
                        if not first:
                            sp.wait_ge(comb_mm, T * e)
                        load_expert(e + 1, 1 - u, "comb")

            expert_loads(0, 0, first=True)
            with sp.Fori(0, E // 2 - 1) as i:
                expert_loads(2 * i + 1, 1)
                expert_loads(2 * i + 2, 0)
            expert_loads(E - 1, 1, last=True)

            out_rows = out.rearrange("b (t p) d -> p (b t) d", p=P)
            for t in range(T):
                sp.wait_ge(comb_kept, T * (E - 1) + t + 1)
                sp.dma_start(out_rows[:, t, :], resid[:, t, :]).then_inc(stored, 16)
            sp.wait_ge(stored, 16 * T)

        @block.gpsimd
        def _(pool):
            for b in range(B):
                if b:
                    pool.wait_ge(stat_mm, 3 * b)
                nc.gpsimd.memset(run_sum[:, :], 0.0).then_inc(sum_kept, 1)
                with pool.Fori(0, KC) as j:
                    pool.wait_ge(exp_done, KC * b + j + 1)
                    for k in range(CT):
                        tile = 4 * j + k
                        pool.wait_ge(sum_kept, (KT + 1) * b + 1 + tile)
                        nc.gpsimd.tensor_tensor(
                            run_sum[:, :], run_sum[:, :], flat(S[:, bass.ds(tile, 1), :]),
                            ALU.add).then_inc(sum_kept, 1)
                if b == 0:
                    pool.wait_ge(o_ready, QT)
                    pool.dma_start(o_scratch, flat(S[:, KT - QT:KT, :])).then_inc(o_moved, 16)

            with pool.Fori(0, NH // 2) as i:
                for u in range(2):
                    pool.wait_ge(head_hi, 2 * i + u + 1)
                    nc.gpsimd.tensor_tensor(prob_16[u][1], prob_t[u], prob_16[u][0],
                                            ALU.subtract).then_inc(head_lo, 1)

            for g in range(GROUPS):
                pool.wait_ge(slot_hi, g + 1)
                nc.gpsimd.tensor_tensor(slots_16[:, 1, :, :], slots, slots_16[:, 0, :, :],
                                        ALU.subtract).then_inc(slot_lo, 1)

        @block.scalar
        def _(act):
            def hi_part(pair, u):
                n = 2 * pair + u
                act.wait_ge(raw_loaded[u], 16 * pair + 16)
                if not (isinstance(n, int) and n < 2):
                    act.wait_ge(products, products_after(n - 2))
                nc.scalar.activation(flat(whi[:, u, :, :]), raw[:, u, :], ACT.Copy, scale=UP).then_inc(split_hi, 1)

            roots = [0]

            def square_root(b):
                cols = slice(QT * b, QT * (b + 1))
                roots[0] += 1
                act.wait_ge(var_ready, roots[0])
                nc.scalar.activation(std[:, cols], var_eps[:, cols], ACT.Sqrt).then_inc(std_ready, 1)

            def turn_hi(first, tiles, dst, scale):
                for t in tiles:
                    act.wait_ge(turned, first + t + 1)
                    nc.scalar.activation(dst[:, :, t * P:(t + 1) * P],
                                         psum[:, (first + t) % 4, :].rearrange("p (c n) -> p c n", c=DC),
                                         ACT.Copy, scale=scale).then_inc(turned_hi, 1)

            square_root(0)
            hi_part(0, 0)
            turn_hi(TURN_X, range(0, QT), qT[0], UP)
            square_root(1)
            act.wait_ge(setup_done, 3)

            for b in range(B):
                start = b * N_CTX // 4
                if b == 0:
                    hi_part(0, 1)
                    hi_part(1, 0)
                with act.Fori(start + (b == 0), start + KC // 2) as i:
                    hi_part(i, 1)
                    hi_part(i + 1, 0)

                def probabilities(i, u):
                    j = 2 * i + u - KC * (2 * b + 1)
                    act.wait_ge(shifted, KC * b + j + 1)
                    act.nop(nofuse=True)
                    s = S[:, bass.ds(CT * j, CT), :]
                    nc.scalar.activation(s, s, ACT.Exp, bias=exp_up[:, 0:1],
                                         scale=DOWN / D ** 0.5).then_inc(exp_done, 1)
                    act.wait_ge(exp_done, KC * b + j + 1)
                    act.wait_ge(products, products_after(2 * i + u - 2))
                    act.nop(nofuse=True)
                    nc.scalar.activation(pp[u][0], s, ACT.Copy).then_inc(p_hi, 1)

                start += KC // 2
                nc.scalar.activation(table[:, b:b + 1], exp_up[:, 0:1], ACT.Exp)
                if b:
                    act.wait_ge(products, products_after(N_CTX // B - 1))
                for k in range(CT):
                    head_of = tile_shifted if k < CT - 1 else shifted
                    act.wait_ge(head_of, (CT - 1) * b + k + 1 if k < CT - 1 else KC * b + 1)
                    last = nc.scalar.activation(S[:, k, :], S[:, k, :], ACT.Exp, bias=exp_up[:, 0:1],
                                                scale=DOWN / D ** 0.5)
                    if k < CT - 1:
                        last.then_inc(tile_exp, 1)
                        act.wait_ge(tile_exp, (CT - 1) * b + k + 1)
                    else:
                        last.then_inc(exp_done, 1)
                        act.wait_ge(exp_done, KC * b + 1)
                    nc.scalar.activation(pp[0][0][:, k, :], S[:, k, :], ACT.Copy).then_inc(
                        tile_hi if k < CT - 1 else p_hi, 1)
                hi_part(start, 1)
                if b == 0:
                    turn_hi(TURN_X, range(QT, T), qT[0], UP)
                probabilities(start, 1)
                hi_part(start + 1, 0)
                with act.Fori(start + 1, start + KC // 2) as i:
                    probabilities(i, 0)
                    hi_part(i, 1)
                    probabilities(i, 1)
                    hi_part(i + 1, 0)

            turn_hi(TURN_O, range(T), tT[0], UP)
            hi_part(N_WQ // 2, N_WQ % 2)
            square_root(0)
            square_root(1)
            turn_hi(TURN_HN, range(0, QT), tT[0], UP)

            def qkv_high(n, t, dst):
                act.wait_ge(products, products_after(n - 1) + t + 1)
                src = psum[:, 4 + t % 4, :]
                if len(dst.shape) == 3:
                    src = src.rearrange("p (h d) -> p h d", h=H)
                nc.scalar.activation(dst, src, ACT.Copy, scale=1.0 / UP).then_inc(qkv_hi, 1)

            for w, n in enumerate((N_WQ, N_WK)):
                for t in range(T):
                    b, f = divmod(t, DC)
                    if n == N_WQ and t == QT:
                        turn_hi(TURN_HN, range(QT, T), tT[0], UP)
                    qkv_high(n, t, qk[w][0][:, f, b * NQ:(b + 1) * NQ])
                    if t == 0:
                        hi_part((n + 1) // 2, (n + 1) % 2)
            for t in range(T):
                b, k = divmod(t, QT)
                qkv_high(N_WV, t, v_nat[0][:, b * H:(b + 1) * H, k, :])
                if t == 0:
                    hi_part(N_WP // 2, N_WP % 2)

            def head_exponentials(g, u):
                for n, (bank, tiles) in enumerate(SCORE_BANKS):
                    act.wait_ge(head_maxed, 3 * g + n + 1)
                    if not (isinstance(g, int) and g < 2):
                        act.wait_ge(head_turned, g - 1)
                    for q, at in tiles:
                        c, width = SCORE_COL[q], (q + 1) * P
                        last = nc.scalar.activation(
                            prob[u][:, PROB_AT[q]:PROB_AT[q] + width], psum[:, bank, at:at + width], ACT.Exp,
                            bias=head_bias[:, u, c:c + 1], scale=DOWN / HD ** 0.5,
                            accum_out=head_sum[:, u, q:q + 1])
                    last.then_inc(head_exp, 1)

            def head_high(g, u):
                act.wait_ge(head_decayed, g + 1)
                if not (isinstance(g, int) and g < 2):
                    act.wait_ge(head_y, g - 1)
                nc.scalar.activation(prob_16[u][0], prob_t[u], ACT.Copy).then_inc(head_hi, 1)

            act.wait_ge(q_stacked, STACKED)
            act.wait_ge(k_stacked, STACKED)
            head_exponentials(0, 0)
            for g in range(4):
                head_exponentials(g + 1, 1 - g % 2)
                head_high(g, g % 2)
            with act.Fori(2, NH // 2 - 1) as i:
                for u in range(2):
                    head_exponentials(2 * i + u + 1, 1 - u)
                    head_high(2 * i + u, u)
            head_exponentials(NH - 1, 1)
            head_high(NH - 2, 0)
            head_high(NH - 1, 1)
            turn_hi(TURN_Y, range(T), tT[0], UP)
            hi_part(N_EXP // 2, N_EXP % 2)

            square_root(0)
            square_root(1)

            def squares(src, n):
                nc.scalar.activation(bcast[:, :], src, ACT.Square, accum_out=sq_sum[:, n:n + 1]).then_inc(squares_ready, 1)
                act.wait_ge(squares_ready, n + 1)

            for t in range(T):
                act.wait_ge(z_ready, t + 1)
                squares(nat[:, t, :], t)
            nc.scalar.activation(sq_root[:, 0:T], sq_sum[:, 0:T], ACT.Sqrt).then_inc(std_ready, 1)
            act.wait_ge(se_loaded, 16)
            for t in range(M // P):
                squares(se_nat[:, t, :], T + t)
            nc.scalar.activation(sq_root[:, T:], sq_sum[:, T:], ACT.Sqrt).then_inc(std_ready, 1)
            for t in range(T):
                act.wait_ge(rows_ready, ROWS_XN + t + 1)
                nc.scalar.activation(xn_nat[0][:, t, :], nat[:, t, :], ACT.Copy, scale=UP).then_inc(xn_hi, 1)
            turn_hi(TURN_XN, range(T), tT[0], UP)
            turn_hi(TURN_SN, range(M // P), snT[0], UP)

            def disp_high(g):
                act.wait_ge(disp_shift, g + 1)
                nc.scalar.activation(disp, disp, ACT.Exp, bias=exp_up[:, 0:1]).then_inc(disp_exp, 1)
                act.wait_ge(disp_exp, g + 1)
                if g >= 2:
                    act.wait_ge(slot_mm, 4 * (g - 1))
                nc.scalar.activation(disp_16[g % 2][0], disp, ACT.Copy).then_inc(disp_hi, 1)

            def combine_exp(g):
                b, mc = divmod(g, MC)
                act.wait_ge(row_biased, b + 1)
                if g:
                    act.wait_ge(comb_turned, 4 * g)
                for q in range(QT):
                    last = nc.scalar.activation(comb[:, q, :], L[:, q, mc * 512:(mc + 1) * 512], ACT.Exp,
                                                bias=row_bias[:, b, q:q + 1],
                                                accum_out=row_sum[:, b, q, mc:mc + 1])
                last.then_inc(comb_exp, 1)

            def combine_high(g):
                if g:
                    act.wait_ge(comb_moved, 32 * g)
                for m in range(4):
                    act.wait_ge(comb_turned, 4 * g + m + 1)
                    nc.scalar.activation(comb_16[0][:, m, :], psum[:, 2 + m % 2, :], ACT.Copy).then_inc(comb_hi, 1)

            def slots_high(g):
                act.wait_ge(slot_kept, 4 * g + 4)
                if g:
                    act.wait_ge(first_moved, 32 * ((g - 1) // MC + 1))
                    act.wait_ge(slot_moved, 64 * g - 32 * ((g - 1) // MC + 1))
                nc.scalar.activation(slots_16[:, 0, :, :], slots, ACT.Copy).then_inc(slot_hi, 1)

            def keep_logits(g, rows):
                b, mc = divmod(g, MC)
                if b:
                    act.wait_ge(disp_shift, g - MC + 1)
                    act.wait_ge(comb_exp, g - MC + 1)
                for q in rows:
                    act.wait_ge(logit_mm, QT * g + q + 1)
                    nc.scalar.activation(L[:, q, mc * 512:(mc + 1) * 512], psum[:, q % 2, :], ACT.Copy,
                                         scale=DOWN).then_inc(logit_kept, 1)

            for g in range(-2, GROUPS):
                combined = COMBINED[g] if g >= 0 else []
                for c in combined[:1]:
                    combine_exp(c)
                if g + 2 < GROUPS:
                    keep_logits(g + 2, range(0, 2))
                if g >= 1:
                    slots_high(g - 1)
                if g + 2 < GROUPS:
                    keep_logits(g + 2, range(2, QT))
                if 0 <= g + 1 < GROUPS:
                    disp_high(g + 1)
                for c in combined[:1]:
                    combine_high(c)
                for c in combined[1:]:
                    combine_exp(c)
                    combine_high(c)
            slots_high(GROUPS - 1)

            def chunk_high(e, s):
                n = N_EXP + s
                act.wait_ge(raw_loaded[n % 2], 16 * (4 * e + n // 2 + 1))
                act.wait_ge(products, products_after(N_EXP - 1) + 4 * (8 * e + s - 1))
                nc.scalar.activation(flat(whi[:, n % 2, :, :]), raw[:, n % 2, :], ACT.Copy, scale=UP).then_inc(split_hi, 1)

            def hidden(e, hc, s):
                q = HC * e + hc
                first = isinstance(q, int) and q == 0
                if not first:
                    act.wait_ge(hid_lo, q)
                for k in range(CT):
                    act.wait_ge(products, products_after(N_EXP - 1) + 4 * (8 * e + s) + k + 1)
                    act.nop(nofuse=True)
                    nc.scalar.activation(hid[:, k, :], psum[:, k, :], ACT.Gelu,
                                         bias=b1_cols[:, bass.ds(CT * q + k, 1)], scale=DOWN).then_inc(hid_done, 1)
                act.wait_ge(hid_done, CT * q + CT)
                nc.scalar.activation(hid_16[hc % 2][0], hid, ACT.Copy, scale=UP).then_inc(hid_hi, 1)

            def out_high(e):
                act.wait_ge(eo_kept, 4 * e + 4)
                if not (isinstance(e, int) and e == 0):
                    act.wait_ge(comb_mm, T * e)
                nc.scalar.activation(eo_16[0], eo, ACT.Copy).then_inc(eo_hi, 1)

            def expert(e, first=False, last=False):
                chunk_high(e, 2)
                if not first:
                    out_high(e - 1)
                hidden(e, 1, 1)
                chunk_high(e, 3)
                chunk_high(e, 4)
                hidden(e, 2, 3)
                chunk_high(e, 5)
                chunk_high(e, 6)
                hidden(e, 3, 5)
                chunk_high(e, 7)
                if not last:
                    chunk_high(e, 8)
                    hidden(e + 1, 0, -1)
                    chunk_high(e, 9)

            act.wait_ge(comb_moved, 32 * GROUPS)
            chunk_high(0, 1)
            act.wait_ge(bias_loaded, 32)
            hidden(0, 0, 0)
            expert(0, first=True)
            with act.Fori(1, E - 1) as e:
                expert(e)
            expert(E - 1, last=True)
            out_high(E - 1)

        @block.vector
        def _(dve):
            steps = [0]

            def link(ins):
                steps[0] += 1
                ins.then_inc(dve_step, 1)
                dve.wait_ge(dve_step, steps[0])

            def lo_part(pair, u):
                dve.wait_ge(split_hi, 2 * pair + u + 1)
                nc.vector.scalar_tensor_tensor(flat(wlo[:, u, :, :]), raw[:, u, :], UP, flat(whi[:, u, :, :]),
                                               ALU.mult, ALU.subtract).then_inc(split_lo, 1)

            roots = [0]

            def statistics(src, t):
                return nc.vector.bn_stats(bn6[:, t, :], src[:, t % QT, :])

            def layernorm(dst, src, b, last, done):
                link(last)
                tiles = range(QT * b, QT * (b + 1))
                cols = slice(QT * b, QT * (b + 1))
                for t in tiles:
                    last = nc.vector.bn_aggr(mean_var[:, t, :], bn6[:, t, :])
                link(last)
                nc.vector.tensor_scalar(var_eps[:, cols], mean_var[:, cols, 1], EPS, None, ALU.add).then_inc(var_ready, 1)
                roots[0] += 1
                dve.wait_ge(std_ready, roots[0])
                link(nc.vector.reciprocal(rstd[:, cols], std[:, cols]))
                for t in tiles:
                    nc.vector.tensor_scalar(dst[:, t % QT, :], src[:, t % QT, :], mean_var[:, t, 0:1], rstd[:, t:t + 1],
                                            ALU.subtract, ALU.mult).then_inc(done, 1)

            def turn_lo(first, tiles, dst, hi, scale):
                for t in tiles:
                    dve.wait_ge(turned_hi, first + t + 1)
                    nc.vector.scalar_tensor_tensor(
                        dst[:, :, t * P:(t + 1) * P],
                        psum[:, (first + t) % 4, :].rearrange("p (c n) -> p c n", c=DC), scale,
                        hi[:, :, t * P:(t + 1) * P], ALU.mult, ALU.subtract).then_inc(turned_lo, 1)

            def diagonals():
                return nc.vector.tensor_tensor(diag[:, :, :], ident.unsqueeze(1).broadcast_to([P, 4, P]),
                                               col[:, :].unsqueeze(2).broadcast_to([P, 4, P]), ALU.mult)

            def layernorm_x(b):
                dve.wait_ge(x_loaded[b], 16)
                for t in range(QT * b, QT * (b + 1)):
                    last = statistics(x_nat[b], t)
                layernorm(x_nat[b], x_nat[b], b, last, rows_ready)

            nc.vector.memset(exp_up[:, :], EXP_UP).then_inc(setup_done, 1)
            layernorm_x(0)
            lo_part(0, 0)
            turn_lo(TURN_X, range(0, QT), qT[1], qT[0], UP)
            dve.wait_ge(const_loaded, 32)
            nc.vector.tensor_copy(ident16[:, :], ident).then_inc(setup_done, 1)
            nc.vector.memset(one16[:, :], 1.0).then_inc(setup_done, 1)
            link(nc.vector.tensor_copy(lens_f[:, :], lens_i[:, :]))
            layernorm_x(1)

            for b in range(B):
                link(nc.vector.tensor_scalar(qneg[:, :], cst[:, C_QPOS:C_QPOS + NQ], lens_f[:, b:b + 1],
                                             NEG * D ** 0.5 / DOWN, ALU.is_ge, ALU.mult))
                link(nc.vector.tensor_scalar(kmask[:, :], cst[:, C_KPOS:C_KPOS + KT], lens_f[:, b:b + 1],
                                             None, ALU.is_ge))
                if b:
                    dve.wait_ge(o_moved, 16)

                def keep_scores(i, u, k):
                    tile = CT * (2 * i + u - 2 * KC * b) + k
                    dve.wait_ge(products, 4 * (2 * i + u) + k + 1)
                    nc.vector.scalar_tensor_tensor(
                        flat(S[:, bass.ds(tile, 1), :]), qneg[:, :],
                        kmask[:, bass.ds(tile, 1)], psum[:, k, :], ALU.mult, ALU.add).then_inc(scores_kept, 1)

                def keep_maximum(i, u, k):
                    tile = CT * (2 * i + u - 2 * KC * b) + k
                    dve.wait_ge(scores_kept, KT * b + tile + 1)
                    dve.wait_ge(max_kept, (KT + 1) * b + tile + 1)
                    nc.vector.tensor_tensor(run_max[:, :], run_max[:, :], flat(S[:, bass.ds(tile, 1), :]),
                                            ALU.max).then_inc(max_kept, 1)

                nc.vector.memset(run_max[:, :], -3.0e38).then_inc(max_kept, 1)
                start = b * N_CTX // 4
                with dve.Fori(start, start + KC // 2) as i:
                    for u in range(2):
                        keep_scores(i, u, 0)
                        lo_part(i + u, 1 - u)
                        for k in range(1, CT):
                            keep_scores(i, u, k)
                            keep_maximum(i, u, k - 1)
                        keep_maximum(i, u, CT - 1)
                dve.wait_ge(stat_mm, 3 * b + 1)
                link(nc.vector.tensor_reduce(col[:, :], psum[:, 0, :].rearrange("p (a n) -> p a n", a=QT),
                                             AX.X, ALU.max))
                diagonals().then_inc(stat_dve, 1)
                dve.wait_ge(stat_mm, 3 * b + 2)
                link(nc.vector.tensor_copy(bcast[:, :], psum[:, 1, :]))

                for k in range(CT):
                    nc.vector.tensor_tensor(S[:, k, :], S[:, k, :], bcast[:, :], ALU.subtract).then_inc(
                        tile_shifted if k < CT - 1 else shifted, 1)
                for k in range(CT):
                    if k < CT - 1:
                        dve.wait_ge(tile_hi, (CT - 1) * b + k + 1)
                    else:
                        dve.wait_ge(p_hi, KC * b + 1)
                    nc.vector.tensor_tensor(pp[0][1][:, k, :], S[:, k, :], pp[0][0][:, k, :],
                                            ALU.subtract).then_inc(tile_lo if k < CT - 1 else p_lo, 1)

                def shift(i, u):
                    s = S[:, bass.ds(CT * (2 * i + u - KC * (2 * b + 1)), CT), :]
                    nc.vector.tensor_tensor(s, s, bcast[:, :].unsqueeze(1).broadcast_to([P, CT, 512]),
                                            ALU.subtract).then_inc(shifted, 1)

                def p_low(i, u):
                    j = 2 * i + u - KC * (2 * b + 1)
                    dve.wait_ge(p_hi, KC * b + j + 1)
                    nc.vector.tensor_tensor(pp[u][1], S[:, bass.ds(CT * j, CT), :], pp[u][0],
                                            ALU.subtract).then_inc(p_lo, 1)

                last = (b + 1) * N_CTX // 4
                start = last - KC // 2
                shift(start, 1)
                lo_part(start, 1)
                if b == 0:
                    turn_lo(TURN_X, range(QT, T), qT[1], qT[0], UP)
                shift(start + 1, 0)
                p_low(start, 1)
                lo_part(start + 1, 0)
                with dve.Fori(start + 1, last - 1) as i:
                    shift(i, 1)
                    p_low(i, 0)
                    lo_part(i, 1)
                    shift(i + 1, 0)
                    p_low(i, 1)
                    lo_part(i + 1, 0)
                shift(last - 1, 1)
                p_low(last - 1, 0)
                lo_part(last - 1, 1)
                p_low(last - 1, 1)
                lo_part(last, 0)
                dve.wait_ge(stat_mm, 3 * b + 3)
                link(nc.vector.reciprocal(rcol[:, :], psum[:, CT - 1, 0:2 * QT].rearrange("p (a n) -> p a n", n=2)[:, :, 0]))
                for q in range(QT):
                    nc.vector.tensor_scalar(S[:, KT - QT + q, :], psum[:, 4 + q, :], rcol[:, q:q + 1], 1.0 / UP,
                                            ALU.mult, ALU.mult).then_inc(o_ready, 1)

            turn_lo(TURN_O, range(T), tT[1], tT[0], UP)
            dve.wait_ge(phase2_loaded, 16 * 4)
            nc.vector.tensor_copy(causal16[:, :], cst[:, C_CAUSAL:C_CAUSAL + P]).then_inc(setup_done, 1)
            link(nc.vector.tensor_tensor(resid, resid, qneg[:, :].unsqueeze(1).broadcast_to([P, T, 512]), ALU.add))
            lo_part(N_WQ // 2, N_WQ % 2)

            def keep_projection(n, dst, done):
                for b in range(B):
                    for t in range(QT * b, QT * (b + 1)):
                        dve.wait_ge(products, products_after(n - 1) + t + 1)
                        nc.vector.scalar_tensor_tensor(resid[:, t, :], psum[:, 4 + t % 4, :], DOWN, resid[:, t, :],
                                                       ALU.mult, ALU.add).then_inc(proj_kept, 1)
                        dve.wait_ge(proj_kept, (T if n == N_WP else 0) + t + 1)
                        last = statistics(resid[:, QT * b:QT * (b + 1), :], t)
                    layernorm(*(rows[:, QT * b:QT * (b + 1), :] for rows in (dst, resid)), b, last, done)

            keep_projection(N_WO, nat, rows_ready)
            turn_lo(TURN_HN, range(0, QT), tT[1], tT[0], UP)

            def qkv_low(w, t, dst, hi):
                dve.wait_ge(qkv_hi, T * w + t + 1)
                src = psum[:, 4 + t % 4, :]
                if len(dst.shape) == 3:
                    src = src.rearrange("p (h d) -> p h d", h=H)
                nc.vector.scalar_tensor_tensor(dst, src, 1.0 / UP, hi, ALU.mult, ALU.subtract).then_inc(qkv_lo, 1)

            for w, n in enumerate((N_WQ, N_WK)):
                for t in range(T):
                    b, f = divmod(t, DC)
                    if n == N_WQ and t == QT:
                        turn_lo(TURN_HN, range(QT, T), tT[1], tT[0], UP)
                    qkv_low(w, t, *(qk[w][i][:, f, b * NQ:(b + 1) * NQ] for i in (1, 0)))
                    if t == 0:
                        lo_part((n + 1) // 2, (n + 1) % 2)
            for t in range(T):
                b, k = divmod(t, QT)
                qkv_low(2, t, *(v_nat[i][:, b * H:(b + 1) * H, k, :] for i in (1, 0)))
                if t == 0:
                    lo_part(N_WP // 2, N_WP % 2)

            def head_maxima(g, u):
                for n, (bank, tiles) in enumerate(SCORE_BANKS):
                    dve.wait_ge(head_scores, 3 * g + n + 1)
                    for q, at in tiles:
                        c = SCORE_COL[q]
                        last = nc.vector.tensor_reduce(head_max[:, u, c:c + 1], psum[:, bank, at:at + (q + 1) * P],
                                                       AX.X, ALU.max)
                    last.then_inc(head_reduced, 1)
                    dve.wait_ge(head_reduced, 3 * g + n + 1)
                    c0 = SCORE_COL[tiles[0][0]]
                    cols = slice(c0, c0 + len(tiles))
                    nc.vector.tensor_scalar(head_bias[:, u, cols], head_max[:, u, cols], -DOWN / HD ** 0.5, EXP_UP,
                                            ALU.mult, ALU.add).then_inc(head_maxed, 1)

            def head_decay(g, u):
                dve.wait_ge(head_turned, g + 1)
                if not (isinstance(g, int) and g < 2):
                    dve.wait_ge(head_lo, g - 1)
                for bank, tiles in TURN_BANKS:
                    for k, at in tiles:
                        width = (QT - k) * P
                        last = nc.vector.tensor_tensor(prob_t[u][:, BLOCK_AT[k]:BLOCK_AT[k] + width],
                                                       psum[:, bank, at:at + width], decay[:, 0:width], ALU.mult)
                last.then_inc(head_decayed, 1)

            def head_reciprocal(g, u):
                if not isinstance(g, int) or g >= 2:
                    dve.wait_ge(head_kept, g - 1)
                nc.vector.reciprocal(head_rec[:, u, :], head_sum[:, u, :]).then_inc(head_rec_ready, 1)

            def head_keep(g, u):
                dve.wait_ge(head_rec_ready, g + 1)
                dve.wait_ge(head_y, g + 1)
                nc.vector.scalar_tensor_tensor(
                    y_nat[:, :, bass.ds(g, 1), :].rearrange("p q a d -> p (q a) d"),
                    psum[:, 6 + u, 0:QT * HD].rearrange("p (q d) -> p q d", q=QT), 1.0 / UP,
                    head_rec[:, u, :].unsqueeze(2).broadcast_to([P, QT, HD]), ALU.mult, ALU.mult).then_inc(head_kept, 1)

            head_maxima(0, 0)
            for g in range(4):
                head_maxima(g + 1, 1 - g % 2)
                head_decay(g, g % 2)
                if g >= 2:
                    head_keep(g - 2, g % 2)
                head_reciprocal(g, g % 2)
            with dve.Fori(2, NH // 2 - 1) as i:
                for u in range(2):
                    head_maxima(2 * i + u + 1, 1 - u)
                    head_decay(2 * i + u, u)
                    head_keep(2 * i + u - 2, u)
                    head_reciprocal(2 * i + u, u)
            head_maxima(NH - 1, 1)
            for g in range(NH - 2, NH):
                head_decay(g, g % 2)
                head_keep(g - 2, g % 2)
                head_reciprocal(g, g % 2)
            head_keep(NH - 2, 0)
            head_keep(NH - 1, 1)

            turn_lo(TURN_Y, range(T), tT[1], tT[0], UP)
            lo_part(N_EXP // 2, N_EXP % 2)
            keep_projection(N_WP, nat, z_ready)

            def rms_rows(first, n, buf, weight):
                roots[0] += 1
                dve.wait_ge(std_ready, roots[0])
                cols = slice(first, first + n)
                link(nc.vector.tensor_scalar(sq_root[:, cols], sq_root[:, cols], 1e-12, None, ALU.max))
                link(nc.vector.reciprocal(sq_rec[:, cols], sq_root[:, cols]))
                link(nc.vector.tensor_scalar(sq_rec[:, cols], sq_rec[:, cols], D ** 0.5, None, ALU.mult))
                for t in range(n):
                    nc.vector.scalar_tensor_tensor(buf[:, t, :], buf[:, t, :], sq_rec[:, first + t:first + t + 1],
                                                   weight, ALU.mult, ALU.mult).then_inc(rows_ready, 1)

            rms_rows(0, T, nat, run_max[:, :])
            dve.wait_ge(slot_gamma_loaded, 16)
            rms_rows(T, M // P, se_nat, run_sum[:, :])
            for t in range(T):
                dve.wait_ge(xn_hi, t + 1)
                nc.vector.scalar_tensor_tensor(xn_nat[1][:, t, :], nat[:, t, :], UP, xn_nat[0][:, t, :],
                                               ALU.mult, ALU.subtract).then_inc(xn_lo, 1)
            turn_lo(TURN_XN, range(T), tT[1], tT[0], UP)
            turn_lo(TURN_SN, range(M // P), snT[1], snT[0], UP)

            def disp_low(g):
                dve.wait_ge(disp_hi, g + 1)
                nc.vector.tensor_tensor(disp_16[g % 2][1], disp, disp_16[g % 2][0], ALU.subtract).then_inc(disp_lo, 1)

            def disp_maxima(g):
                mc = g % MC
                nc.vector.tensor_reduce(bcast[:, :], L[:, :, mc * 512:(mc + 1) * 512].rearrange("p q n -> p n q"),
                                        AX.X, ALU.max).then_inc(cmax_ready, 1)
                dve.wait_ge(max_mm, 2 * g + 1)
                link(nc.vector.tensor_reduce(col[:, :], psum[:, 4, :].rearrange("p (a n) -> p a n", a=4),
                                             AX.X, ALU.max))
                diagonals().then_inc(max_diag, 1)

            def row_maxima(g):
                b, mc = divmod(g, MC)
                dve.wait_ge(logit_kept, QT * (g + 1))
                link(nc.vector.tensor_reduce(row_part[:, mc, :], L[:, :, mc * 512:(mc + 1) * 512], AX.X, ALU.max))
                if mc == MC - 1:
                    link(nc.vector.tensor_reduce(row_max[:, :], row_part[:, :, :].rearrange("p m q -> p q m"),
                                                 AX.X, ALU.max))
                    nc.vector.tensor_scalar(row_bias[:, b, :], row_max[:, :], -1.0, EXP_UP, ALU.mult,
                                            ALU.add).then_inc(row_biased, 1)

            def disp_subtract(g):
                mc = g % MC
                if g:
                    dve.wait_ge(disp_lo, g)
                dve.wait_ge(max_mm, 2 * g + 2)
                nc.vector.tensor_tensor(disp, L[:, :, mc * 512:(mc + 1) * 512],
                                        psum[:, 5, :].unsqueeze(1).broadcast_to([P, QT, 512]),
                                        ALU.subtract).then_inc(disp_shift, 1)

            def disp_sums(g):
                dve.wait_ge(sum_mm, 2 * g + 1)
                link(nc.vector.reciprocal(col[:, :], psum[:, 4, 0:8].rearrange("p (a n) -> p a n", n=2)[:, :, 0]))
                diagonals().then_inc(sum_diag, 1)
                dve.wait_ge(sum_mm, 2 * g + 2)
                link(nc.vector.tensor_copy(qneg[:, :], psum[:, 5, :]))
                if g:
                    dve.wait_ge(slot_lo, g)

            def keep_slots(g, c):
                dve.wait_ge(slot_mm, 4 * g + c + 1)
                nc.vector.tensor_tensor(slots[:, c, :], psum[:, 6 + c % 2, :], qneg[:, :],
                                        ALU.mult).then_inc(slot_kept, 1)

            def combine_low(g):
                for m in range(4):
                    dve.wait_ge(comb_hi, 4 * g + m + 1)
                    nc.vector.tensor_tensor(comb_16[1][:, m, :], psum[:, 2 + m % 2, :], comb_16[0][:, m, :],
                                            ALU.subtract).then_inc(comb_lo, 1)

            for g in range(-1, GROUPS):
                if g + 1 < GROUPS:
                    dve.wait_ge(logit_kept, QT * (g + 2))
                    disp_maxima(g + 1)
                    if (g + 1) % MC < MC - 1:
                        row_maxima(g + 1)
                    disp_subtract(g + 1)
                if g < 0:
                    disp_low(g + 1)
                    continue
                disp_sums(g)
                keep_slots(g, 0)
                keep_slots(g, 1)
                for c in COMBINED[g][:1]:
                    combine_low(c)
                keep_slots(g, 2)
                if g + 1 < GROUPS:
                    disp_low(g + 1)
                keep_slots(g, 3)
                if (g + 2) % MC == MC - 1:
                    row_maxima(g + 2)
                for c in COMBINED[g][1:]:
                    combine_low(c)
            dve.wait_ge(comb_exp, GROUPS)
            link(nc.vector.tensor_reduce(row_rec[:, :], row_sum[:, :, :, :].rearrange("p b q m -> p (b q) m"),
                                         AX.X, ALU.add))
            link(nc.vector.reciprocal(row_rec[:, :], row_rec[:, :]))
            link(nc.vector.tensor_scalar(row_rec[:, :], row_rec[:, :], 1.0 / UP, None, ALU.mult))

            def chunk_low(e, s):
                n = N_EXP + s
                dve.wait_ge(split_hi, 8 * e + n + 1)
                nc.vector.scalar_tensor_tensor(flat(wlo[:, n % 2, :, :]), raw[:, n % 2, :], UP,
                                               flat(whi[:, n % 2, :, :]), ALU.mult, ALU.subtract).then_inc(split_lo, 1)

            def hidden_low(e, hc):
                dve.wait_ge(hid_hi, HC * e + hc + 1)
                nc.vector.scalar_tensor_tensor(hid_16[hc % 2][1], hid, UP, hid_16[hc % 2][0],
                                               ALU.mult, ALU.subtract).then_inc(hid_lo, 1)

            def keep_out(e):
                for r in range(4):
                    dve.wait_ge(products, products_after(N_EXP - 1) + 4 * (8 * e + (8 if not isinstance(e, int) or e < E - 1 else 7) + 1))
                    nc.vector.scalar_tensor_tensor(eo[:, r, :], psum[:, 4 + r, :], 1.0 / UP,
                                                   flat(b2_rows[:, bass.ds(e, 1), :]), ALU.mult, ALU.add).then_inc(eo_kept, 1)

            def out_low(e):
                dve.wait_ge(eo_hi, e + 1)
                nc.vector.tensor_tensor(eo_16[1], eo, eo_16[0], ALU.subtract).then_inc(eo_lo, 1)

            def keep_combined(e):
                for t in range(T):
                    dve.wait_ge(comb_mm, T * e + t + 1)
                    nc.vector.scalar_tensor_tensor(resid[:, t, :], psum[:, t % 4, :], row_rec[:, t:t + 1],
                                                   resid[:, t, :], ALU.mult, ALU.add).then_inc(comb_kept, 1)

            def expert(e, first=False, last=False):
                if not first:
                    keep_out(e - 1)
                chunk_low(e, 2)
                if not first:
                    out_low(e - 1)
                hidden_low(e, 1)
                chunk_low(e, 3)
                if not first:
                    keep_combined(e - 1)
                chunk_low(e, 4)
                hidden_low(e, 2)
                chunk_low(e, 5)
                chunk_low(e, 6)
                hidden_low(e, 3)
                chunk_low(e, 7)
                if not last:
                    chunk_low(e, 8)
                    hidden_low(e + 1, 0)
                    chunk_low(e, 9)

            chunk_low(0, 1)
            hidden_low(0, 0)
            dve.wait_ge(bias_loaded, 32)
            link(nc.vector.tensor_scalar(b2_rows, b2_rows, UP, None, ALU.mult))
            expert(0, first=True)
            with dve.Fori(1, E - 1) as e:
                expert(e)
            expert(E - 1, last=True)
            keep_out(E - 1)
            out_low(E - 1)
            keep_combined(E - 1)

        @block.tensor
        def _(pe):
            def product(out_, lhs, rhs, start, stop):
                nc.tensor.matmul(out_, lhs[0], rhs[0], start=start, stop=False)
                nc.tensor.matmul(out_, lhs[0], rhs[1], start=False, stop=False)
                return nc.tensor.matmul(out_, lhs[1], rhs[0], start=False, stop=stop)

            def turn(first, tiles, src):
                for t in tiles:
                    src_ready(first, t)
                    if first + t >= 4:
                        pe.wait_ge(turned_lo, first + t - 3)
                    for c in range(DC):
                        last = nc.tensor.transpose(psum[:, (first + t) % 4, c * P:(c + 1) * P], src(t, c), ident)
                    last.then_inc(turned, 1)

            def src_ready(first, t):
                rows = {TURN_X: ROWS_X, TURN_HN: ROWS_HN, TURN_XN: ROWS_XN, TURN_SN: ROWS_SN}
                if first in rows:
                    pe.wait_ge(rows_ready, rows[first] + t + 1)

            def rows_of(buf):
                return lambda t, c: buf[:, t, c * P:(c + 1) * P]

            w = [[x_[:, u, :, :] for x_ in (whi, wlo)] for u in range(2)]

            pe.wait_ge(const_loaded, 32)
            turn(TURN_X, range(0, QT), rows_of(x_nat[0]))
            pe.wait_ge(turned_lo, QT)

            for b in range(B):
                def scores(i, u):
                    j = 2 * i + u - 2 * KC * b
                    pe.wait_ge(split_lo, 2 * i + u + 1)
                    for k in range(CT):
                        if not (isinstance(j, int) and j == 0):
                            pe.wait_ge(scores_kept, KT * b + CT * (j - 1) + k + 1)
                        elif b and k == CT - 1:
                            pe.wait_ge(o_ready, QT * b)
                        for c in range(DC):
                            last = product(psum[:, k, :], [x_[:, c, k * P:(k + 1) * P] for x_ in w[u]],
                                           [x_[:, c, b * NQ:(b + 1) * NQ] for x_ in qT], c == 0, c == DC - 1)
                        last.then_inc(products, 1)

                start = b * N_CTX // 4
                scores(start, 0)
                scores(start, 1)
                with pe.Fori(start + 1, start + KC // 2) as i:
                    scores(i, 0)
                    scores(i, 1)

                pe.wait_ge(max_kept, (KT + 1) * (b + 1))
                for q in range(QT):
                    last = nc.tensor.transpose(psum[:, 0, q * P:(q + 1) * P], run_max[:, q * P:(q + 1) * P], ident)
                last.then_inc(stat_mm, 1)
                pe.wait_ge(stat_dve, b + 1)
                nc.tensor.matmul(psum[:, 1, :], ones, diag[:, :, :].rearrange("p a n -> p (a n)"),
                                 start=True, stop=True).then_inc(stat_mm, 1)
                if b == 0:
                    pe.wait_ge(tile_shifted, 1)
                    turn(TURN_X, range(QT, T), lambda t, c: x_nat[1][:, t - QT, c * P:(c + 1) * P])

                def values(i, u, last=False):
                    j = 2 * i + u - KC * (2 * b + 1)
                    pe.wait_ge(split_lo, 2 * i + u + 1)
                    pe.wait_ge(p_lo, KC * b + j + 1)
                    for q in range(QT):
                        for k in range(CT):
                            done = product(psum[:, 4 + q, :], [x_[:, k, q * P:(q + 1) * P] for x_ in pp[u]],
                                           [x_[:, k, :] for x_ in w[u]], False, last and k == CT - 1)
                        done.then_inc(products, 1)

                def first_values(i):
                    pe.wait_ge(split_lo, 2 * i + 1)
                    for k in range(CT):
                        if k < CT - 1:
                            pe.wait_ge(tile_lo, (CT - 1) * b + k + 1)
                        else:
                            pe.wait_ge(p_lo, KC * b + 1)
                        for q in range(QT):
                            done = product(psum[:, 4 + q, :], [x_[:, k, q * P:(q + 1) * P] for x_ in pp[0]],
                                           [x_[:, k, :] for x_ in w[0]], k == 0, False)
                        done.then_inc(products, 1)

                if b:
                    pe.wait_ge(o_ready, QT * b)
                last_pair = (b + 1) * N_CTX // 4 - 1
                start = last_pair + 1 - KC // 2
                first_values(start)
                values(start, 1)
                with pe.Fori(start + 1, last_pair) as i:
                    values(i, 0)
                    values(i, 1)
                values(last_pair, 0)
                values(last_pair, 1, last=True)
                pe.wait_ge(sum_kept, (KT + 1) * (b + 1))
                for q in range(QT):
                    done = nc.tensor.matmul(psum[:, CT - 1, 2 * q:2 * q + 2], run_sum[:, q * P:(q + 1) * P], ones[:, 0:2],
                                            start=True, stop=True)
                done.then_inc(stat_mm, 1)

            def project(n, first):
                pe.wait_ge(split_lo, n + 1)
                for t in range(T):
                    pe.wait_ge(turned_lo, first + t + 1)
                    if t >= 4:
                        pe.wait_ge(proj_kept, (T if n == N_WP else 0) + t - 3)
                    for c in range(DC):
                        last = product(psum[:, 4 + t % 4, :], [x_[:, c, t * P:(t + 1) * P] for x_ in tT],
                                       [x_[:, c, :] for x_ in w[n % 2]], c == 0, c == DC - 1)
                    last.then_inc(products, 1)

            pe.wait_ge(o_loaded, 16)
            turn(TURN_O, range(0, CT - 1), rows_of(o_nat))
            pe.wait_ge(o_ready, T)
            turn(TURN_O, range(CT - 1, T), rows_of(o_nat))
            project(N_WO, TURN_O)
            turn(TURN_HN, range(0, QT), rows_of(nat))

            pe.wait_ge(turned_lo, TURN_HN + QT)
            pe.wait_ge(proj_kept, T)
            for k, n in enumerate((N_WQ, N_WK, N_WV)):
                pe.wait_ge(split_lo, n + 1)
                for t in range(T):
                    if T * k + t >= 4:
                        pe.wait_ge(qkv_lo, T * k + t - 3)
                    b, f = divmod(t, DC)
                    if n == N_WQ and t == QT:
                        turn(TURN_HN, range(QT, T), rows_of(nat))
                        pe.wait_ge(turned_lo, TURN_HN + T)
                    for c in range(DC):
                        if n == N_WV:
                            lhs = [x_[:, c, t * P:(t + 1) * P] for x_ in tT]
                            rhs = [x_[:, c, :] for x_ in w[n % 2]]
                        else:
                            lhs = [x_[:, c, f * P:(f + 1) * P] for x_ in w[n % 2]]
                            rhs = [x_[:, c, b * NQ:(b + 1) * NQ] for x_ in tT]
                        last = product(psum[:, 4 + t % 4, :], lhs, rhs, c == 0, c == DC - 1)
                    last.then_inc(products, 1)

            q_heads, k_heads = (s_.rearrange("p b h n -> p (b h n)") for s_ in (q_stack, k_stack))

            def score_head(g, u):
                for n, (bank, tiles) in enumerate(SCORE_BANKS):
                    if not (isinstance(g, int) and g == 0):
                        pe.wait_ge(head_exp, 3 * (g - 1) + n + 1)
                    for q, at in tiles:
                        width = (q + 1) * P
                        nc.tensor.matmul(psum[:, bank, at:at + width], q_heads[:, bass.ds(NQ * g + q * P, P)],
                                         k_heads[:, bass.ds(NQ * g, width)], start=True, stop=False)
                        last = nc.tensor.matmul(psum[:, bank, at + q * P:at + width], ident16[:, :], causal16[:, :],
                                                start=False, stop=True)
                    last.then_inc(head_scores, 1)

            def turn_head(g, u):
                pe.wait_ge(head_exp, 3 * g + 3)
                if not (isinstance(g, int) and g == 0):
                    pe.wait_ge(head_decayed, g)
                for bank, tiles in TURN_BANKS:
                    for k, at in tiles:
                        for q in range(k, QT):
                            a_ = at + (q - k) * P
                            src = PROB_AT[q] + k * P
                            last = nc.tensor.transpose(psum[:, bank, a_:a_ + P], prob[u][:, src:src + P], ident)
                last.then_inc(head_turned, 1)

            v_heads = [v_.rearrange("p g k d -> p (g k d)") for v_ in v_nat]

            def head_out(g, u):
                pe.wait_ge(head_lo, g + 1)
                if not (isinstance(g, int) and g < 2):
                    pe.wait_ge(head_kept, g - 1)
                for q in range(QT):
                    for k in range(q + 1):
                        at = BLOCK_AT[k] + (q - k) * P
                        last = product(psum[:, 6 + u, q * HD:(q + 1) * HD],
                                       [x_[:, at:at + P] for x_ in prob_16[u]],
                                       [x_[:, bass.ds(QT * HD * g + k * HD, HD)] for x_ in v_heads], k == 0, k == q)
                last.then_inc(head_y, 1)

            pe.wait_ge(q_stacked, STACKED)
            pe.wait_ge(k_stacked, STACKED)
            pe.wait_ge(qkv_lo, 3 * T)
            pe.wait_ge(setup_done, 4)
            score_head(0, 0)
            for g in range(4):
                score_head(g + 1, 1 - g % 2)
                turn_head(g, g % 2)
                if g >= 2:
                    head_out(g - 2, g % 2)
            with pe.Fori(2, NH // 2 - 1) as i:
                for u in range(2):
                    score_head(2 * i + u + 1, 1 - u)
                    turn_head(2 * i + u, u)
                    head_out(2 * i + u - 2, u)
            score_head(NH - 1, 1)
            for g in range(NH - 2, NH):
                turn_head(g, g % 2)
                head_out(g - 2, g % 2)
            head_out(NH - 2, 0)
            head_out(NH - 1, 1)

            pe.wait_ge(head_kept, NH)
            turn(TURN_Y, range(T), lambda t, c: y_nat[:, t % QT, H * (t // QT) + 4 * c:H * (t // QT) + 4 * c + 4, :].rearrange(
                "p h d -> p (h d)"))
            project(N_WP, TURN_Y)
            turn(TURN_XN, range(T), rows_of(nat))
            turn(TURN_SN, range(M // P), rows_of(se_nat))

            def turn_maxima(g):
                pe.wait_ge(cmax_ready, g + 1)
                for m in range(4):
                    last = nc.tensor.transpose(psum[:, 4, m * P:(m + 1) * P], bcast[:, m * P:(m + 1) * P], ident)
                last.then_inc(max_mm, 1)

            def spread_maxima(g):
                pe.wait_ge(max_diag, g + 1)
                nc.tensor.matmul(psum[:, 5, :], ones, diag[:, :, :].rearrange("p a n -> p (a n)"),
                                 start=True, stop=True).then_inc(max_mm, 1)

            def logits(g, rows):
                b, mc = divmod(g, MC)
                for q in rows:
                    if QT * g + q >= 2:
                        pe.wait_ge(logit_kept, QT * g + q - 1)
                    for c in range(DC):
                        at = (QT * b + q) * P
                        last = product(psum[:, q % 2, :], [x_[:, c, at:at + P] for x_ in tT],
                                       [x_[:, c, mc * 512:(mc + 1) * 512] for x_ in snT], c == 0, c == DC - 1)
                    last.then_inc(logit_mm, 1)

            def dispatch_sums(g):
                pe.wait_ge(disp_lo, g + 1)
                for m in range(4):
                    for q in range(QT):
                        for part in range(2):
                            last = nc.tensor.matmul(psum[:, 4, 2 * m:2 * m + 2],
                                                    disp_16[g % 2][part][:, q, m * P:(m + 1) * P], one16[:, :],
                                                    start=q + part == 0, stop=q + part == QT)
                last.then_inc(sum_mm, 1)

            def spread_sums(g):
                pe.wait_ge(sum_diag, g + 1)
                if g + 1 < GROUPS:
                    pe.wait_ge(disp_shift, g + 2)
                nc.tensor.matmul(psum[:, 5, :], ones, diag[:, :, :].rearrange("p a n -> p (a n)"),
                                 start=True, stop=True).then_inc(sum_mm, 1)

            def slot_products(g, c):
                b = g // MC
                if 4 * g + c >= 2:
                    pe.wait_ge(slot_kept, 4 * g + c - 1)
                for q in range(QT):
                    last = product(psum[:, 6 + c % 2, :], [x_[:, QT * b + q, c * P:(c + 1) * P] for x_ in xn_nat],
                                   [x_[:, q, :] for x_ in disp_16[g % 2]], q == 0, q == QT - 1)
                last.then_inc(slot_mm, 1)

            def turn_combine(g):
                pe.wait_ge(comb_exp, g + 1)
                for m in range(4):
                    if 4 * g + m >= 2:
                        pe.wait_ge(comb_lo, 4 * g + m - 1)
                    for q in range(QT):
                        last = nc.tensor.transpose(psum[:, 2 + m % 2, q * P:(q + 1) * P],
                                                   comb[:, q, m * P:(m + 1) * P], ident)
                    last.then_inc(comb_turned, 1)

            pe.wait_ge(turned_lo, TURN_SN + M // P)
            pe.wait_ge(proj_kept, 2 * T)
            pe.wait_ge(xn_lo, T)
            for g in range(-2, GROUPS):
                if g + 2 < GROUPS:
                    logits(g + 2, range(0, 2))
                if 0 <= g + 1 < GROUPS:
                    turn_maxima(g + 1)
                if g + 2 < GROUPS:
                    logits(g + 2, range(2, QT))
                if 0 <= g + 1 < GROUPS:
                    spread_maxima(g + 1)
                if g < 0:
                    continue
                dispatch_sums(g)
                slot_products(g, 0)
                spread_sums(g)
                slot_products(g, 1)
                for c in COMBINED[g][:1]:
                    turn_combine(c)
                slot_products(g, 2)
                slot_products(g, 3)
                for c in COMBINED[g][1:]:
                    turn_combine(c)

            def first_products(e, hc, s, u):
                q = HC * e + hc
                n = N_EXP + s
                pe.wait_ge(split_lo, 8 * e + n + 1)
                for k in range(CT):
                    if not (isinstance(q, int) and q == 0):
                        pe.wait_ge(hid_done, CT * (q - 1) + k + 1)
                    for c in range(DC):
                        last = product(psum[:, k, :], [x_[:, c, k * P:(k + 1) * P] for x_ in w[n % 2]],
                                       [e_slots[u][:, i, c, :] for i in range(2)], c == 0, c == DC - 1)
                    last.then_inc(products, 1)

            def second_products(e, hc, s):
                q = HC * e + hc
                n = N_EXP + s
                pe.wait_ge(split_lo, 8 * e + n + 1)
                pe.wait_ge(hid_lo, q + 1)
                for k in range(CT):
                    for r in range(4):
                        last = product(psum[:, 4 + r, :], [x_[:, k, r * P:(r + 1) * P] for x_ in hid_16[hc % 2]],
                                       [x_[:, k, :] for x_ in w[n % 2]],
                                       hc == 0 and k == 0, hc == HC - 1 and k == CT - 1)
                    last.then_inc(products, 1)

            def combine(e, u, nth):
                pe.wait_ge(e_comb_in[u], 16 * nth)
                pe.wait_ge(eo_lo, e + 1)
                for t in range(T):
                    b, q = divmod(t, QT)
                    if t >= 4:
                        pe.wait_ge(comb_kept, T * e + t - 3)
                    for m in range(2):
                        last = product(psum[:, t % 4, :],
                                       [e_comb[u][:, i, 2 * b + m, q * P:(q + 1) * P] for i in range(2)],
                                       [x_[:, 2 * b + m, :] for x_ in eo_16], m == 0, m == 1)
                    last.then_inc(comb_mm, 1)

            def expert(e, u, nth, first=False, last=False):
                first_products(e, 1, 1, u)
                if not first:
                    pe.wait_ge(eo_kept, 4 * e)
                second_products(e, 0, 2)
                if not first:
                    pe.wait_ge(hid_done, CT * (HC * e + 1) + CT)
                    combine(e - 1, 1 - u, nth - (1 if u == 0 else 0))
                    pe.wait_ge(comb_kept, T * e)
                first_products(e, 2, 3, u)
                second_products(e, 1, 4)
                first_products(e, 3, 5, u)
                second_products(e, 2, 6)
                if not last:
                    pe.wait_ge(e_slots_in[1 - u], 16 * (nth + (1 if u == 1 else 0)))
                    first_products(e + 1, 0, -1 , 1 - u)
                    second_products(e, 3, 8)
                else:
                    second_products(e, 3, 7)

            pe.wait_ge(e_slots_in[0], 16)
            pe.wait_ge(comb_lo, 4 * GROUPS)
            first_products(0, 0, 0, 0)
            pe.wait_ge(slot_kept, 4 * GROUPS)
            expert(0, 0, 1, first=True)
            with pe.Fori(0, E // 2 - 1) as i:
                expert(2 * i + 1, 1, i + 1)
                expert(2 * i + 2, 0, i + 2)
            expert(E - 1, 1, E // 2, last=True)
            pe.wait_ge(hid_done, CT * HC * E)
            combine(E - 1, 1, E // 2)


def kernel(**inputs):
    import numpy as np
    import concourse.bacc as bacc
    from concourse.bass_utils import run_bass_kernel_spmd

    a = {k: np.asarray(v) for k, v in inputs.items()}

    def cut(m, inner):
        return m.reshape(-1, P, inner).transpose(1, 0, 2).reshape(P, -1)

    ctx = a["ctx_1024"]
    ctx_stream = np.empty((N_CTX, P, CT * 512), ctx.dtype)
    for b in range(B):
        turned = ctx[b].T
        for j in range(KC):
            part = slice(512 * j, 512 * (j + 1))
            ctx_stream[2 * KC * b + j] = cut(turned[:, part], 512)
            ctx_stream[2 * KC * b + KC + j] = cut(ctx[b, part, :], 512)
    w_attn = a["L0_attn_W_attn"]
    square_stream = np.stack([cut(a["L0_xattn_W"].T, 512)]
                             + [cut(w_attn[:, D * i:D * (i + 1)], 512) for i in range(3)]
                             + [cut(a["L0_attn_W_proj"], 512)])
    w1, w2 = a["L0_ffn_w1"], a["L0_ffn_w2"]

    def first(e, hc):
        return cut(w1[e][:, 512 * hc:512 * (hc + 1)], 512)

    def second(e, hc):
        return cut(w2[e][512 * hc:512 * (hc + 1), :], 512)

    order = [first(0, 0)]
    for e in range(E):
        for hc in range(1, HC):
            order += [first(e, hc), second(e, hc - 1)]
        if e + 1 < E:
            order.append(first(e + 1, 0))
        order.append(second(e, HC - 1))
    expert_stream = np.stack(order)

    consts = np.zeros((2, P, C_END), np.float32)
    rows = np.arange(P)
    consts[:, rows, C_ID + rows] = 1.0
    consts[:, :, C_ONE:C_ONE + P] = 1.0
    consts[0, :, C_QPOS:C_QPOS + NQ] = np.arange(NQ)
    consts[0, :, C_KPOS:C_KPOS + KT] = rows[:, None] + P * np.arange(KT)
    length, echoic = 1024, 16
    fall = 1.0 - np.linspace(0.0, 1.0, length - echoic + 1) ** (1.0 / np.e)
    values = np.concatenate([np.ones(echoic - 1), fall])
    back = np.arange(QT * P)[None, :] - rows[:, None]
    consts[1, :, C_DECAY:C_DECAY + QT * P] = np.where(back >= 0, values[np.maximum(back, 0)], 0.0)
    consts[1, :, C_CAUSAL:C_CAUSAL + P] = np.where(rows[None, :P] <= rows[:, None], 0.0, MASKED)

    arrays = {
        "x": a["x"], "ctx_stream": ctx_stream, "square_stream": square_stream, "expert_stream": expert_stream,
        "lens": a["_lenS2"], "xattn_b": a["L0_xattn_b"], "gamma": a["L0_ffn_norm_gamma"],
        "slot_gamma": a["L0_ffn_slot_norm_gamma"], "slot_embeds": a["L0_ffn_slot_embeds"].reshape(M, D),
        "b1": np.ascontiguousarray(a["L0_ffn_b1"].reshape(E * HID // P, P).T), "b2": a["L0_ffn_b2"],
        "consts": consts,
    }
    arrays = {k: np.ascontiguousarray(v) for k, v in arrays.items()}
    nc = bacc.Bacc("TRN2", target_bir_lowering=False, num_devices=1)
    handles = {k: nc.dram_tensor(f"in_{k}", v.shape, mybir.dt.from_np(v.dtype), kind="ExternalInput").ap()
               for k, v in arrays.items()}
    out = nc.dram_tensor("out", a["x"].shape, F32, kind="ExternalOutput").ap()
    program(nc, **handles, out=out)
    result = run_bass_kernel_spmd(nc, [{f"in_{k}": v for k, v in arrays.items()}], core_ids=[0])
    return result.results[0]["out"]
```

```python
from contextlib import ExitStack

import concourse.bass as bass
from concourse import mybir

ALU = mybir.AluOpType
ACT = mybir.ActivationFunctionType
AX = mybir.AxisListType
F32 = mybir.dt.float32
F16 = mybir.dt.float16
BF16 = mybir.dt.bfloat16
I32 = mybir.dt.int32

P = 128
D = 512
DC = D // P
B = 2
NQ = 512
QT = NQ // P
T = B * QT
NK = 8192
KT = NK // P
CT = 4
KC = KT // CT
H = 16
HD = D // H
E = 8
ES = 256
M = E * ES
HID = 2048
HC = HID // 512
MC = M // 512

UP = 32.0
DOWN = 1.0 / (UP * UP)
EXP_UP = 7.0
NEG = -1e13
EPS = 1e-5
MASKED = -1e30

C_ID = 0
C_ONE = C_ID + P
C_SET = C_ONE + P
C_QPOS = C_SET
C_KPOS = C_QPOS + NQ
C_DECAY = C_SET
C_CAUSAL = C_DECAY + QT * P
C_END = C_CAUSAL + P
C_BLOCKS = C_END
C_ALL = C_BLOCKS + 6 * P


BLOCK_AT = {0: 0, 1: 4 * P, 3: 7 * P, 2: 8 * P}

N_CTX = B * 2 * KC
N_WO, N_WQ, N_WK, N_WV, N_WP = range(N_CTX, N_CTX + 5)
N_EXP = N_CTX + 5
GROUPS = B * MC
COMBINED = [[], []] + [[c] for c in range(MC)] + [[c, c + 1] for c in range(MC, GROUPS, 2)]
SMALL = 8


def products_after(n):
    if isinstance(n, int) and n >= N_CTX:
        if n < N_EXP:
            return 4 * N_CTX + SMALL * (n + 1 - N_CTX)
        return 4 * N_CTX + SMALL * 5 + 4 * (n + 1 - N_EXP)
    return 4 * n + 4


def program(nc, x, ctx_stream, square_stream, expert_stream, lens, xattn_b, gamma, slot_gamma,
            slot_embeds, b1, b2, consts, out):
    with ExitStack() as ctx:
        def sb(name, shape, dt):
            return ctx.enter_context(nc.sbuf_tensor(name, shape, dt))

        def sem(name):
            return ctx.enter_context(nc.semaphore(name))

        def dram(name, shape, dt):
            return nc.dram_tensor(name, shape, dt, kind="Internal").ap()

        psum = ctx.enter_context(nc.psum_tensor("psum", [P, 8, 512], F32))
        S = sb("S", [P, KT, 512], F32)
        A = sb("A", [P, 16, 512], F32)
        raw = sb("raw", [P, 2, CT * 512], F32)
        whi = sb("whi", [P, 2, CT, 512], F16)
        wlo = sb("wlo", [P, 2, CT, 512], F16)
        cst = sb("cst", [P, C_END], F32)
        run_max = sb("run_max", [P, 512], F32)
        run_sum = sb("run_sum", [P, 512], F32)
        rows_2 = sb("rows_2", [P, 2, 512], F32)
        bcast = rows_2[:, 0, :]
        diag = rows_2[:, 1, :].rearrange("p (a n) -> p a n", a=4)
        decay_blocks = rows_2[:, :, :].rearrange("p a n -> p (a n)")[:, 0:6 * P]
        qneg = sb("qneg", [P, 512], F32)
        lens_i = sb("lens_i", [P, B], I32)
        lens_f = sb("lens_f", [P, B], F32)
        kmask = sb("kmask", [P, KT], F32)
        col = sb("col", [P, 4], F32)
        rcol = sb("rcol", [P, 4], F32)
        ident16 = sb("ident16", [P, P], BF16)
        causal16 = sb("causal16", [P, P], BF16)
        one16 = sb("one16", [P, 2], F16)
        bn6 = sb("bn6", [P, T, 6], F32)
        mean_var = sb("mean_var", [P, T, 2], F32)
        var_eps = sb("var_eps", [P, 2 * T], F32)
        std = sb("std", [P, 2 * T], F32)
        rstd = sb("rstd", [P, 2 * T], F32)
        table = sb("table", [P, B], F32)
        exp_up = sb("exp_up", [P, 1], F32)
        head_max = sb("head_max", [P, 2, QT], F32)
        head_bias = sb("head_bias", [P, 2, QT], F32)
        head_sum = sb("head_sum", [P, 2, QT], F32)
        head_rec = sb("head_rec", [P, 2, QT], F32)
        row_max = sb("row_max", [P, QT], F32)
        row_part = sb("row_part", [P, MC, QT], F32)
        row_bias = sb("row_bias", [P, B, QT], F32)
        row_sum = sb("row_sum", [P, B, QT, MC], F32)
        row_rec = sb("row_rec", [P, T], F32)
        sq_sum = sb("sq_sum", [P, T + M // P], F32)
        sq_root = sb("sq_root", [P, T + M // P], F32)
        sq_rec = sb("sq_rec", [P, T + M // P], F32)

        ident = cst[:, C_ID:C_ID + P]
        ones = cst[:, C_ONE:C_ONE + P]
        decay = cst[:, C_DECAY:C_DECAY + QT * P]

        def view(buf, at, n, dt, *dims):
            v = buf[:, at:at + n, :].rearrange("p a b -> p (a b)")
            if dt != F32:
                v = v.bitcast(dt)
            names = "abc"[:len(dims)]
            if len(dims) > 1:
                v = v.rearrange(f"p ({' '.join(names)}) -> p {' '.join(names)}", **dict(zip(names, dims)))
            return v

        def flat(v):
            return v.rearrange("p a n -> p (a n)")

        NH = B * H
        qT = [view(A, 4 * i, 4, F16, DC, T * P) for i in range(2)]
        pp = [[view(A, 8 + 4 * u + 2 * i, 2, F16, CT, 512) for i in range(2)] for u in range(2)]
        x_nat = [view(S, 16, 4, F32, QT, 512), view(A, 12, 4, F32, QT, 512)]
        resid = view(S, 0, 8, F32, T, 512)
        tT = [view(S, 8 + 4 * i, 4, F16, DC, T * P) for i in range(2)]
        nat = view(S, 16, 8, F32, T, 512)
        q_stack = view(S, 24, 16, F16, B, H, NQ)
        k_stack = view(S, 40, 16, F16, B, H, NQ)
        o_nat = view(S, 56, 8, F32, T, 512)
        v_nat = [view(S, 56 + 4 * i, 4, F16, NH, QT, HD) for i in range(2)]
        y_nat = view(S, 16, 8, F32, QT, NH, HD)
        qk = [[view(A, 8 * w + 4 * i, 4, F16, B, DC, NQ) for i in range(2)] for w in range(2)]
        a_flat = flat(A[:, :, :])
        NB = QT * (QT + 1) // 2 * P
        prob = [a_flat[:, u * NB:(u + 1) * NB] for u in range(2)]
        prob_t = [a_flat[:, (2 + u) * NB:(3 + u) * NB] for u in range(2)]
        prob_16 = [[a_flat[:, (4 + u) * NB:(5 + u) * NB].bitcast(F16)[:, i * NB:(i + 1) * NB]
                    for i in range(2)] for u in range(2)]
        xn_nat = [view(S, 24 + 4 * i, 4, F16, T, 512) for i in range(2)]
        snT = [view(S, 48 + 8 * i, 8, F16, DC, M) for i in range(2)]
        L = view(S, 32, 16, F32, MC, QT, 512)
        se_nat = [view(S, at, 8, F32, M // P // 2, 512) for at in (24, 40)]
        disp = view(A, 0, 4, F32, QT, 512)
        disp_16 = [[view(A, 4 + 4 * u + 2 * i, 2, F16, QT, 512) for i in range(2)] for u in range(2)]
        comb = view(A, 12, 4, F32, QT, 512)
        slots = view(S, 16, 4, F32, DC, 512)
        slots_16 = view(S, 20, 4, F16, 2, DC, 512)
        comb_16 = [[whi[:, 0, :, :], wlo[:, 0, :, :]], [view(A, 12 + 2 * i, 2, F16, 4, 512) for i in range(2)]]
        e_slots = [view(S, 8 + 4 * u, 4, F16, 2, DC, 512) for u in range(2)]
        e_comb = [view(S, 16 + 4 * u, 4, F16, 2, 4, 512) for u in range(2)]
        hid = view(S, 24, 4, F32, CT, 512)
        hid_16 = [[view(S, 28 + 4 * u + 2 * i, 2, F16, CT, 512) for i in range(2)] for u in range(2)]
        eo = view(S, 56, 4, F32, 4, 512)
        eo_16 = [view(S, 44 + 2 * i, 2, F16, 4, 512) for i in range(2)]
        b2_rows = view(S, 48, 8, F32, E, 512)
        b1_cols = run_max[:, 0:E * HID // P]

        o_scratch = dram("o_scratch", [P, QT * 512], F32)
        slots_dram = dram("slots_dram", [E, P, 2, DC, B, ES], F16)
        comb_dram = dram("comb_dram", [E, P, 2, B, 2, NQ], F16)

        raw_loaded = [sem(f"raw_loaded{u}") for u in range(2)]
        split_hi = sem("split_hi")
        split_lo = sem("split_lo")
        products = sem("products")
        const_loaded = sem("const_loaded")
        x_loaded = [sem(f"x_loaded{b}") for b in range(B)]
        dve_step = sem("dve_step")
        setup_done = sem("setup_done")
        stats_ready = sem("stats_ready")
        var_ready = sem("var_ready")
        std_ready = sem("std_ready")
        squares_ready = sem("squares_ready")
        z_ready = sem("z_ready")
        rows_ready = sem("rows_ready")
        sn_factors = sem("sn_factors")
        sn_scaled = sem("sn_scaled")
        sn_ready = sem("sn_ready")
        turned = sem("turned")
        turned_hi = sem("turned_hi")
        turned_lo = sem("turned_lo")
        scores_kept = sem("scores_kept")
        max_kept = sem("max_kept")
        sum_kept = sem("sum_kept")
        stat_mm = sem("stat_mm")
        stat_dve = sem("stat_dve")
        shifted = sem("shifted")
        tile_shifted = sem("tile_shifted")
        tile_exp = sem("tile_exp")
        tile_hi = sem("tile_hi")
        tile_lo = sem("tile_lo")
        exp_done = sem("exp_done")
        p_hi = sem("p_hi")
        p_lo = sem("p_lo")
        o_ready = sem("o_ready")
        o_moved = sem("o_moved")
        phase2_loaded = sem("phase2_loaded")
        o_loaded = sem("o_loaded")
        decay_loaded = sem("decay_loaded")
        slot_gamma_loaded = sem("slot_gamma_loaded")
        proj_kept = sem("proj_kept")
        qkv_hi = sem("qkv_hi")
        qkv_lo = sem("qkv_lo")
        q_stacked = sem("q_stacked")
        k_stacked = sem("k_stacked")
        head_scores = sem("head_scores")
        head_maxed = sem("head_maxed")
        head_reduced = sem("head_reduced")
        head_rec_ready = sem("head_rec_ready")
        head_exp = sem("head_exp")
        head_turned = sem("head_turned")
        head_decayed = sem("head_decayed")
        head_hi = sem("head_hi")
        head_lo = sem("head_lo")
        head_y = sem("head_y")
        head_kept = sem("head_kept")
        se_loaded = sem("se_loaded")
        xn_hi = sem("xn_hi")
        xn_lo = sem("xn_lo")
        logit_mm = sem("logit_mm")
        logit_kept = sem("logit_kept")
        row_biased = sem("row_biased")
        cmax_ready = sem("cmax_ready")
        max_mm = sem("max_mm")
        sum_mm = sem("sum_mm")
        max_diag = sem("max_diag")
        sum_diag = sem("sum_diag")
        disp_shift = sem("disp_shift")
        disp_exp = sem("disp_exp")
        disp_hi = sem("disp_hi")
        disp_lo = sem("disp_lo")
        slot_mm = sem("slot_mm")
        slot_kept = sem("slot_kept")
        slot_hi = sem("slot_hi")
        slot_lo = sem("slot_lo")
        first_moved = sem("first_moved")
        slot_moved = sem("slot_moved")
        comb_exp = sem("comb_exp")
        comb_turned = sem("comb_turned")
        comb_hi = sem("comb_hi")
        comb_lo = sem("comb_lo")
        comb_moved = [sem(f"comb_moved{u}") for u in range(2)]
        bias_loaded = sem("bias_loaded")
        e_slots_in = [sem(f"e_slots_in{u}") for u in range(2)]
        e_comb_in = [sem(f"e_comb_in{u}") for u in range(2)]
        hid_done = sem("hid_done")
        hid_hi = sem("hid_hi")
        hid_lo = sem("hid_lo")
        eo_kept = sem("eo_kept")
        eo_half_hi = sem("eo_half_hi")
        eo_half_lo = sem("eo_half_lo")
        eo_hi = sem("eo_hi")
        eo_lo = sem("eo_lo")
        comb_mm = sem("comb_mm")
        comb_kept = sem("comb_kept")
        stored = sem("stored")

        def numerators(g):
            b, mc = divmod(g, MC)
            return L[:, mc, :, :] if b == B - 1 else comb

        def staging(g):
            return g % 2 if g // MC == B - 1 else 0

        def staged_before(g, u):
            return sum(staging(h) == u for h in range(g))

        block = ctx.enter_context(nc.Block())

        TURN_X, TURN_O, TURN_HN, TURN_Y = (range(T * i, T * (i + 1)) for i in range(4))
        late = ([("sn", t) for t in range(QT)] + [("xn", t) for t in range(QT)]
                + [("sn", t) for t in range(QT, M // P)] + [("xn", t) for t in range(QT, T)])
        TURN_SN = [4 * T + late.index(("sn", t)) for t in range(M // P)]
        TURN_XN = [4 * T + late.index(("xn", t)) for t in range(T)]
        TURN_BANK = [n % 4 for n in range(5 * T)] + [2 + n % 2 for n in range(len(late) - T)]

        def beside(g):
            tiles = range(QT * (g + 1), QT * (g + 2))
            return ("sn", tiles) if g + 1 < MC else ("xn", range(QT, T)) if g + 1 == MC else ("", range(0))

        ROWS_X, ROWS_HN, ROWS_XN = 0, T, 2 * T
        SCORE_BANKS = [(0, [(0, 0), (2, P)]), (1, [(1, 0)]), (2, [(3, 0)])]
        SCORE_COL = {q: n for n, q in enumerate([0, 2, 1, 3])}
        TURN_BANKS = [(3, [(0, 0)]), (4, [(1, 0), (3, 3 * P)]), (5, [(2, 0)])]
        PROB_AT = {q: q * (q + 1) // 2 * P for q in range(QT)}
        STACKED = 16 * (P // HD) ** 2


        @block.sync
        def _(sp):
            x_rows = x.rearrange("b (t p) d -> p (b t) d", p=P)

            def load(u, src):
                sp.dma_start(raw[:, u, :], src).then_inc(raw_loaded[u], 16)

            sp.dma_start(x_nat[0], x_rows[:, 0:QT, :]).then_inc(x_loaded[0], 16)
            load(0, ctx_stream[0])
            sp.dma_start(cst[:, 0:C_KPOS + KT], consts[0][:, 0:C_KPOS + KT]).then_inc(const_loaded, 16)
            sp.dma_start(lens_i[:, :], lens.partition_broadcast(P)).then_inc(const_loaded, 16)
            sp.dma_start(x_nat[1], x_rows[:, QT:T, :]).then_inc(x_loaded[1], 16)
            load(1, ctx_stream[1])
            with sp.Fori(1, N_CTX // 2) as i:
                for u in range(2):
                    sp.wait_ge(split_lo, 2 * i + u - 1)
                    load(u, ctx_stream[bass.ds(2 * i + u, 1)].rearrange("a p n -> p (a n)"))
            sp.wait_ge(split_lo, N_WO - 1)
            load(N_WO % 2, square_stream[0])
            sp.wait_ge(p_lo, KC * (B - 1) + 2)
            sp.wait_ge(sum_kept, (KT + 1) * (B - 1) + 1 + 2 * CT)
            for dst, src in ((resid, x_rows), (cst[:, C_SET:C_END], consts[1][:, C_SET:C_END]),
                             (qneg[:, :], xattn_b.partition_broadcast(P)),
                             (run_max[:, :], gamma.partition_broadcast(P))):
                sp.dma_start(dst, src).then_inc(phase2_loaded, 16)
            sp.wait_ge(p_lo, KC * B - 1)
            sp.wait_ge(sum_kept, (KT + 1) * B - CT)
            sp.wait_ge(o_moved, 16)
            sp.dma_start(flat(o_nat[:, 0:QT, :]), o_scratch).then_inc(o_loaded, 16)
            sp.wait_ge(split_lo, N_WQ - 1)
            load(N_WQ % 2, square_stream[N_WQ - N_WO])
            sp.wait_ge(o_ready, T)
            sp.dma_start(decay_blocks, consts[1][:, C_BLOCKS:C_ALL]).then_inc(decay_loaded, 16)
            sp.dma_start(run_sum[:, :], slot_gamma.partition_broadcast(P)).then_inc(slot_gamma_loaded, 16)
            for n in (N_WK, N_WV, N_WP):
                sp.wait_ge(split_lo, n - 1)
                load(n % 2, square_stream[n - N_WO])
            for w, (stack, done, parts) in enumerate(((q_stack, q_stacked, (0, 0, 1, 1)),
                                                      (k_stack, k_stacked, (0, 1, 0, 1)))):
                sp.wait_ge(qkv_lo, T * (w + 1))
                if w:
                    sp.wait_ge(split_lo, N_EXP - 1)
                    load(N_EXP % 2, expert_stream[0])
                for j in range(P // HD):
                    for g, part in enumerate(parts):
                        sp.dma_start(stack[HD * g:HD * (g + 1), :, j::P // HD, :],
                                     qk[w][part][HD * j:HD * (j + 1), :, :, :]
                                     ).then_inc(done, 16)
            sp.wait_ge(head_scores, len(SCORE_BANKS) * H)
            for i in range(2):
                half = slice(M // 2 * i, M // 2 * (i + 1))
                sp.dma_start(se_nat[i], slot_embeds[half, :].rearrange("(t p) d -> p t d", p=P)).then_inc(se_loaded, 16)
            sp.wait_ge(split_lo, N_EXP)
            load((N_EXP + 1) % 2, expert_stream[1])

            def load_expert(e, u, what):
                if what == "slots":
                    sp.dma_start(e_slots[u].rearrange("p a b n -> p (a b n)"),
                                 slots_dram[bass.ds(e, 1)].rearrange("e p a c b s -> p (e a c b s)")
                                 ).then_inc(e_slots_in[u], 16)
                else:
                    sp.dma_start(e_comb[u].rearrange("p a b n -> p (a b n)"),
                                 comb_dram[bass.ds(e, 1)].rearrange("e p a b m n -> p (e a b m n)")
                                 ).then_inc(e_comb_in[u], 16)

            def store_combine(g):
                b, mc = divmod(g, MC)
                sp.wait_ge(comb_lo, 4 * (g + 1))
                for part in range(2):
                    sp.dma_start(comb_dram[2 * mc:2 * mc + 2, :, part, b, :, :].rearrange("e p m n -> p e (m n)"),
                                 comb_16[staging(g)][part].rearrange("p (e m) n -> p e (m n)", e=2)
                                 ).then_inc(comb_moved[staging(g)], 16)

            def store_slots(g):
                b, mc = divmod(g, MC)
                sp.wait_ge(slot_lo, g + 1)
                for e in range(2 * mc, 2 * mc + 2):
                    for part in range(2):
                        sp.dma_start(slots_dram[e, :, part, :, b, :],
                                     slots_16[:, part, :, (e % 2) * ES:(e % 2 + 1) * ES]
                                     ).then_inc(slot_moved if e else first_moved, 16)

            for g in range(GROUPS):
                for c in COMBINED[g][:1]:
                    store_combine(c)
                if g:
                    store_slots(g - 1)
                for c in COMBINED[g][1:]:
                    store_combine(c)
                if g == GROUPS - 2:
                    sp.wait_ge(first_moved, 32 * B)
                    sp.wait_ge(logit_mm, QT * GROUPS)
                    load_expert(0, 0, "slots")
                    sp.dma_start(b1_cols, b1).then_inc(bias_loaded, 16)
                    sp.dma_start(b2_rows, b2.partition_broadcast(P)).then_inc(bias_loaded, 16)
                    load(N_EXP % 2, expert_stream[2])
            store_slots(GROUPS - 1)

            def expert_loads(e, u, first=False, last=False):
                for s in range(3 if first else 2, 8 if last else 10):
                    n = N_EXP + s
                    sp.wait_ge(split_lo, 8 * e + n - 1)
                    load(n % 2, expert_stream[bass.ds(8 * e + s, 1)].rearrange("a p n -> p (a n)"))
                    if s == 3 and first:
                        sp.wait_ge(slot_moved, 64 * GROUPS - 32 * B)
                        for pair in range(2):
                            sp.wait_ge(comb_moved[pair], 32 * staged_before(GROUPS, pair))
                        load_expert(e, u, "comb")
                    if s == 3 and not last:
                        load_expert(e + 1, 1 - u, "slots")
                    if s == 8:
                        if not first:
                            sp.wait_ge(comb_mm, T * e)
                        load_expert(e + 1, 1 - u, "comb")

            expert_loads(0, 0, first=True)
            with sp.Fori(0, E // 2 - 1) as i:
                expert_loads(2 * i + 1, 1)
                expert_loads(2 * i + 2, 0)
            expert_loads(E - 1, 1, last=True)

            out_rows = out.rearrange("b (t p) d -> p (b t) d", p=P)
            for t in range(T):
                sp.wait_ge(comb_kept, T * (E - 1) + t + 1)
                sp.dma_start(out_rows[:, t, :], resid[:, t, :]).then_inc(stored, 16)
            sp.wait_ge(stored, 16 * T)

        @block.gpsimd
        def _(pool):
            for b in range(B):
                if b:
                    pool.wait_ge(stat_mm, 3 * b)
                nc.gpsimd.memset(run_sum[:, :], 0.0).then_inc(sum_kept, 1)
                with pool.Fori(0, KC) as j:
                    pool.wait_ge(exp_done, KC * b + j + 1)
                    for k in range(CT):
                        tile = 4 * j + k
                        pool.wait_ge(sum_kept, (KT + 1) * b + 1 + tile)
                        nc.gpsimd.tensor_tensor(
                            run_sum[:, :], run_sum[:, :], flat(S[:, bass.ds(tile, 1), :]),
                            ALU.add).then_inc(sum_kept, 1)
                if b == 0:
                    pool.wait_ge(o_ready, QT)
                    pool.dma_start(o_scratch, flat(S[:, KT - QT:KT, :])).then_inc(o_moved, 16)

            with pool.Fori(0, NH // 2) as i:
                for u in range(2):
                    pool.wait_ge(head_hi, 2 * i + u + 1)
                    nc.gpsimd.tensor_tensor(prob_16[u][1], prob_t[u], prob_16[u][0],
                                            ALU.subtract).then_inc(head_lo, 1)

            pool.wait_ge(slot_gamma_loaded, 16)
            for t in range(M // P):
                pool.wait_ge(sn_scaled, t + 1)
                rows = se_nat[t // 8][:, t % 8, :]
                nc.gpsimd.tensor_tensor(rows, rows, run_sum[:, :], ALU.mult).then_inc(sn_ready, 1)

            for g in range(GROUPS):
                pool.wait_ge(slot_hi, g + 1)
                nc.gpsimd.tensor_tensor(slots_16[:, 1, :, :], slots, slots_16[:, 0, :, :],
                                        ALU.subtract).then_inc(slot_lo, 1)

        @block.scalar
        def _(act):
            def hi_part(pair, u):
                n = 2 * pair + u
                act.wait_ge(raw_loaded[u], 16 * pair + 16)
                if not (isinstance(n, int) and n < 2):
                    act.wait_ge(products, products_after(n - 2))
                nc.scalar.activation(flat(whi[:, u, :, :]), raw[:, u, :], ACT.Copy, scale=UP).then_inc(split_hi, 1)

            roots = [0]

            def square_root(b):
                cols = slice(QT * b, QT * (b + 1))
                roots[0] += 1
                act.wait_ge(var_ready, roots[0])
                nc.scalar.activation(std[:, cols], var_eps[:, cols], ACT.Sqrt).then_inc(std_ready, 1)

            def turn_hi(order, tiles, dst, scale):
                for t in tiles:
                    act.wait_ge(turned, order[t] + 1)
                    nc.scalar.activation(dst[:, :, t * P:(t + 1) * P],
                                         psum[:, TURN_BANK[order[t]], :].rearrange("p (c n) -> p c n", c=DC),
                                         ACT.Copy, scale=scale).then_inc(turned_hi, 1)

            square_root(0)
            hi_part(0, 0)
            turn_hi(TURN_X, range(0, QT), qT[0], UP)
            square_root(1)
            act.wait_ge(setup_done, 3)

            for b in range(B):
                start = b * N_CTX // 4
                if b == 0:
                    hi_part(0, 1)
                    hi_part(1, 0)
                with act.Fori(start + (b == 0), start + KC // 2) as i:
                    hi_part(i, 1)
                    hi_part(i + 1, 0)

                def probabilities(i, u):
                    j = 2 * i + u - KC * (2 * b + 1)
                    act.wait_ge(shifted, KC * b + j + 1)
                    act.nop(nofuse=True)
                    s = S[:, bass.ds(CT * j, CT), :]
                    nc.scalar.activation(s, s, ACT.Exp, bias=exp_up[:, 0:1],
                                         scale=DOWN / D ** 0.5).then_inc(exp_done, 1)
                    act.wait_ge(exp_done, KC * b + j + 1)
                    act.wait_ge(products, products_after(2 * i + u - 2))
                    act.nop(nofuse=True)
                    nc.scalar.activation(pp[u][0], s, ACT.Copy).then_inc(p_hi, 1)

                start += KC // 2
                nc.scalar.activation(table[:, b:b + 1], exp_up[:, 0:1], ACT.Exp)
                if b:
                    act.wait_ge(products, products_after(N_CTX // B - 1))
                for k in range(CT):
                    if k < CT - 1:
                        act.wait_ge(tile_shifted, (CT - 1) * b + k + 1)
                    else:
                        act.wait_ge(shifted, KC * b + 1)
                    last = nc.scalar.activation(S[:, k, :], S[:, k, :], ACT.Exp, bias=exp_up[:, 0:1],
                                                scale=DOWN / D ** 0.5)
                    if k < CT - 1:
                        last.then_inc(tile_exp, 1)
                        act.wait_ge(tile_exp, (CT - 1) * b + k + 1)
                    else:
                        last.then_inc(exp_done, 1)
                        act.wait_ge(exp_done, KC * b + 1)
                    nc.scalar.activation(pp[0][0][:, k, :], S[:, k, :], ACT.Copy).then_inc(
                        tile_hi if k < CT - 1 else p_hi, 1)
                hi_part(start, 1)
                if b == 0:
                    turn_hi(TURN_X, range(QT, T), qT[0], UP)
                probabilities(start, 1)
                hi_part(start + 1, 0)
                with act.Fori(start + 1, start + KC // 2) as i:
                    probabilities(i, 0)
                    hi_part(i, 1)
                    probabilities(i, 1)
                    hi_part(i + 1, 0)

            turn_hi(TURN_O, range(T), tT[0], UP)
            hi_part(N_WQ // 2, N_WQ % 2)
            square_root(0)
            turn_hi(TURN_HN, range(0, QT), tT[0], UP)
            square_root(1)

            def qkv_high(n, t, dst):
                act.wait_ge(products, products_after(n - 1) + t + 1)
                src = psum[:, 4 + t % 4, :]
                if len(dst.shape) == 3:
                    src = src.rearrange("p (h d) -> p h d", h=H)
                nc.scalar.activation(dst, src, ACT.Copy, scale=1.0 / UP).then_inc(qkv_hi, 1)

            for w, n in enumerate((N_WQ, N_WK)):
                for t in range(T):
                    b, f = divmod(t, DC)
                    if n == N_WQ and t == QT:
                        turn_hi(TURN_HN, range(QT, T), tT[0], UP)
                    qkv_high(n, t, qk[w][0][:, b, f, :])
                    if t == 0:
                        hi_part((n + 1) // 2, (n + 1) % 2)
            for t in range(T):
                b, k = divmod(t, QT)
                qkv_high(N_WV, t, v_nat[0][:, b * H:(b + 1) * H, k, :])
                if t == 0:
                    hi_part(N_WP // 2, N_WP % 2)

            def head_exponentials(g, u):
                for n, (bank, tiles) in enumerate(SCORE_BANKS):
                    act.wait_ge(head_maxed, 3 * g + n + 1)
                    if not (isinstance(g, int) and g < 2):
                        act.wait_ge(head_turned, g - 1)
                    for q, at in tiles:
                        c, width = SCORE_COL[q], (q + 1) * P
                        last = nc.scalar.activation(
                            prob[u][:, PROB_AT[q]:PROB_AT[q] + width], psum[:, bank, at:at + width], ACT.Exp,
                            bias=head_bias[:, u, c:c + 1], scale=DOWN / HD ** 0.5,
                            accum_out=head_sum[:, u, q:q + 1])
                    last.then_inc(head_exp, 1)

            def head_high(g, u):
                act.wait_ge(head_decayed, g + 1)
                if not (isinstance(g, int) and g < 2):
                    act.wait_ge(head_y, g - 1)
                nc.scalar.activation(prob_16[u][0], prob_t[u], ACT.Copy).then_inc(head_hi, 1)

            act.wait_ge(q_stacked, STACKED)
            act.wait_ge(k_stacked, STACKED)
            head_exponentials(0, 0)
            for g in range(4):
                head_exponentials(g + 1, 1 - g % 2)
                head_high(g, g % 2)
            with act.Fori(2, NH // 2 - 1) as i:
                for u in range(2):
                    head_exponentials(2 * i + u + 1, 1 - u)
                    head_high(2 * i + u, u)
            head_exponentials(NH - 1, 1)
            head_high(NH - 2, 0)
            head_high(NH - 1, 1)
            turn_hi(TURN_Y, range(T), tT[0], UP)
            hi_part(N_EXP // 2, N_EXP % 2)

            n_squares = [0]

            def squares(tiles, first):
                for n, rows in enumerate(tiles):
                    n_squares[0] += 1
                    nc.scalar.activation(bcast[:, :], rows, ACT.Square,
                                         accum_out=sq_sum[:, first + n:first + n + 1]).then_inc(squares_ready, 1)
                    act.wait_ge(squares_ready, n_squares[0])
                cols = slice(first, first + len(tiles))
                nc.scalar.activation(sq_root[:, cols], sq_sum[:, cols], ACT.Sqrt).then_inc(std_ready, 1)

            def token_squares(b):
                square_root(b)
                act.wait_ge(z_ready, QT * (b + 1))
                squares([nat[:, t, :] for t in range(QT * b, QT * (b + 1))], QT * b)

            def slot_squares(i):
                squares([se_nat[t // 8][:, t % 8, :] for t in range(4 * i, 4 * i + 4)], T + 4 * i)

            def scale_slots(i):
                act.wait_ge(sn_factors, i + 1)
                for t in range(4 * i, 4 * i + 4):
                    rows = se_nat[t // 8][:, t % 8, :]
                    nc.scalar.activation(rows, rows, ACT.Copy, scale=sq_rec[:, T + t:T + t + 1]).then_inc(sn_scaled, 1)

            act.wait_ge(se_loaded, 32)
            slot_squares(0)
            slot_squares(1)
            scale_slots(0)
            token_squares(0)
            turn_hi(TURN_SN, range(0, QT), snT[0], UP)
            scale_slots(1)
            slot_squares(2)
            turn_hi(TURN_XN, range(0, QT), tT[0], UP)
            scale_slots(2)
            token_squares(1)

            def turn_hi_beside(kind, tiles):
                if kind == "sn":
                    turn_hi(TURN_SN, tiles, snT[0], UP)
                elif kind == "xn":
                    turn_hi(TURN_XN, tiles, tT[0], UP)

            def disp_high(g):
                act.wait_ge(disp_shift, g + 1)
                nc.scalar.activation(disp, disp, ACT.Exp, bias=exp_up[:, 0:1]).then_inc(disp_exp, 1)
                act.wait_ge(disp_exp, g + 1)
                if g >= 2:
                    act.wait_ge(slot_mm, 4 * (g - 1))
                nc.scalar.activation(disp_16[g % 2][0], disp, ACT.Copy).then_inc(disp_hi, 1)

            def combine_exp(g):
                b, mc = divmod(g, MC)
                act.wait_ge(row_biased, b + 1)
                if b:
                    act.wait_ge(disp_shift, g + 1)
                elif g:
                    act.wait_ge(comb_turned, 4 * g)
                for q in range(QT):
                    last = nc.scalar.activation(numerators(g)[:, q, :], L[:, mc, q, :], ACT.Exp,
                                                bias=row_bias[:, b, q:q + 1],
                                                accum_out=row_sum[:, b, q, mc:mc + 1])
                last.then_inc(comb_exp, 1)

            def combine_high(g):
                if staged_before(g, staging(g)):
                    act.wait_ge(comb_moved[staging(g)], 32 * staged_before(g, staging(g)))
                for m in range(4):
                    act.wait_ge(comb_turned, 4 * g + m + 1)
                    nc.scalar.activation(comb_16[staging(g)][0][:, m, :], psum[:, 2 + m % 2, :], ACT.Copy).then_inc(comb_hi, 1)

            def slots_high(g):
                act.wait_ge(slot_kept, 4 * g + 4)
                if g:
                    act.wait_ge(first_moved, 32 * ((g - 1) // MC + 1))
                    act.wait_ge(slot_moved, 64 * g - 32 * ((g - 1) // MC + 1))
                nc.scalar.activation(slots_16[:, 0, :, :], slots, ACT.Copy).then_inc(slot_hi, 1)

            def keep_logits(g, rows):
                b, mc = divmod(g, MC)
                if b:
                    act.wait_ge(disp_shift, g - MC + 1)
                    act.wait_ge(comb_exp, g - MC + 1)
                for q in rows:
                    act.wait_ge(logit_mm, QT * g + q + 1)
                    nc.scalar.activation(L[:, mc, q, :], psum[:, q % 2, :], ACT.Copy,
                                         scale=DOWN).then_inc(logit_kept, 1)

            def tokens_high(b):
                for t in range(QT * b, QT * (b + 1)):
                    act.wait_ge(rows_ready, ROWS_XN + t + 1)
                    nc.scalar.activation(xn_nat[0][:, t, :], nat[:, t, :], ACT.Copy, scale=UP).then_inc(xn_hi, 1)

            for g in range(-2, GROUPS):
                combined = COMBINED[g] if g >= 0 else []
                for c in combined[:1]:
                    combine_exp(c)
                if g + 2 < GROUPS:
                    kind, tiles = beside(g + 2)
                    keep_logits(g + 2, range(0, 1))
                    turn_hi_beside(kind, tiles[0:2])
                    keep_logits(g + 2, range(1, 2))
                    turn_hi_beside(kind, tiles[2:4])
                    if g == 0:
                        tokens_high(0)
                if g >= 1:
                    slots_high(g - 1)
                if g + 2 < GROUPS:
                    keep_logits(g + 2, range(2, QT))
                    if g == -2:
                        slot_squares(3)
                        scale_slots(3)
                    if g == 0:
                        tokens_high(1)
                if 0 <= g + 1 < GROUPS:
                    disp_high(g + 1)
                for c in combined[1:]:
                    combine_exp(c)
                for c in combined:
                    combine_high(c)
            slots_high(GROUPS - 1)

            def chunk_high(e, s):
                n = N_EXP + s
                act.wait_ge(raw_loaded[n % 2], 16 * (4 * e + n // 2 + 1))
                act.wait_ge(products, products_after(N_EXP - 1) + 4 * (8 * e + s - 1))
                nc.scalar.activation(flat(whi[:, n % 2, :, :]), raw[:, n % 2, :], ACT.Copy, scale=UP).then_inc(split_hi, 1)

            def hidden(e, hc, s):
                q = HC * e + hc
                first = isinstance(q, int) and q == 0
                if not first:
                    act.wait_ge(hid_lo, q)
                for k in range(CT):
                    act.wait_ge(products, products_after(N_EXP - 1) + 4 * (8 * e + s) + k + 1)
                    act.nop(nofuse=True)
                    nc.scalar.activation(hid[:, k, :], psum[:, k, :], ACT.Gelu,
                                         bias=b1_cols[:, bass.ds(CT * q + k, 1)], scale=DOWN).then_inc(hid_done, 1)
                act.wait_ge(hid_done, CT * q + CT)
                nc.scalar.activation(hid_16[hc % 2][0], hid, ACT.Copy, scale=UP).then_inc(hid_hi, 1)

            def out_high(e):
                act.wait_ge(eo_kept, 4 * e + 4)
                if not (isinstance(e, int) and e == 0):
                    act.wait_ge(comb_mm, T * e)
                nc.scalar.activation(eo_16[0], eo, ACT.Copy).then_inc(eo_hi, 1)

            def expert(e, first=False, last=False):
                chunk_high(e, 2)
                if not first:
                    out_high(e - 1)
                hidden(e, 1, 1)
                chunk_high(e, 3)
                chunk_high(e, 4)
                hidden(e, 2, 3)
                chunk_high(e, 5)
                chunk_high(e, 6)
                hidden(e, 3, 5)
                chunk_high(e, 7)
                if not last:
                    chunk_high(e, 8)
                    hidden(e + 1, 0, -1)
                    chunk_high(e, 9)

            act.wait_ge(comb_moved[0], 32 * staged_before(GROUPS, 0))
            chunk_high(0, 1)
            act.wait_ge(bias_loaded, 32)
            hidden(0, 0, 0)
            expert(0, first=True)
            with act.Fori(1, E - 1) as e:
                expert(e)
            expert(E - 1, last=True)
            act.wait_ge(eo_kept, 4 * E - 2)
            act.wait_ge(comb_mm, T * (E - 1))
            nc.scalar.activation(eo_16[0][:, 0:2, :], eo[:, 0:2, :], ACT.Copy).then_inc(eo_half_hi, 1)
            act.wait_ge(eo_kept, 4 * E)
            nc.scalar.activation(eo_16[0][:, 2:4, :], eo[:, 2:4, :], ACT.Copy).then_inc(eo_hi, 1)

        @block.vector
        def _(dve):
            steps = [0]

            def link(ins):
                steps[0] += 1
                ins.then_inc(dve_step, 1)
                dve.wait_ge(dve_step, steps[0])

            def lo_part(pair, u):
                dve.wait_ge(split_hi, 2 * pair + u + 1)
                nc.vector.scalar_tensor_tensor(flat(wlo[:, u, :, :]), raw[:, u, :], UP, flat(whi[:, u, :, :]),
                                               ALU.mult, ALU.subtract).then_inc(split_lo, 1)

            roots = [0]

            n_statistics = [0]

            def statistics(src, t):
                n_statistics[0] += 1
                nc.vector.bn_stats(bn6[:, t, :], src[:, t % QT, :]).then_inc(stats_ready, 1)

            def layernorm(dst, src, b, done):
                dve.wait_ge(stats_ready, n_statistics[0])
                tiles = range(QT * b, QT * (b + 1))
                cols = slice(QT * b, QT * (b + 1))
                for t in tiles:
                    last = nc.vector.bn_aggr(mean_var[:, t, :], bn6[:, t, :])
                link(last)
                nc.vector.tensor_scalar(var_eps[:, cols], mean_var[:, cols, 1], EPS, None, ALU.add).then_inc(var_ready, 1)
                roots[0] += 1
                dve.wait_ge(std_ready, roots[0])
                link(nc.vector.reciprocal(rstd[:, cols], std[:, cols]))
                for t in tiles:
                    nc.vector.tensor_scalar(dst[:, t % QT, :], src[:, t % QT, :], mean_var[:, t, 0:1], rstd[:, t:t + 1],
                                            ALU.subtract, ALU.mult).then_inc(done, 1)

            def turn_lo(order, tiles, dst, hi, scale):
                for t in tiles:
                    dve.wait_ge(turned_hi, order[t] + 1)
                    nc.vector.scalar_tensor_tensor(
                        dst[:, :, t * P:(t + 1) * P],
                        psum[:, TURN_BANK[order[t]], :].rearrange("p (c n) -> p c n", c=DC), scale,
                        hi[:, :, t * P:(t + 1) * P], ALU.mult, ALU.subtract).then_inc(turned_lo, 1)

            def diagonals():
                return nc.vector.tensor_tensor(diag[:, :, :], ident.unsqueeze(1).broadcast_to([P, 4, P]),
                                               col[:, :].unsqueeze(2).broadcast_to([P, 4, P]), ALU.mult)

            def layernorm_x(b):
                dve.wait_ge(x_loaded[b], 16)
                for t in range(QT * b, QT * (b + 1)):
                    statistics(x_nat[b], t)
                layernorm(x_nat[b], x_nat[b], b, rows_ready)

            nc.vector.memset(exp_up[:, :], EXP_UP).then_inc(setup_done, 1)
            layernorm_x(0)
            lo_part(0, 0)
            turn_lo(TURN_X, range(0, QT), qT[1], qT[0], UP)
            dve.wait_ge(const_loaded, 32)
            nc.vector.tensor_copy(ident16[:, :], ident).then_inc(setup_done, 1)
            nc.vector.memset(one16[:, :], 1.0).then_inc(setup_done, 1)
            link(nc.vector.tensor_copy(lens_f[:, :], lens_i[:, :]))
            layernorm_x(1)

            for b in range(B):
                link(nc.vector.tensor_scalar(qneg[:, :], cst[:, C_QPOS:C_QPOS + NQ], lens_f[:, b:b + 1],
                                             NEG * D ** 0.5 / DOWN, ALU.is_ge, ALU.mult))
                link(nc.vector.tensor_scalar(kmask[:, :], cst[:, C_KPOS:C_KPOS + KT], lens_f[:, b:b + 1],
                                             None, ALU.is_ge))

                def keep_scores(i, u, k):
                    tile = CT * (2 * i + u - 2 * KC * b) + k
                    dve.wait_ge(products, 4 * (2 * i + u) + k + 1)
                    nc.vector.scalar_tensor_tensor(
                        flat(S[:, bass.ds(tile, 1), :]), qneg[:, :],
                        kmask[:, bass.ds(tile, 1)], psum[:, k, :], ALU.mult, ALU.add).then_inc(scores_kept, 1)

                def keep_maximum(i, u, k):
                    tile = CT * (2 * i + u - 2 * KC * b) + k
                    dve.wait_ge(scores_kept, KT * b + tile + 1)
                    dve.wait_ge(max_kept, (KT + 1) * b + tile + 1)
                    nc.vector.tensor_tensor(run_max[:, :], run_max[:, :], flat(S[:, bass.ds(tile, 1), :]),
                                            ALU.max).then_inc(max_kept, 1)

                nc.vector.memset(run_max[:, :], -3.0e38).then_inc(max_kept, 1)
                start = b * N_CTX // 4

                def keep_pair(i):
                    for u in range(2):
                        keep_scores(i, u, 0)
                        lo_part(i + u, 1 - u)
                        for k in range(1, CT):
                            keep_maximum(i, u, k - 1)
                            keep_scores(i, u, k)
                        keep_maximum(i, u, CT - 1)

                keep_pair(start)
                if b:
                    dve.wait_ge(o_moved, 16)
                with dve.Fori(start + 1, start + KC // 2) as i:
                    keep_pair(i)
                dve.wait_ge(stat_mm, 3 * b + 1)
                link(nc.vector.tensor_reduce(col[:, :], psum[:, 0, :].rearrange("p (a n) -> p a n", a=QT),
                                             AX.X, ALU.max))
                diagonals().then_inc(stat_dve, 1)
                dve.wait_ge(stat_mm, 3 * b + 2)

                nc.vector.tensor_tensor(S[:, 0, :], S[:, 0, :], psum[:, 1, :], ALU.subtract).then_inc(tile_shifted, 1)
                link(nc.vector.tensor_copy(bcast[:, :], psum[:, 1, :]))
                for k in range(1, CT):
                    nc.vector.tensor_tensor(S[:, k, :], S[:, k, :], bcast[:, :], ALU.subtract).then_inc(
                        tile_shifted if k < CT - 1 else shifted, 1)
                for k in range(CT):
                    if k < CT - 1:
                        dve.wait_ge(tile_hi, (CT - 1) * b + k + 1)
                    else:
                        dve.wait_ge(p_hi, KC * b + 1)
                    nc.vector.tensor_tensor(pp[0][1][:, k, :], S[:, k, :], pp[0][0][:, k, :],
                                            ALU.subtract).then_inc(tile_lo if k < CT - 1 else p_lo, 1)

                def shift(i, u):
                    s = S[:, bass.ds(CT * (2 * i + u - KC * (2 * b + 1)), CT), :]
                    nc.vector.tensor_tensor(s, s, bcast[:, :].unsqueeze(1).broadcast_to([P, CT, 512]),
                                            ALU.subtract).then_inc(shifted, 1)

                def p_low(i, u):
                    j = 2 * i + u - KC * (2 * b + 1)
                    dve.wait_ge(p_hi, KC * b + j + 1)
                    nc.vector.tensor_tensor(pp[u][1], S[:, bass.ds(CT * j, CT), :], pp[u][0],
                                            ALU.subtract).then_inc(p_lo, 1)

                last = (b + 1) * N_CTX // 4
                start = last - KC // 2
                shift(start, 1)
                lo_part(start, 1)
                if b == 0:
                    turn_lo(TURN_X, range(QT, T), qT[1], qT[0], UP)
                shift(start + 1, 0)
                p_low(start, 1)
                lo_part(start + 1, 0)
                with dve.Fori(start + 1, last - 1) as i:
                    shift(i, 1)
                    p_low(i, 0)
                    lo_part(i, 1)
                    shift(i + 1, 0)
                    p_low(i, 1)
                    lo_part(i + 1, 0)
                shift(last - 1, 1)
                p_low(last - 1, 0)
                lo_part(last - 1, 1)
                p_low(last - 1, 1)
                lo_part(last, 0)
                dve.wait_ge(stat_mm, 3 * b + 3)
                link(nc.vector.reciprocal(rcol[:, :], psum[:, CT - 1, 0:2 * QT].rearrange("p (a n) -> p a n", n=2)[:, :, 0]))
                for q in range(QT):
                    nc.vector.tensor_scalar(S[:, KT - QT + q, :], psum[:, 4 + q, :], rcol[:, q:q + 1], 1.0 / UP,
                                            ALU.mult, ALU.mult).then_inc(o_ready, 1)

            turn_lo(TURN_O, range(T), tT[1], tT[0], UP)
            dve.wait_ge(phase2_loaded, 16 * 4)
            nc.vector.tensor_copy(causal16[:, :], cst[:, C_CAUSAL:C_CAUSAL + P]).then_inc(setup_done, 1)
            link(nc.vector.tensor_tensor(resid, resid, qneg[:, :].unsqueeze(1).broadcast_to([P, T, 512]), ALU.add))
            lo_part(N_WQ // 2, N_WQ % 2)

            def keep_projection(n, tiles):
                for t in tiles:
                    dve.wait_ge(products, products_after(n - 1) + t + 1)
                    nc.vector.scalar_tensor_tensor(resid[:, t, :], psum[:, 4 + t % 4, :], DOWN, resid[:, t, :],
                                                   ALU.mult, ALU.add).then_inc(proj_kept, 1)
                    dve.wait_ge(proj_kept, (T if n == N_WP else 0) + t + 1)
                    b = t // QT
                    statistics(resid[:, QT * b:QT * (b + 1), :], t)

            def layernorm_residual(b, done):
                layernorm(*(rows[:, QT * b:QT * (b + 1), :] for rows in (nat, resid)), b, done)

            keep_projection(N_WO, range(0, QT))
            layernorm_residual(0, rows_ready)
            keep_projection(N_WO, range(QT, T - 1))
            turn_lo(TURN_HN, range(0, QT), tT[1], tT[0], UP)
            keep_projection(N_WO, range(T - 1, T))
            layernorm_residual(1, rows_ready)

            def qkv_low(w, t, dst, hi):
                dve.wait_ge(qkv_hi, T * w + t + 1)
                src = psum[:, 4 + t % 4, :]
                if len(dst.shape) == 3:
                    src = src.rearrange("p (h d) -> p h d", h=H)
                nc.vector.scalar_tensor_tensor(dst, src, 1.0 / UP, hi, ALU.mult, ALU.subtract).then_inc(qkv_lo, 1)

            for w, n in enumerate((N_WQ, N_WK)):
                for t in range(T):
                    b, f = divmod(t, DC)
                    if n == N_WQ and t == QT:
                        turn_lo(TURN_HN, range(QT, T), tT[1], tT[0], UP)
                    qkv_low(w, t, *(qk[w][i][:, b, f, :] for i in (1, 0)))
                    if t == 0:
                        lo_part((n + 1) // 2, (n + 1) % 2)
            for t in range(T):
                b, k = divmod(t, QT)
                qkv_low(2, t, *(v_nat[i][:, b * H:(b + 1) * H, k, :] for i in (1, 0)))
                if t == 0:
                    lo_part(N_WP // 2, N_WP % 2)

            def head_maximum(g, u, n):
                bank, tiles = SCORE_BANKS[n]
                dve.wait_ge(head_scores, 3 * g + n + 1)
                for q, at in tiles:
                    c = SCORE_COL[q]
                    last = nc.vector.tensor_reduce(head_max[:, u, c:c + 1], psum[:, bank, at:at + (q + 1) * P],
                                                   AX.X, ALU.max)
                last.then_inc(head_reduced, 1)

            def head_negate(g, u, n):
                tiles = SCORE_BANKS[n][1]
                dve.wait_ge(head_reduced, 3 * g + n + 1)
                cols = slice(SCORE_COL[tiles[0][0]], SCORE_COL[tiles[0][0]] + len(tiles))
                nc.vector.tensor_scalar(head_bias[:, u, cols], head_max[:, u, cols], -DOWN / HD ** 0.5, EXP_UP,
                                        ALU.mult, ALU.add).then_inc(head_maxed, 1)

            def head_decay(u, cols, factors):
                blocks = psum[:, TURN_BANKS[0][0]:TURN_BANKS[-1][0] + 1, :].rearrange("p a n -> p (a n)")
                return nc.vector.tensor_tensor(prob_t[u][:, cols], blocks[:, cols], factors, ALU.mult)

            def head_reciprocal(g, u):
                if not isinstance(g, int) or g >= 2:
                    dve.wait_ge(head_kept, g - 1)
                nc.vector.reciprocal(head_rec[:, u, :], head_sum[:, u, :]).then_inc(head_rec_ready, 1)

            def head_keep(g, u):
                dve.wait_ge(head_rec_ready, g + 1)
                dve.wait_ge(head_y, g + 1)
                nc.vector.scalar_tensor_tensor(
                    y_nat[:, :, bass.ds(g, 1), :].rearrange("p q a d -> p (q a) d"),
                    psum[:, 6 + u, 0:QT * HD].rearrange("p (q d) -> p q d", q=QT), 1.0 / UP,
                    head_rec[:, u, :].unsqueeze(2).broadcast_to([P, QT, HD]), ALU.mult, ALU.mult).then_inc(head_kept, 1)

            def head_step(g, u, scores=True, before=True, out=True):
                if scores:
                    head_maximum(g + 1, 1 - u, 0)
                if before:
                    head_reciprocal(g - 1, 1 - u)
                if scores:
                    head_maximum(g + 1, 1 - u, 1)
                    head_negate(g + 1, 1 - u, 0)
                    head_maximum(g + 1, 1 - u, 2)
                    head_negate(g + 1, 1 - u, 1)
                dve.wait_ge(head_turned, g + 1)
                if not (isinstance(g, int) and g < 2):
                    dve.wait_ge(head_lo, g - 1)
                head_decay(u, slice(0, QT * P), decay)
                if scores:
                    head_negate(g + 1, 1 - u, 2)
                head_decay(u, slice(QT * P, NB), decay_blocks).then_inc(head_decayed, 1)
                if out:
                    head_keep(g - 2, u)

            dve.wait_ge(decay_loaded, 16)
            head_maximum(0, 0, 0)
            head_negate(0, 0, 0)
            head_maximum(0, 0, 1)
            head_negate(0, 0, 1)
            head_maximum(0, 0, 2)
            head_negate(0, 0, 2)
            for g in range(4):
                head_step(g, g % 2, before=g >= 1, out=g >= 2)
            with dve.Fori(2, NH // 2 - 1) as i:
                for u in range(2):
                    head_step(2 * i + u, u)
            head_step(NH - 2, 0)
            head_step(NH - 1, 1, scores=False)
            head_reciprocal(NH - 1, 1)
            head_keep(NH - 2, 0)
            turn_lo(TURN_Y, range(0, QT), tT[1], tT[0], UP)
            head_keep(NH - 1, 1)

            turn_lo(TURN_Y, range(QT, T), tT[1], tT[0], UP)
            lo_part(N_EXP // 2, N_EXP % 2)

            def rms_factors(cols):
                roots[0] += 1
                dve.wait_ge(std_ready, roots[0])
                link(nc.vector.tensor_scalar(sq_root[:, cols], sq_root[:, cols], 1e-12, None, ALU.max))
                link(nc.vector.reciprocal(sq_rec[:, cols], sq_root[:, cols]))
                return nc.vector.tensor_scalar(sq_rec[:, cols], sq_rec[:, cols], D ** 0.5, None, ALU.mult)

            def rms_tokens(b):
                tiles = range(QT * b, QT * (b + 1))
                link(rms_factors(slice(QT * b, QT * (b + 1))))
                for t in tiles:
                    nc.vector.scalar_tensor_tensor(nat[:, t, :], nat[:, t, :], sq_rec[:, t:t + 1],
                                                   run_max[:, :], ALU.mult, ALU.mult).then_inc(rows_ready, 1)

            def slot_factors(i):
                rms_factors(slice(T + 4 * i, T + 4 * i + 4)).then_inc(sn_factors, 1)

            keep_projection(N_WP, range(0, 2))
            slot_factors(0)
            keep_projection(N_WP, range(2, 3))
            slot_factors(1)
            keep_projection(N_WP, range(3, 4))
            layernorm_residual(0, z_ready)
            keep_projection(N_WP, range(4, 6))
            rms_tokens(0)
            keep_projection(N_WP, range(6, T - 1))
            turn_lo(TURN_SN, range(0, QT), snT[1], snT[0], UP)
            keep_projection(N_WP, range(T - 1, T))
            slot_factors(2)
            turn_lo(TURN_XN, range(0, QT), tT[1], tT[0], UP)
            layernorm_residual(1, z_ready)
            rms_tokens(1)

            def turn_lo_beside(kind, tiles):
                if kind == "sn":
                    turn_lo(TURN_SN, tiles, snT[1], snT[0], UP)
                elif kind == "xn":
                    turn_lo(TURN_XN, tiles, tT[1], tT[0], UP)

            def disp_low(g):
                dve.wait_ge(disp_hi, g + 1)
                nc.vector.tensor_tensor(disp_16[g % 2][1], disp, disp_16[g % 2][0], ALU.subtract).then_inc(disp_lo, 1)

            def tokens_low(b):
                for t in range(QT * b, QT * (b + 1)):
                    dve.wait_ge(xn_hi, t + 1)
                    nc.vector.scalar_tensor_tensor(xn_nat[1][:, t, :], nat[:, t, :], UP, xn_nat[0][:, t, :],
                                                   ALU.mult, ALU.subtract).then_inc(xn_lo, 1)

            def column_maxima(g):
                mc = g % MC
                dve.wait_ge(logit_kept, QT * (g + 1))
                nc.vector.tensor_reduce(bcast[:, :], L[:, mc, :, :].rearrange("p q n -> p n q"),
                                        AX.X, ALU.max).then_inc(cmax_ready, 1)

            def disp_maxima(g):
                if g + 1 < GROUPS:
                    turn_lo_beside(*beside(g + 1))
                dve.wait_ge(max_mm, 2 * g + 1)
                link(nc.vector.tensor_reduce(col[:, :], psum[:, 4, :].rearrange("p (a n) -> p a n", a=4),
                                             AX.X, ALU.max))
                diagonals().then_inc(max_diag, 1)

            def row_maxima(g):
                b, mc = divmod(g, MC)
                dve.wait_ge(logit_kept, QT * (g + 1))
                link(nc.vector.tensor_reduce(row_part[:, mc, :], L[:, mc, :, :], AX.X, ALU.max))
                if mc == MC - 1:
                    link(nc.vector.tensor_reduce(row_max[:, :], row_part[:, :, :].rearrange("p m q -> p q m"),
                                                 AX.X, ALU.max))
                    nc.vector.tensor_scalar(row_bias[:, b, :], row_max[:, :], -1.0, EXP_UP, ALU.mult,
                                            ALU.add).then_inc(row_biased, 1)

            def disp_subtract(g):
                mc = g % MC
                if g:
                    dve.wait_ge(disp_lo, g)
                dve.wait_ge(max_mm, 2 * g + 2)
                nc.vector.tensor_tensor(disp, L[:, mc, :, :],
                                        psum[:, 5, :].unsqueeze(1).broadcast_to([P, QT, 512]),
                                        ALU.subtract).then_inc(disp_shift, 1)

            def disp_sums(g):
                dve.wait_ge(sum_mm, 2 * g + 1)
                link(nc.vector.reciprocal(col[:, :], psum[:, 4, 0:8].rearrange("p (a n) -> p a n", n=2)[:, :, 0]))
                diagonals().then_inc(sum_diag, 1)
                dve.wait_ge(sum_mm, 2 * g + 2)
                link(nc.vector.tensor_copy(qneg[:, :], psum[:, 5, :]))
                if g:
                    dve.wait_ge(slot_lo, g)

            def keep_slots(g, c):
                dve.wait_ge(slot_mm, 4 * g + c + 1)
                nc.vector.tensor_tensor(slots[:, c, :], psum[:, 6 + c % 2, :], qneg[:, :],
                                        ALU.mult).then_inc(slot_kept, 1)

            def combine_low(g, pieces=range(4)):
                for m in pieces:
                    dve.wait_ge(comb_hi, 4 * g + m + 1)
                    nc.vector.tensor_tensor(comb_16[staging(g)][1][:, m, :], psum[:, 2 + m % 2, :],
                                            comb_16[staging(g)][0][:, m, :],
                                            ALU.subtract).then_inc(comb_lo, 1)

            turn_lo_beside(*beside(0))
            slot_factors(3)
            for g in range(-1, GROUPS):
                if g + 1 < GROUPS:
                    if g + 1 < GROUPS - 1:
                        column_maxima(g + 1)
                    disp_maxima(g + 1)
                    if g == 0:
                        disp_low(0)
                        tokens_low(0)
                    if (g + 1) % MC < MC - 1 or g + 1 == GROUPS - 1:
                        row_maxima(g + 1)
                    disp_subtract(g + 1)
                if g < 0:
                    continue
                disp_sums(g)
                keep_slots(g, 0)
                keep_slots(g, 1)
                for c in COMBINED[g][:1]:
                    combine_low(c, range(0, 2))
                keep_slots(g, 2)
                for c in COMBINED[g][:1]:
                    combine_low(c, range(2, 4))
                if g + 1 < GROUPS:
                    disp_low(g + 1)
                if g == 0:
                    tokens_low(1)
                if g + 2 == GROUPS - 1:
                    column_maxima(g + 2)
                keep_slots(g, 3)
                if (g + 2) % MC == MC - 1 and g + 2 < GROUPS - 1:
                    row_maxima(g + 2)
                for c in COMBINED[g][1:]:
                    combine_low(c)
            dve.wait_ge(comb_exp, GROUPS)
            link(nc.vector.tensor_reduce(row_rec[:, :], row_sum[:, :, :, :].rearrange("p b q m -> p (b q) m"),
                                         AX.X, ALU.add))
            link(nc.vector.reciprocal(row_rec[:, :], row_rec[:, :]))
            link(nc.vector.tensor_scalar(row_rec[:, :], row_rec[:, :], 1.0 / UP, None, ALU.mult))

            def chunk_low(e, s):
                n = N_EXP + s
                dve.wait_ge(split_hi, 8 * e + n + 1)
                nc.vector.scalar_tensor_tensor(flat(wlo[:, n % 2, :, :]), raw[:, n % 2, :], UP,
                                               flat(whi[:, n % 2, :, :]), ALU.mult, ALU.subtract).then_inc(split_lo, 1)

            def hidden_low(e, hc):
                dve.wait_ge(hid_hi, HC * e + hc + 1)
                nc.vector.scalar_tensor_tensor(hid_16[hc % 2][1], hid, UP, hid_16[hc % 2][0],
                                               ALU.mult, ALU.subtract).then_inc(hid_lo, 1)

            def keep_out(e):
                for r in range(4):
                    dve.wait_ge(products, products_after(N_EXP - 1) + 4 * (8 * e + (8 if not isinstance(e, int) or e < E - 1 else 7) + 1))
                    nc.vector.scalar_tensor_tensor(eo[:, r, :], psum[:, 4 + r, :], 1.0 / UP,
                                                   flat(b2_rows[:, bass.ds(e, 1), :]), ALU.mult, ALU.add).then_inc(eo_kept, 1)

            def out_low(e):
                dve.wait_ge(eo_hi, e + 1)
                nc.vector.tensor_tensor(eo_16[1], eo, eo_16[0], ALU.subtract).then_inc(eo_lo, 1)

            def keep_combined(e):
                for t in range(T):
                    dve.wait_ge(comb_mm, T * e + t + 1)
                    nc.vector.scalar_tensor_tensor(resid[:, t, :], psum[:, t % 4, :], row_rec[:, t:t + 1],
                                                   resid[:, t, :], ALU.mult, ALU.add).then_inc(comb_kept, 1)

            def expert(e, first=False, last=False):
                if not first:
                    keep_out(e - 1)
                chunk_low(e, 2)
                if not first:
                    out_low(e - 1)
                hidden_low(e, 1)
                chunk_low(e, 3)
                if not first:
                    keep_combined(e - 1)
                chunk_low(e, 4)
                hidden_low(e, 2)
                chunk_low(e, 5)
                chunk_low(e, 6)
                hidden_low(e, 3)
                chunk_low(e, 7)
                if not last:
                    chunk_low(e, 8)
                    hidden_low(e + 1, 0)
                    chunk_low(e, 9)

            chunk_low(0, 1)
            hidden_low(0, 0)
            dve.wait_ge(bias_loaded, 32)
            link(nc.vector.tensor_scalar(b2_rows, b2_rows, UP, None, ALU.mult))
            expert(0, first=True)
            with dve.Fori(1, E - 1) as e:
                expert(e)
            expert(E - 1, last=True)
            keep_out(E - 1)
            dve.wait_ge(eo_half_hi, 1)
            nc.vector.tensor_tensor(eo_16[1][:, 0:2, :], eo[:, 0:2, :], eo_16[0][:, 0:2, :],
                                    ALU.subtract).then_inc(eo_half_lo, 1)
            dve.wait_ge(eo_hi, E)
            nc.vector.tensor_tensor(eo_16[1][:, 2:4, :], eo[:, 2:4, :], eo_16[0][:, 2:4, :],
                                    ALU.subtract).then_inc(eo_lo, 1)
            keep_combined(E - 1)

        @block.tensor
        def _(pe):
            def product(out_, lhs, rhs, start, stop):
                nc.tensor.matmul(out_, lhs[0], rhs[0], start=start, stop=False)
                nc.tensor.matmul(out_, lhs[0], rhs[1], start=False, stop=False)
                return nc.tensor.matmul(out_, lhs[1], rhs[0], start=False, stop=stop)

            def turn(order, tiles, src):
                for t in tiles:
                    n = order[t]
                    if order is TURN_SN:
                        pe.wait_ge(sn_ready, t + 1)
                    elif order is TURN_X:
                        pe.wait_ge(rows_ready, ROWS_X + t + 1)
                    elif order is TURN_HN:
                        pe.wait_ge(rows_ready, ROWS_HN + t + 1)
                    elif order is TURN_XN:
                        pe.wait_ge(rows_ready, ROWS_XN + t + 1)
                    before = [m for m in range(n) if TURN_BANK[m] == TURN_BANK[n]]
                    if before:
                        pe.wait_ge(turned_lo, before[-1] + 1)
                    for c in range(DC):
                        last = nc.tensor.transpose(psum[:, TURN_BANK[n], c * P:(c + 1) * P], src(t, c), ident)
                    last.then_inc(turned, 1)

            def rows_of(buf):
                return lambda t, c: buf[:, t, c * P:(c + 1) * P]

            w = [[x_[:, u, :, :] for x_ in (whi, wlo)] for u in range(2)]

            pe.wait_ge(const_loaded, 32)
            turn(TURN_X, range(0, QT), rows_of(x_nat[0]))
            pe.wait_ge(turned_lo, QT)

            for b in range(B):
                def scores(i, u):
                    j = 2 * i + u - 2 * KC * b
                    pe.wait_ge(split_lo, 2 * i + u + 1)
                    for k in range(CT):
                        if not (isinstance(j, int) and j == 0):
                            pe.wait_ge(scores_kept, KT * b + CT * (j - 1) + k + 1)
                        elif b and k == CT - 1:
                            pe.wait_ge(o_ready, QT * b)
                        for c in range(DC):
                            last = product(psum[:, k, :], [x_[:, c, k * P:(k + 1) * P] for x_ in w[u]],
                                           [x_[:, c, b * NQ:(b + 1) * NQ] for x_ in qT], c == 0, c == DC - 1)
                        last.then_inc(products, 1)

                start = b * N_CTX // 4
                scores(start, 0)
                scores(start, 1)
                with pe.Fori(start + 1, start + KC // 2) as i:
                    scores(i, 0)
                    scores(i, 1)

                pe.wait_ge(max_kept, (KT + 1) * (b + 1))
                for q in range(QT):
                    last = nc.tensor.transpose(psum[:, 0, q * P:(q + 1) * P], run_max[:, q * P:(q + 1) * P], ident)
                last.then_inc(stat_mm, 1)
                pe.wait_ge(stat_dve, b + 1)
                nc.tensor.matmul(psum[:, 1, :], ones, diag[:, :, :].rearrange("p a n -> p (a n)"),
                                 start=True, stop=True).then_inc(stat_mm, 1)
                if b == 0:
                    pe.wait_ge(tile_shifted, 2)
                    turn(TURN_X, range(QT, T), lambda t, c: x_nat[1][:, t - QT, c * P:(c + 1) * P])

                def values(i, u, last=False):
                    j = 2 * i + u - KC * (2 * b + 1)
                    pe.wait_ge(split_lo, 2 * i + u + 1)
                    pe.wait_ge(p_lo, KC * b + j + 1)
                    for q in range(QT):
                        for k in range(CT):
                            done = product(psum[:, 4 + q, :], [x_[:, k, q * P:(q + 1) * P] for x_ in pp[u]],
                                           [x_[:, k, :] for x_ in w[u]], False, last and k == CT - 1)
                        done.then_inc(products, 1)

                def first_values(i):
                    pe.wait_ge(split_lo, 2 * i + 1)
                    for k in range(CT):
                        if k < CT - 1:
                            pe.wait_ge(tile_lo, (CT - 1) * b + k + 1)
                        else:
                            pe.wait_ge(p_lo, KC * b + 1)
                        for q in range(QT):
                            done = product(psum[:, 4 + q, :], [x_[:, k, q * P:(q + 1) * P] for x_ in pp[0]],
                                           [x_[:, k, :] for x_ in w[0]], k == 0, False)
                        done.then_inc(products, 1)

                if b:
                    pe.wait_ge(o_ready, QT * b)
                last_pair = (b + 1) * N_CTX // 4 - 1
                start = last_pair + 1 - KC // 2
                first_values(start)
                values(start, 1)
                with pe.Fori(start + 1, last_pair) as i:
                    values(i, 0)
                    values(i, 1)
                values(last_pair, 0)
                values(last_pair, 1, last=True)
                pe.wait_ge(sum_kept, (KT + 1) * (b + 1))
                for q in range(QT):
                    done = nc.tensor.matmul(psum[:, CT - 1, 2 * q:2 * q + 2], run_sum[:, q * P:(q + 1) * P], ones[:, 0:2],
                                            start=True, stop=True)
                done.then_inc(stat_mm, 1)

            def project(n, order, tiles):
                pe.wait_ge(split_lo, n + 1)
                for t in tiles:
                    pe.wait_ge(turned_lo, order[t] + 1)
                    if t >= 4:
                        pe.wait_ge(proj_kept, (T if n == N_WP else 0) + t - 3)
                    for c in range(DC):
                        last = product(psum[:, 4 + t % 4, :], [x_[:, c, t * P:(t + 1) * P] for x_ in tT],
                                       [x_[:, c, :] for x_ in w[n % 2]], c == 0, c == DC - 1)
                    last.then_inc(products, 1)

            pe.wait_ge(o_loaded, 16)
            turn(TURN_O, range(0, CT - 1), rows_of(o_nat))
            pe.wait_ge(o_ready, T)
            turn(TURN_O, range(CT - 1, T), rows_of(o_nat))
            project(N_WO, TURN_O, range(0, T - 1))
            turn(TURN_HN, range(0, QT), rows_of(nat))
            project(N_WO, TURN_O, range(T - 1, T))

            pe.wait_ge(turned_lo, TURN_HN[QT - 1] + 1)
            pe.wait_ge(proj_kept, T)
            for k, n in enumerate((N_WQ, N_WK, N_WV)):
                pe.wait_ge(split_lo, n + 1)
                for t in range(T):
                    if T * k + t >= 4:
                        pe.wait_ge(qkv_lo, T * k + t - 3)
                    b, f = divmod(t, DC)
                    if n == N_WQ and t == QT:
                        turn(TURN_HN, range(QT, T), rows_of(nat))
                        pe.wait_ge(turned_lo, TURN_HN[T - 1] + 1)
                    for c in range(DC):
                        if n == N_WV:
                            lhs = [x_[:, c, t * P:(t + 1) * P] for x_ in tT]
                            rhs = [x_[:, c, :] for x_ in w[n % 2]]
                        else:
                            lhs = [x_[:, c, f * P:(f + 1) * P] for x_ in w[n % 2]]
                            rhs = [x_[:, c, b * NQ:(b + 1) * NQ] for x_ in tT]
                        last = product(psum[:, 4 + t % 4, :], lhs, rhs, c == 0, c == DC - 1)
                    last.then_inc(products, 1)

            q_heads, k_heads = (s_.rearrange("p b h n -> p (b h n)") for s_ in (q_stack, k_stack))

            def score_head(g, u):
                for n, (bank, tiles) in enumerate(SCORE_BANKS):
                    if not (isinstance(g, int) and g == 0):
                        pe.wait_ge(head_exp, 3 * (g - 1) + n + 1)
                    for q, at in tiles:
                        width = (q + 1) * P
                        nc.tensor.matmul(psum[:, bank, at:at + width], q_heads[:, bass.ds(NQ * g + q * P, P)],
                                         k_heads[:, bass.ds(NQ * g, width)], start=True, stop=False)
                        last = nc.tensor.matmul(psum[:, bank, at + q * P:at + width], ident16[:, :], causal16[:, :],
                                                start=False, stop=True)
                    last.then_inc(head_scores, 1)

            def turn_head(g, u):
                pe.wait_ge(head_exp, 3 * g + 3)
                if not (isinstance(g, int) and g == 0):
                    pe.wait_ge(head_decayed, g)
                for bank, tiles in TURN_BANKS:
                    for k, at in tiles:
                        for q in range(k, QT):
                            a_ = at + (q - k) * P
                            src = PROB_AT[q] + k * P
                            last = nc.tensor.transpose(psum[:, bank, a_:a_ + P], prob[u][:, src:src + P], ident)
                last.then_inc(head_turned, 1)

            v_heads = [v_.rearrange("p g k d -> p (g k d)") for v_ in v_nat]

            def head_out(g, u):
                pe.wait_ge(head_lo, g + 1)
                if not (isinstance(g, int) and g < 2):
                    pe.wait_ge(head_kept, g - 1)
                for q in range(QT):
                    for k in range(q + 1):
                        at = BLOCK_AT[k] + (q - k) * P
                        last = product(psum[:, 6 + u, q * HD:(q + 1) * HD],
                                       [x_[:, at:at + P] for x_ in prob_16[u]],
                                       [x_[:, bass.ds(QT * HD * g + k * HD, HD)] for x_ in v_heads], k == 0, k == q)
                last.then_inc(head_y, 1)

            pe.wait_ge(q_stacked, STACKED)
            pe.wait_ge(k_stacked, STACKED)
            pe.wait_ge(qkv_lo, 3 * T)
            pe.wait_ge(setup_done, 4)
            score_head(0, 0)
            for g in range(4):
                score_head(g + 1, 1 - g % 2)
                turn_head(g, g % 2)
                if g >= 2:
                    head_out(g - 2, g % 2)
            with pe.Fori(2, NH // 2 - 1) as i:
                for u in range(2):
                    score_head(2 * i + u + 1, 1 - u)
                    turn_head(2 * i + u, u)
                    head_out(2 * i + u - 2, u)
            score_head(NH - 1, 1)
            for g in range(NH - 2, NH):
                turn_head(g, g % 2)
                head_out(g - 2, g % 2)

            def turn_y(tiles):
                turn(TURN_Y, tiles, lambda t, c: y_nat[:, t % QT, H * (t // QT) + 4 * c:H * (t // QT) + 4 * c + 4, :].rearrange(
                    "p h d -> p (h d)"))

            turn_y(range(0, 3))
            head_out(NH - 2, 0)
            pe.wait_ge(head_decayed, NH)
            turn_y(range(3, QT))
            project(N_WP, TURN_Y, range(0, 2))
            head_out(NH - 1, 1)
            pe.wait_ge(head_kept, NH)
            turn_y(range(QT, T))

            def turn_sn(tiles):
                turn(TURN_SN, tiles, lambda t, c: se_nat[t // 8][:, t % 8, c * P:(c + 1) * P])

            def turn_beside(kind, tiles):
                if kind == "sn":
                    turn_sn(tiles)
                elif kind == "xn":
                    turn(TURN_XN, tiles, rows_of(nat))

            project(N_WP, TURN_Y, range(2, T - 1))
            turn_sn(range(0, QT))
            project(N_WP, TURN_Y, range(T - 1, T))
            turn(TURN_XN, range(0, QT), rows_of(nat))

            def turn_maxima(g):
                pe.wait_ge(cmax_ready, g + 1)
                for m in range(4):
                    last = nc.tensor.transpose(psum[:, 4, m * P:(m + 1) * P], bcast[:, m * P:(m + 1) * P], ident)
                last.then_inc(max_mm, 1)

            def spread_maxima(g):
                pe.wait_ge(max_diag, g + 1)
                nc.tensor.matmul(psum[:, 5, :], ones, diag[:, :, :].rearrange("p a n -> p (a n)"),
                                 start=True, stop=True).then_inc(max_mm, 1)

            def logits(g, rows):
                b, mc = divmod(g, MC)
                pe.wait_ge(turned_lo, max(TURN_SN[QT * mc + QT - 1] if b == 0 else 0, TURN_XN[QT * b + QT - 1]) + 1)
                for q in rows:
                    if QT * g + q >= 2:
                        pe.wait_ge(logit_kept, QT * g + q - 1)
                    for c in range(DC):
                        at = (QT * b + q) * P
                        last = product(psum[:, q % 2, :], [x_[:, c, at:at + P] for x_ in tT],
                                       [x_[:, c, mc * 512:(mc + 1) * 512] for x_ in snT], c == 0, c == DC - 1)
                    last.then_inc(logit_mm, 1)

            def dispatch_sums(g):
                pe.wait_ge(disp_lo, g + 1)
                for m in range(4):
                    for q in range(QT):
                        for part in range(2):
                            last = nc.tensor.matmul(psum[:, 4, 2 * m:2 * m + 2],
                                                    disp_16[g % 2][part][:, q, m * P:(m + 1) * P], one16[:, :],
                                                    start=q + part == 0, stop=q + part == QT)
                last.then_inc(sum_mm, 1)

            def spread_sums(g):
                pe.wait_ge(sum_diag, g + 1)
                if g + 1 < GROUPS:
                    pe.wait_ge(disp_shift, g + 2)
                nc.tensor.matmul(psum[:, 5, :], ones, diag[:, :, :].rearrange("p a n -> p (a n)"),
                                 start=True, stop=True).then_inc(sum_mm, 1)

            def slot_products(g, c):
                b = g // MC
                if 4 * g + c >= 2:
                    pe.wait_ge(slot_kept, 4 * g + c - 1)
                for q in range(QT):
                    last = product(psum[:, 6 + c % 2, :], [x_[:, QT * b + q, c * P:(c + 1) * P] for x_ in xn_nat],
                                   [x_[:, q, :] for x_ in disp_16[g % 2]], q == 0, q == QT - 1)
                last.then_inc(slot_mm, 1)

            def turn_combine(g, pieces=range(4)):
                pe.wait_ge(comb_exp, g + 1)
                for m in pieces:
                    if 4 * g + m >= 2:
                        pe.wait_ge(comb_lo, 4 * g + m - 1)
                    for q in range(QT):
                        last = nc.tensor.transpose(psum[:, 2 + m % 2, q * P:(q + 1) * P],
                                                   numerators(g)[:, q, m * P:(m + 1) * P], ident)
                    last.then_inc(comb_turned, 1)

            pe.wait_ge(proj_kept, 2 * T)
            for g in range(-2, GROUPS):
                if g + 2 < GROUPS:
                    kind, tiles = beside(g + 2)
                    logits(g + 2, range(0, 1))
                    turn_beside(kind, tiles[0:2])
                    logits(g + 2, range(1, 2))
                    turn_beside(kind, tiles[2:4])
                if 0 <= g + 1 < GROUPS:
                    turn_maxima(g + 1)
                if g + 2 < GROUPS:
                    logits(g + 2, range(2, QT))
                if 0 <= g + 1 < GROUPS:
                    spread_maxima(g + 1)
                if g < 0:
                    continue
                pe.wait_ge(xn_lo, QT * (g // MC + 1))
                dispatch_sums(g)
                slot_products(g, 0)
                spread_sums(g)
                slot_products(g, 1)
                for c in COMBINED[g][:1]:
                    turn_combine(c, range(0, 2))
                slot_products(g, 2)
                for c in COMBINED[g][:1]:
                    turn_combine(c, range(2, 4))
                slot_products(g, 3)
                for c in COMBINED[g][1:]:
                    turn_combine(c)

            def first_products(e, hc, s, u, combined=False):
                q = HC * e + hc
                n = N_EXP + s
                pe.wait_ge(split_lo, 8 * e + n + 1)
                for k in range(CT):
                    if combined:
                        pe.wait_ge(comb_kept, T * (e - 1) + QT + k + 1)
                    if not (isinstance(q, int) and q == 0):
                        pe.wait_ge(hid_done, CT * (q - 1) + k + 1)
                    for c in range(DC):
                        last = product(psum[:, k, :], [x_[:, c, k * P:(k + 1) * P] for x_ in w[n % 2]],
                                       [e_slots[u][:, i, c, :] for i in range(2)], c == 0, c == DC - 1)
                    last.then_inc(products, 1)

            def second_products(e, hc, s):
                q = HC * e + hc
                n = N_EXP + s
                pe.wait_ge(split_lo, 8 * e + n + 1)
                pe.wait_ge(hid_lo, q + 1)
                for k in range(CT):
                    for r in range(4):
                        last = product(psum[:, 4 + r, :], [x_[:, k, r * P:(r + 1) * P] for x_ in hid_16[hc % 2]],
                                       [x_[:, k, :] for x_ in w[n % 2]],
                                       hc == 0 and k == 0, hc == HC - 1 and k == CT - 1)
                    last.then_inc(products, 1)

            def combine(e, u, nth, halves=False):
                pe.wait_ge(e_comb_in[u], 16 * nth)
                if not halves:
                    pe.wait_ge(eo_lo, e + 1)
                for t in range(T):
                    b, q = divmod(t, QT)
                    if halves and q == 0:
                        pe.wait_ge(*((eo_lo, E) if b else (eo_half_lo, 1)))
                    if t >= 4:
                        pe.wait_ge(comb_kept, T * e + t - 3)
                    for m in range(2):
                        last = product(psum[:, t % 4, :],
                                       [e_comb[u][:, i, 2 * b + m, q * P:(q + 1) * P] for i in range(2)],
                                       [x_[:, 2 * b + m, :] for x_ in eo_16], m == 0, m == 1)
                    last.then_inc(comb_mm, 1)

            def expert(e, u, nth, first=False, last=False):
                first_products(e, 1, 1, u)
                if not first:
                    pe.wait_ge(eo_kept, 4 * e)
                second_products(e, 0, 2)
                if not first:
                    pe.wait_ge(hid_done, CT * (HC * e + 1) + CT)
                    combine(e - 1, 1 - u, nth - (1 if u == 0 else 0))
                first_products(e, 2, 3, u, combined=not first)
                second_products(e, 1, 4)
                first_products(e, 3, 5, u)
                second_products(e, 2, 6)
                if not last:
                    pe.wait_ge(e_slots_in[1 - u], 16 * (nth + (1 if u == 1 else 0)))
                    first_products(e + 1, 0, -1 , 1 - u)
                    second_products(e, 3, 8)
                else:
                    second_products(e, 3, 7)

            pe.wait_ge(e_slots_in[0], 16)
            pe.wait_ge(comb_lo, 4 * GROUPS)
            first_products(0, 0, 0, 0)
            pe.wait_ge(slot_kept, 4 * GROUPS)
            expert(0, 0, 1, first=True)
            with pe.Fori(0, E // 2 - 1) as i:
                expert(2 * i + 1, 1, i + 1)
                expert(2 * i + 2, 0, i + 2)
            expert(E - 1, 1, E // 2, last=True)
            pe.wait_ge(hid_done, CT * HC * E)
            combine(E - 1, 1, E // 2, halves=True)


def kernel(**inputs):
    import numpy as np
    import concourse.bacc as bacc
    from concourse.bass_utils import run_bass_kernel_spmd

    a = {k: np.asarray(v) for k, v in inputs.items()}

    def cut(m, inner):
        return m.reshape(-1, P, inner).transpose(1, 0, 2).reshape(P, -1)

    ctx = a["ctx_1024"]
    ctx_stream = np.empty((N_CTX, P, CT * 512), ctx.dtype)
    for b in range(B):
        turned = ctx[b].T
        for j in range(KC):
            part = slice(512 * j, 512 * (j + 1))
            ctx_stream[2 * KC * b + j] = cut(turned[:, part], 512)
            ctx_stream[2 * KC * b + KC + j] = cut(ctx[b, part, :], 512)
    w_attn = a["L0_attn_W_attn"]
    square_stream = np.stack([cut(a["L0_xattn_W"].T, 512)]
                             + [cut(w_attn[:, D * i:D * (i + 1)], 512) for i in range(3)]
                             + [cut(a["L0_attn_W_proj"], 512)])
    w1, w2 = a["L0_ffn_w1"], a["L0_ffn_w2"]

    def first(e, hc):
        return cut(w1[e][:, 512 * hc:512 * (hc + 1)], 512)

    def second(e, hc):
        return cut(w2[e][512 * hc:512 * (hc + 1), :], 512)

    order = [first(0, 0)]
    for e in range(E):
        for hc in range(1, HC):
            order += [first(e, hc), second(e, hc - 1)]
        if e + 1 < E:
            order.append(first(e + 1, 0))
        order.append(second(e, HC - 1))
    expert_stream = np.stack(order)

    consts = np.zeros((2, P, C_ALL), np.float32)
    rows = np.arange(P)
    consts[:, rows, C_ID + rows] = 1.0
    consts[:, :, C_ONE:C_ONE + P] = 1.0
    consts[0, :, C_QPOS:C_QPOS + NQ] = np.arange(NQ)
    consts[0, :, C_KPOS:C_KPOS + KT] = rows[:, None] + P * np.arange(KT)
    length, echoic = 1024, 16
    fall = 1.0 - np.linspace(0.0, 1.0, length - echoic + 1) ** (1.0 / np.e)
    values = np.concatenate([np.ones(echoic - 1), fall])
    back = np.arange(QT * P)[None, :] - rows[:, None]
    decay = np.where(back >= 0, values[np.maximum(back, 0)], 0.0)
    consts[1, :, C_DECAY:C_DECAY + QT * P] = decay
    for k in (1, 3, 2):
        at, width = C_BLOCKS + BLOCK_AT[k] - QT * P, (QT - k) * P
        consts[1, :, at:at + width] = decay[:, 0:width]
    consts[1, :, C_CAUSAL:C_CAUSAL + P] = np.where(rows[None, :P] <= rows[:, None], 0.0, MASKED)

    arrays = {
        "x": a["x"], "ctx_stream": ctx_stream, "square_stream": square_stream, "expert_stream": expert_stream,
        "lens": a["_lenS2"], "xattn_b": a["L0_xattn_b"], "gamma": a["L0_ffn_norm_gamma"],
        "slot_gamma": a["L0_ffn_slot_norm_gamma"], "slot_embeds": a["L0_ffn_slot_embeds"].reshape(M, D),
        "b1": np.ascontiguousarray(a["L0_ffn_b1"].reshape(E * HID // P, P).T), "b2": a["L0_ffn_b2"],
        "consts": consts,
    }
    arrays = {k: np.ascontiguousarray(v) for k, v in arrays.items()}
    nc = bacc.Bacc("TRN2", target_bir_lowering=False, num_devices=1)
    handles = {k: nc.dram_tensor(f"in_{k}", v.shape, mybir.dt.from_np(v.dtype), kind="ExternalInput").ap()
               for k, v in arrays.items()}
    out = nc.dram_tensor("out", a["x"].shape, F32, kind="ExternalOutput").ap()
    program(nc, **handles, out=out)
    result = run_bass_kernel_spmd(nc, [{f"in_{k}": v for k, v in arrays.items()}], core_ids=[0])
    return result.results[0]["out"]
```
